# Optimizing a Trainium2 kernel written in Bass

```python
import numpy as np
import jax
import jax.numpy as jnp

def _softmax(x, axis=-1):
    return jax.nn.softmax(x, axis=axis)

def _gelu(x):
    return jax.nn.gelu(x, approximate=True)

def _silu(x):
    return jax.nn.silu(x)

def _sigmoid(x):
    return jax.nn.sigmoid(x)

def _layernorm(x, axis=-1, eps=1e-05):
    m = jnp.mean(x, axis=axis, keepdims=True)
    v = jnp.var(x, axis=axis, keepdims=True)
    return (x - m) / jnp.sqrt(v + eps)

def _scatter_add(tgt, idx, src, axis=0):
    return tgt.at[idx].add(src)

def _segment_sum(src, seg, n):
    return jax.ops.segment_sum(src, seg, n)
kernel_name = 'mk_gnn_resnorm_d2_gnn_r16_17e3e7'

def setup_inputs(seed: int=0):
    np.random.seed(seed)
    _w = jnp.asarray

    def _rec_inputs():
        import jax
        import jax.numpy as jnp
        _gk = jax.random.key(seed)
        x = -6.415e-05 + 1 * jax.random.normal(jax.random.fold_in(_gk, 1), (1250, 512), jnp.float32)
        _s = jax.random.randint(jax.random.fold_in(_gk, 2), (10000,), 0, 1250, jnp.int32)
        _d = jax.random.randint(jax.random.fold_in(_gk, 3), (10000,), 0, 1250, jnp.int32)
        _loop = jnp.arange(1250, dtype=jnp.int32)
        src = jnp.concatenate([_s, _d, _loop])
        dst = jnp.concatenate([_d, _s, _loop])
        _o = jnp.argsort(dst, stable=True)
        src = src[_o]
        dst = dst[_o]
        edge_attr_64 = 0.000279952 + 1.00013 * jax.random.normal(jax.random.fold_in(_gk, 11), (21250, 64), jnp.float32)
        return (x, src, dst, edge_attr_64)
    x, src, dst, edge_attr_64 = _rec_inputs()

    def _L0_gnn_setup():
        import jax, jax.numpy as jnp
        import numpy as np
        N, E, H = (1250, 10000, 512)
        EPS = 1e-07

        def _ln(x, g, b, eps=1e-05):
            mu = jnp.mean(x, axis=-1, keepdims=True)
            var = jnp.mean((x - mu) ** 2, axis=-1, keepdims=True)
            return (x - mu) * jax.lax.rsqrt(var + eps) * g + b

        def _genconv(x, src, dst, t, w1, b1, lg, lb, w2, b2):
            m = jax.nn.relu(x[src]) + EPS
            z = m * t
            zmax = jax.lax.stop_gradient(jax.ops.segment_max(z, dst, num_segments=N))
            zmax = jnp.where(jnp.isfinite(zmax), zmax, 0.0)
            e = jnp.exp(z - zmax[dst])
            denom = jax.ops.segment_sum(e, dst, num_segments=N)
            alpha = e / (denom[dst] + 1e-16)
            agg = jax.ops.segment_sum(alpha * m, dst, num_segments=N)
            h = agg + x
            h = jax.nn.relu(_ln(h @ w1 + b1, lg, lb))
            return h @ w2 + b2

        def _forward(x, edge_index, p):
            src, dst = (edge_index[0], edge_index[1])
            x1 = _genconv(x, src, dst, *p['c0'])
            x2 = x1 + jax.nn.relu(_ln(_genconv(x1, src, dst, *p['c1']), p['lng_1'], p['lnb_1']))
            x3 = x2 + jax.nn.relu(_ln(_genconv(x2, src, dst, *p['c2']), p['lng_2'], p['lnb_2']))
            return jnp.concatenate([x1, x2, x3], axis=1) @ p['cw'] + p['cb']
        key = jax.random.key(seed)
        ks = iter(jax.random.split(key, 16))
        s = 0.05
        d = {'x': jax.random.normal(next(ks), (N, H), jnp.float32), 'edge_index': jax.random.randint(next(ks), (2, E), 0, N, jnp.int32)}
        for i in range(3):
            d[f't{i}'] = jnp.ones((1,), jnp.float32)
            d[f'mw1_{i}'] = jax.random.normal(next(ks), (H, 2 * H), jnp.float32) * s
            d[f'mb1_{i}'] = jnp.zeros((2 * H,), jnp.float32)
            d[f'mlg_{i}'] = jnp.ones((2 * H,), jnp.float32)
            d[f'mlb_{i}'] = jnp.zeros((2 * H,), jnp.float32)
            d[f'mw2_{i}'] = jax.random.normal(next(ks), (2 * H, H), jnp.float32) * s
            d[f'mb2_{i}'] = jnp.zeros((H,), jnp.float32)
        for i in (1, 2):
            d[f'lng_{i}'] = jnp.ones((H,), jnp.float32)
            d[f'lnb_{i}'] = jnp.zeros((H,), jnp.float32)
        d['cw'] = jax.random.normal(next(ks), (3 * H, H), jnp.float32) * s
        d['cb'] = jnp.zeros((H,), jnp.float32)
        return d
    _L0_gnn_all = _L0_gnn_setup()
    _L0_gnn_in = {k: v for k, v in _L0_gnn_all.items() if k in ('t0', 'mw1_0', 'mb1_0', 'mlg_0', 'mlb_0', 'mw2_0', 'mb2_0', 't1', 'mw1_1', 'mb1_1', 'mlg_1', 'mlb_1', 'mw2_1', 'mb2_1', 't2', 'mw1_2', 'mb1_2', 'mlg_2', 'mlb_2', 'mw2_2', 'mb2_2', 'lng_1', 'lnb_1', 'lng_2', 'lnb_2', 'cw', 'cb')}
    del _L0_gnn_all

    def _L1_gnn_setup():
        import jax, jax.numpy as jnp
        import numpy as np
        N_NODES = 1250
        N_EDGES = 20000
        HIDDEN = 512
        EDGE_DIM = 64
        LN_EPS = 1e-05

        def mish(x):
            return x * jnp.tanh(jax.nn.softplus(x))
        key = jax.random.key(seed)
        ks = jax.random.split(key, 8)
        s = lambda fan_in: 1.0 / np.sqrt(fan_in)
        return {'x': jax.random.normal(ks[0], (N_NODES, HIDDEN), dtype=jnp.float32), 'edge_index': jax.random.randint(ks[1], (2, N_EDGES), 0, N_NODES, dtype=jnp.int64), 'edge_attr': jax.random.normal(ks[2], (N_EDGES, EDGE_DIM), dtype=jnp.float32), 'W1': jax.random.normal(ks[3], (2 * HIDDEN + EDGE_DIM, HIDDEN), dtype=jnp.float32) * s(2 * HIDDEN + EDGE_DIM), 'b1': jnp.zeros((HIDDEN,), dtype=jnp.float32), 'W2': jax.random.normal(ks[4], (HIDDEN, HIDDEN), dtype=jnp.float32) * s(HIDDEN), 'b2': jnp.zeros((HIDDEN,), dtype=jnp.float32), 'W3': jax.random.normal(ks[5], (2 * HIDDEN, HIDDEN), dtype=jnp.float32) * s(2 * HIDDEN), 'b3': jnp.zeros((HIDDEN,), dtype=jnp.float32), 'W4': jax.random.normal(ks[6], (HIDDEN, HIDDEN), dtype=jnp.float32) * s(HIDDEN), 'b4': jnp.zeros((HIDDEN,), dtype=jnp.float32), 'gamma': jnp.ones((HIDDEN,), dtype=jnp.float32), 'beta': jnp.zeros((HIDDEN,), dtype=jnp.float32)}
    _L1_gnn_all = _L1_gnn_setup()
    _L1_gnn_in = {k: v for k, v in _L1_gnn_all.items() if k in ('W1', 'b1', 'W2', 'b2', 'W3', 'b3', 'W4', 'b4', 'gamma', 'beta')}
    del _L1_gnn_all
    return {'x': x, 'src': src, 'dst': dst, 'edge_attr_64': edge_attr_64, 'L0_gnn_t0': _L0_gnn_in['t0'], 'L0_gnn_mw1_0': _L0_gnn_in['mw1_0'], 'L0_gnn_mb1_0': _L0_gnn_in['mb1_0'], 'L0_gnn_mlg_0': _L0_gnn_in['mlg_0'], 'L0_gnn_mlb_0': _L0_gnn_in['mlb_0'], 'L0_gnn_mw2_0': _L0_gnn_in['mw2_0'], 'L0_gnn_mb2_0': _L0_gnn_in['mb2_0'], 'L0_gnn_t1': _L0_gnn_in['t1'], 'L0_gnn_mw1_1': _L0_gnn_in['mw1_1'], 'L0_gnn_mb1_1': _L0_gnn_in['mb1_1'], 'L0_gnn_mlg_1': _L0_gnn_in['mlg_1'], 'L0_gnn_mlb_1': _L0_gnn_in['mlb_1'], 'L0_gnn_mw2_1': _L0_gnn_in['mw2_1'], 'L0_gnn_mb2_1': _L0_gnn_in['mb2_1'], 'L0_gnn_t2': _L0_gnn_in['t2'], 'L0_gnn_mw1_2': _L0_gnn_in['mw1_2'], 'L0_gnn_mb1_2': _L0_gnn_in['mb1_2'], 'L0_gnn_mlg_2': _L0_gnn_in['mlg_2'], 'L0_gnn_mlb_2': _L0_gnn_in['mlb_2'], 'L0_gnn_mw2_2': _L0_gnn_in['mw2_2'], 'L0_gnn_mb2_2': _L0_gnn_in['mb2_2'], 'L0_gnn_lng_1': _L0_gnn_in['lng_1'], 'L0_gnn_lnb_1': _L0_gnn_in['lnb_1'], 'L0_gnn_lng_2': _L0_gnn_in['lng_2'], 'L0_gnn_lnb_2': _L0_gnn_in['lnb_2'], 'L0_gnn_cw': _L0_gnn_in['cw'], 'L0_gnn_cb': _L0_gnn_in['cb'], 'L1_gnn_W1': _L1_gnn_in['W1'], 'L1_gnn_b1': _L1_gnn_in['b1'], 'L1_gnn_W2': _L1_gnn_in['W2'], 'L1_gnn_b2': _L1_gnn_in['b2'], 'L1_gnn_W3': _L1_gnn_in['W3'], 'L1_gnn_b3': _L1_gnn_in['b3'], 'L1_gnn_W4': _L1_gnn_in['W4'], 'L1_gnn_b4': _L1_gnn_in['b4'], 'L1_gnn_gamma': _L1_gnn_in['gamma'], 'L1_gnn_beta': _L1_gnn_in['beta']}

def reference(x, src, dst, edge_attr_64, L0_gnn_t0, L0_gnn_mw1_0, L0_gnn_mb1_0, L0_gnn_mlg_0, L0_gnn_mlb_0, L0_gnn_mw2_0, L0_gnn_mb2_0, L0_gnn_t1, L0_gnn_mw1_1, L0_gnn_mb1_1, L0_gnn_mlg_1, L0_gnn_mlb_1, L0_gnn_mw2_1, L0_gnn_mb2_1, L0_gnn_t2, L0_gnn_mw1_2, L0_gnn_mb1_2, L0_gnn_mlg_2, L0_gnn_mlb_2, L0_gnn_mw2_2, L0_gnn_mb2_2, L0_gnn_lng_1, L0_gnn_lnb_1, L0_gnn_lng_2, L0_gnn_lnb_2, L0_gnn_cw, L0_gnn_cb, L1_gnn_W1, L1_gnn_b1, L1_gnn_W2, L1_gnn_b2, L1_gnn_W3, L1_gnn_b3, L1_gnn_W4, L1_gnn_b4, L1_gnn_gamma, L1_gnn_beta):
    import jax
    import jax.numpy as jnp

    def _L0_gnn_ref(x, edge_index, t0, mw1_0, mb1_0, mlg_0, mlb_0, mw2_0, mb2_0, t1, mw1_1, mb1_1, mlg_1, mlb_1, mw2_1, mb2_1, t2, mw1_2, mb1_2, mlg_2, mlb_2, mw2_2, mb2_2, lng_1, lnb_1, lng_2, lnb_2, cw, cb):
        import jax, jax.numpy as jnp
        import numpy as np
        N, E, H = (1250, 10000, 512)
        EPS = 1e-07

        def _ln(x, g, b, eps=1e-05):
            mu = jnp.mean(x, axis=-1, keepdims=True)
            var = jnp.mean((x - mu) ** 2, axis=-1, keepdims=True)
            return (x - mu) * jax.lax.rsqrt(var + eps) * g + b

        def _genconv(x, src, dst, t, w1, b1, lg, lb, w2, b2):
            m = jax.nn.relu(x[src]) + EPS
            z = m * t
            zmax = jax.lax.stop_gradient(jax.ops.segment_max(z, dst, num_segments=N))
            zmax = jnp.where(jnp.isfinite(zmax), zmax, 0.0)
            e = jnp.exp(z - zmax[dst])
            denom = jax.ops.segment_sum(e, dst, num_segments=N)
            alpha = e / (denom[dst] + 1e-16)
            agg = jax.ops.segment_sum(alpha * m, dst, num_segments=N)
            h = agg + x
            h = jax.nn.relu(_ln(h @ w1 + b1, lg, lb))
            return h @ w2 + b2

        def _forward(x, edge_index, p):
            src, dst = (edge_index[0], edge_index[1])
            x1 = _genconv(x, src, dst, *p['c0'])
            x2 = x1 + jax.nn.relu(_ln(_genconv(x1, src, dst, *p['c1']), p['lng_1'], p['lnb_1']))
            x3 = x2 + jax.nn.relu(_ln(_genconv(x2, src, dst, *p['c2']), p['lng_2'], p['lnb_2']))
            return jnp.concatenate([x1, x2, x3], axis=1) @ p['cw'] + p['cb']
        p = {'c0': (t0, mw1_0, mb1_0, mlg_0, mlb_0, mw2_0, mb2_0), 'c1': (t1, mw1_1, mb1_1, mlg_1, mlb_1, mw2_1, mb2_1), 'c2': (t2, mw1_2, mb1_2, mlg_2, mlb_2, mw2_2, mb2_2), 'lng_1': lng_1, 'lnb_1': lnb_1, 'lng_2': lng_2, 'lnb_2': lnb_2, 'cw': cw, 'cb': cb}
        return _forward(x, edge_index, p)

    def _L1_gnn_ref(x, edge_index, edge_attr, W1, b1, W2, b2, W3, b3, W4, b4, gamma, beta):
        import jax, jax.numpy as jnp
        import numpy as np
        N_NODES = 1250
        N_EDGES = 20000
        HIDDEN = 512
        EDGE_DIM = 64
        LN_EPS = 1e-05

        def mish(x):
            return x * jnp.tanh(jax.nn.softplus(x))
        src, dst = (edge_index[0], edge_index[1])
        edge_feat = jnp.concatenate([x[src], x[dst], edge_attr], axis=-1)
        h = mish(edge_feat @ W1 + b1)
        messages = mish(h @ W2 + b2)
        agg = jax.ops.segment_sum(messages, dst, num_segments=x.shape[0])
        u = mish(jnp.concatenate([x, agg], axis=-1) @ W3 + b3)
        out = u @ W4 + b4
        y = x + out
        mu = jnp.mean(y, axis=-1, keepdims=True)
        var = jnp.mean(jnp.square(y - mu), axis=-1, keepdims=True)
        return (y - mu) * jax.lax.rsqrt(var + LN_EPS) * gamma + beta
    edge_index = jnp.stack([src, dst])
    x = _layernorm(x + _L0_gnn_ref(x, edge_index, L0_gnn_t0, L0_gnn_mw1_0, L0_gnn_mb1_0, L0_gnn_mlg_0, L0_gnn_mlb_0, L0_gnn_mw2_0, L0_gnn_mb2_0, L0_gnn_t1, L0_gnn_mw1_1, L0_gnn_mb1_1, L0_gnn_mlg_1, L0_gnn_mlb_1, L0_gnn_mw2_1, L0_gnn_mb2_1, L0_gnn_t2, L0_gnn_mw1_2, L0_gnn_mb1_2, L0_gnn_mlg_2, L0_gnn_mlb_2, L0_gnn_mw2_2, L0_gnn_mb2_2, L0_gnn_lng_1, L0_gnn_lnb_1, L0_gnn_lng_2, L0_gnn_lnb_2, L0_gnn_cw, L0_gnn_cb), axis=-1)
    x = _layernorm(x + _L1_gnn_ref(x, edge_index, edge_attr_64, L1_gnn_W1, L1_gnn_b1, L1_gnn_W2, L1_gnn_b2, L1_gnn_W3, L1_gnn_b3, L1_gnn_W4, L1_gnn_b4, L1_gnn_gamma, L1_gnn_beta), axis=-1)
    return x

_drawn_inputs = setup_inputs


def setup_inputs(seed=0):
    import zlib

    import numpy as np

    out = dict(_drawn_inputs(seed))
    spreads = {'L0_gnn_mb1_0': (0.0, 0.1),
     'L0_gnn_mlg_0': (1.0, 0.2),
     'L0_gnn_mlb_0': (0.0, 0.1),
     'L0_gnn_mb2_0': (0.0, 0.1),
     'L0_gnn_mb1_1': (0.0, 0.428),
     'L0_gnn_mlg_1': (1.0, 0.2),
     'L0_gnn_mlb_1': (0.0, 0.1),
     'L0_gnn_mb2_1': (0.0, 0.1),
     'L0_gnn_mb1_2': (0.0, 0.8),
     'L0_gnn_mlg_2': (1.0, 0.2),
     'L0_gnn_mlb_2': (0.0, 0.312),
     'L0_gnn_mb2_2': (0.0, 0.346),
     'L0_gnn_lng_1': (1.0, 0.2),
     'L0_gnn_lnb_1': (0.0, 0.1),
     'L0_gnn_lng_2': (1.0, 0.2),
     'L0_gnn_lnb_2': (0.0, 0.275),
     'L0_gnn_cb': (0.0, 0.1),
     'L1_gnn_b1': (0.0, 0.1),
     'L1_gnn_b2': (0.0, 0.1),
     'L1_gnn_b3': (0.0, 0.547),
     'L1_gnn_b4': (0.0, 0.4),
     'L1_gnn_gamma': (1.0, 0.2),
     'L1_gnn_beta': (0.0, 0.1)}
    factors = {}
    for name, (base, spread) in spreads.items():
        noise = np.random.default_rng([zlib.crc32(name.encode()), seed]).standard_normal(out[name].shape)
        drawn = base * np.exp(spread * noise) if base else spread * noise
        out[name] = jnp.asarray(drawn.astype(out[name].dtype))
    for name, factor in factors.items():
        out[name] = (out[name] * factor).astype(out[name].dtype)
    return out
```

```python
import concourse.bass as bass
from concourse import mybir
from contextlib import ExitStack

F32 = mybir.dt.float32
F32R = mybir.dt.float32r
BF16 = mybir.dt.bfloat16
F16 = mybir.dt.float16
I32 = mybir.dt.int32
ALU = mybir.AluOpType
ACT = mybir.ActivationFunctionType
AX = mybir.AxisListType

P = 128
N, H, E, ED = 1250, 512, 21250, 64
NT = (N + P - 1) // P
NP = NT * P
LAST = N - (NT - 1) * P
KC = H // P
H2 = 2 * H
K2 = H2 // P
EP, EJ = 125, E // 125
PAIRS = (E + NT * 255) // 256
QUADS = PAIRS // 2
TILES = 2 * PAIRS
ROWS = TILES * P
ROW = ED + 4
SC = 10
EPS = 1e-7
LN_EPS = 1e-5
TINY = 1e-16
EXP_AND_LOG = "natural_log_exp_and_others"
CAP = float(2 ** 24)
NB = [(0, 512), (512, 512), (1024, 256)]


def carry(eng, S):
    eng.sem_inc(S("carried"), 1)


def r32(ap):
    return ap.bitcast(F32)


CREDIT, DMA_CREDIT = 2, 32
CREDITED_1 = ("onehots pair_counted pair_added h_hi h_lo u_psum u_added parts1 stat1 log1 rstd1 normed g_turned g_relu g_hi g_lo "
              "x_psum x_added parts2 stat2 log2 rstd2 x_normed x_scaled x_shifted x_out").split()
CREDITED_DMA_1 = "old_in0 old_in1 x_stored0 x_stored1".split()
CREDITED_2 = ("cat_turned cat_hi cat_lo y_psum y_biased y_added y_parts y_stat y_log y_rstd y_norm x_kept n_turned n_hi n_lo pq_psum p_out q_out "
              "index_copied attr_turned attr_hi attr_lo z_ready z_exp z_min z_u z_ln z_r z_h z_hi z_lo "
              "m_ready m_x m_exp m_min m_u m_ln m_r m_msg onehot seg_ready seg_added "
              "o_kept o_agg o_turned o_hi o_lo v_psum v_x v_exp v_min v_u v_ln v_r v_out v_turned v_hi v_lo w_psum "
              "f_base f_y f_parts1 f_stat1 f_log1 f_rstd1 f_norm1 f_scaled f_shifted f_sum f_parts2 f_stat2 f_log2 f_rstd2 f_out").split()
CREDITED_DMA_2 = "cat_in p_stored q_stored attr_in0 attr_in1 f_stored0 f_stored1".split()


def at(n):
    return n + CREDIT


def dma_at(n):
    return 16 * n + DMA_CREDIT


class Sems:

    def __init__(self, nc, half):
        self.nc, self.half, self.made = nc, half, {}

    def __call__(self, name):
        if name not in self.made:
            self.made[name] = self.nc.alloc_semaphore(name=f"{name}.{self.half}")
        return self.made[name]

    def give_credit(self, eng, compute, dma):
        for name in compute:
            eng.sem_inc(self(name), CREDIT)
        for name in dma:
            eng.sem_inc(self(name), DMA_CREDIT)

    def close(self):
        self.nc.clear_and_free_semaphores(list(self.made.values()))
        self.nc.all_engine_barrier()


def sort_edges(nc, S, K, T, A):
    with ExitStack() as c:
        sb = lambda n, s, d=F32: c.enter_context(nc.sbuf_tensor(n, s, d))
        src_i, dst_i = sb("src_i", [EP, EJ], I32), sb("dst_i", [EP, EJ], I32)
        bkt_i = sb("bkt_i", [EP, EJ], I32)
        src_f, dst_f, bkt_f = sb("src_f", [EP, EJ]), sb("dst_f", [EP, EJ]), sb("bkt_f", [EP, EJ])
        oh, cum = sb("oh", [EP, NT, EJ]), sb("cum", [EP, NT, EJ])
        ones_e = sb("ones_e", [EP, EJ])
        pos, tmp = sb("pos", [EP, EJ]), sb("tmp", [EP, EJ])
        pos_i = sb("pos_i", [EP, EJ], I32)
        pay = sb("pay", [EP, EJ, ROW])
        payb = sb("payb", [EP, SC, ROW])
        posb = sb("posb", [EP, SC], I32)
        dum = sb("dum", [P, ROW])
        below = sb("below", [EP, EP])
        tot, npair, incl, excl = (sb(n, [P, NT]) for n in ("tot", "npair", "incl", "excl"))
        tot_i = sb("tot_i", [P, NT], I32)
        base = sb("base", [EP, NT])
        qi, qd, qs = sb("qi", [P, PAIRS]), sb("qd", [P, PAIRS]), sb("qs", [P, PAIRS])
        pc = c.enter_context(nc.psum_tensor("pc", [P, 512], F32))
        table_rows = T["table"]
        with nc.Block() as block:
            @block.sync
            def _(sp):
                S.give_credit(sp, CREDITED_1, CREDITED_DMA_1)
                sp.dma_start(dst_i[:], A["dst"].rearrange("(p j) -> p j", p=EP)).then_inc(S("dst_in"), 16)
                sp.dma_start(src_i[:], A["src"].rearrange("(p j) -> p j", p=EP)).then_inc(S("src_in"), 16)
                sp.dma_start(pay[:, :, 0:ED], A["edge_attr_64"].rearrange("(p j) f -> p j f", p=EP)).then_inc(S("attr_in"), 16)
                sp.wait_ge(S("dummy_set"), 2)
                sp.dma_start(table_rows.rearrange("(p r) f -> p r f", p=P),
                             dum[:].unsqueeze(1).to_broadcast([P, ROWS // P, ROW])).then_inc(S("table_filled"), 16)
                sp.dma_start(T["x"][0][0:N, :], A["x"]).then_inc(S("x_padded"), 16)
                sp.wait_ge(S("zero_set"), 1)
                sp.dma_start(T["x"][0][N:NP, :], K["zeros"][0:NP - N, :]).then_inc(S("x_padded"), 16)
                sp.wait_ge(S("x_padded"), 32)
                sp.wait_ge(S("table_filled"), 16)

            @block.gpsimd
            def _(pool):
                g = nc.gpsimd
                g.memset(K["ident"][:], 0.0).then_inc(S("ident_0"), 1)
                g.memset(K["zeros"][:], 0.0).then_inc(S("zero_set"), 1)
                g.memset(below[:], 1.0).then_inc(S("below_1"), 1)
                g.memset(K["ones"][:], 1.0).then_inc(S("const_ready"), 1)
                g.iota(K["iota"][:], [[1, P]], base=0, channel_multiplier=0,
                       allow_small_or_imprecise_dtypes=True).then_inc(S("const_ready"), 1)
                g.iota(K["iota_n"][:], [[1, NP]], base=0, channel_multiplier=0,
                       allow_small_or_imprecise_dtypes=True).then_inc(S("const_ready"), 1)
                g.iota(qi[:], [[1, PAIRS]], base=0, channel_multiplier=0,
                       allow_small_or_imprecise_dtypes=True).then_inc(S("const_ready"), 1)
                pool.wait_ge(S("below_1"), 1)
                g.affine_select(out=below[:], in_=below[:], compare_op=ALU.is_gt, fill=0.0, base=0,
                                pattern=[[1, EP]], channel_multiplier=-1).then_inc(S("const_ready"), 1)
                pool.wait_ge(S("ident_0"), 1)
                g.affine_select(out=K["ident"][:], in_=K["ident"][:], compare_op=ALU.not_equal, fill=1.0, base=0,
                                pattern=[[-1, P]], channel_multiplier=1).then_inc(S("const_ready"), 1)
                pool.wait_ge(S("table_filled"), 16)
                with pool.Fori(0, EJ // SC) as it:
                    pool.wait_ge(S("batch_ready"), 2 * it + 2)
                    carry(pool, S)
                    for s in range(SC):
                        g.indirect_dma_start(out=table_rows, out_offset=bass.IndirectOffsetOnAxis(ap=posb[:, s:s + 1], axis=0),
                                             in_=payb[:, s, :], in_offset=None).then_inc(S("scattered"), 16)
                pool.wait_ge(S("scattered"), 16 * EJ)

            @block.tensor
            def _(pe):
                pe.wait_ge(S("const_ready"), 6)
                pe.wait_ge(S("counted"), NT)
                counts = cum[:, :, EJ - 1]
                nc.tensor.matmul(pc[0:EP, 0:NT], below[:], counts, start=True, stop=True)
                nc.tensor.matmul(pc[:, 64:64 + NT], K["ones"][0:EP, :], counts, start=True, stop=True).then_inc(S("count_sums"), 1)

            @block.vector
            def _(dve):
                v = nc.vector
                done = [0]

                def step(ins):
                    done[0] += 1
                    ins.then_inc(S("sort_steps"), 1)
                    dve.wait_ge(S("sort_steps"), done[0])

                v.memset(dum[:], 0.0).then_inc(S("dummy_set"), 1)
                dve.wait_ge(S("dummy_set"), 1)
                v.memset(dum[:, ED + 2:ED + 3], -1.0).then_inc(S("dummy_set"), 1)
                step(v.memset(ones_e[:], 1.0))
                dve.wait_ge(S("dst_in"), 16)
                v.tensor_copy(dst_f[:], dst_i[:])
                step(v.tensor_single_scalar(bkt_i[:], dst_i[:], 7, ALU.arith_shift_right))
                step(v.tensor_copy(bkt_f[:], bkt_i[:]))
                for b in range(NT):
                    step(v.tensor_single_scalar(oh[:, b, :], bkt_f[:], float(b), ALU.is_equal))
                    v.tensor_tensor_scan(cum[:, b, :], ones_e[:], oh[:, b, :], 0.0, ALU.mult, ALU.add).then_inc(S("counted"), 1)
                dve.wait_ge(S("src_in"), 16)
                v.tensor_copy(src_f[:], src_i[:])
                dve.wait_ge(S("count_sums"), 1)
                step(v.tensor_copy(tot[:], pc[:, 64:64 + NT]))
                step(v.tensor_scalar(tot[:], tot[:], 255.0, None, ALU.add))
                step(v.tensor_copy(tot_i[:], tot[:]))
                step(v.tensor_single_scalar(tot_i[:], tot_i[:], 8, ALU.arith_shift_right))
                step(v.tensor_copy(npair[:], tot_i[:]))
                step(v.tensor_tensor_scan(incl[:], ones_e[0:P, 0:NT] if EP >= P else K["ones"][:, 0:NT], npair[:], 0.0, ALU.mult, ALU.add))
                step(v.tensor_tensor(excl[:], incl[:], npair[:], ALU.subtract))
                step(v.tensor_scalar(base[:], excl[0:EP, :], 256.0, -1.0, ALU.mult, ALU.add))
                step(v.tensor_tensor(base[:], base[:], pc[0:EP, 0:NT], ALU.add))
                step(v.memset(pos[:], 0.0))
                for b in range(NT):
                    step(v.scalar_tensor_tensor(tmp[:], cum[:, b, :], base[:, b:b + 1], oh[:, b, :], ALU.add, ALU.mult))
                    step(v.tensor_tensor(pos[:], pos[:], tmp[:], ALU.add))
                step(v.tensor_copy(pos_i[:], pos[:]))
                dve.wait_ge(S("attr_in"), 16)
                v.tensor_copy(pay[:, :, ED], src_f[:])
                v.tensor_copy(pay[:, :, ED + 1], dst_f[:])
                v.memset(pay[:, :, ED + 3], 0.0)
                step(v.scalar_tensor_tensor(pay[:, :, ED + 2], bkt_f[:], -float(P), dst_f[:], ALU.mult, ALU.add))
                dve.wait_ge(S("const_ready"), 6)
                step(v.memset(qd[:], -1.0))
                for b in range(NT):
                    step(v.tensor_scalar(qs[:], qi[:], excl[:, b:b + 1], None, ALU.is_ge))
                    step(v.tensor_tensor(qd[:], qd[:], qs[:], ALU.add))
                step(v.tensor_copy(K["pair_tile"][:], qd[:]))
                v.memset(K["counts"][:].bitcast(F32), 0.0).then_inc(S("counts_zero"), 1)
                v.memset(K["ln_eps"][:], LN_EPS).then_inc(S("counts_zero"), 1)
                v.tensor_copy(payb[:], pay[:, 0:SC, :]).then_inc(S("batch_ready"), 1)
                v.tensor_copy(posb[:], pos_i[:, 0:SC]).then_inc(S("batch_ready"), 1)
                with dve.Fori(1, EJ // SC) as it:
                    dve.wait_ge(S("scattered"), 16 * SC * it)
                    v.tensor_copy(payb[:], pay[:, bass.ds(it * SC, SC), :]).then_inc(S("batch_ready"), 1)
                    v.tensor_copy(posb[:], pos_i[:, bass.ds(it * SC, SC)]).then_inc(S("batch_ready"), 1)


def count_edges(nc, S, K, T):
    with ExitStack() as c:
        sb = lambda n, s, d=F32: c.enter_context(nc.sbuf_tensor(n, s, d))
        oh_src = [sb(f"oh_src{u}", [P, 2, NP], BF16) for u in range(2)]
        oh_dst = [sb(f"oh_dst{u}", [P, 2, P], BF16) for u in range(2)]
        ps = [c.enter_context(nc.psum_tensor(f"pcount{u}", [P, 3 * 512], F32)) for u in range(2)]
        meta, counts = K["meta"], K["counts"]
        PART = TILES // 4
        with nc.Block() as block:
            @block.sync
            def _(sp):
                for k in range(4):
                    sp.dma_start(meta[:, k * PART:(k + 1) * PART, :],
                                 T["table"].rearrange("(t p) f -> p t f", p=P)[:, k * PART:(k + 1) * PART, ED:ROW]).then_inc(S(f"meta_in{k}"), 16)

            def pair(eng, q, u):
                v = nc.vector
                eng.wait_ge(S("pair_counted"), at(q - 1))
                for k in range(2):
                    v.tensor_scalar(oh_dst[u][:, k, :], K["iota"][:], meta[:, bass.ds(2 * q + k, 1), 2], None, ALU.is_equal)
                    last = v.tensor_scalar(oh_src[u][:, k, :], K["iota_n"][:], meta[:, bass.ds(2 * q + k, 1), 0], None, ALU.is_equal)
                last.then_inc(S("onehots"), 1)

            def add(eng, q, u):
                v = nc.vector
                tile = eng.value_load(K["pair_tile"][0:1, bass.ds(q, 1)], min_val=0, max_val=NT - 1)
                eng.wait_ge(S("pair_counted"), at(q + 1))
                dst = counts[:, :, bass.ds(tile * P, P)]
                eng.wait_ge(S("pair_added"), at(q))
                v.tensor_tensor(dst, r32(dst), ps[u][:, 0:NP].rearrange("p (j d) -> p j d", j=NT), ALU.add).then_inc(S("pair_added"), 1)

            @block.vector
            def _(dve):
                for k in range(4):
                    dve.wait_ge(S(f"meta_in{k}"), 16)
                nc.vector.tensor_copy(K["src_dst"][:], meta[:, :, 0:2]).then_inc(S("index_ready"), 1)
                pair(dve, 0, 0)
                with dve.Fori(0, PAIRS // 2 - 1) as it:
                    for u in range(2):
                        pair(dve, 2 * it + u + 1, 1 - u)
                        add(dve, 2 * it + u, u)
                pair(dve, PAIRS - 1, 1)
                add(dve, PAIRS - 2, 0)
                add(dve, PAIRS - 1, 1)

            @block.tensor
            def _(pe):
                with pe.Fori(0, PAIRS // 2) as it:
                    for u in range(2):
                        q = 2 * it + u
                        pe.wait_ge(S("onehots"), at(q + 1))
                        pe.wait_ge(S("pair_added"), at(q - 1))
                        for k in range(2):
                            for j in range(NT):
                                last = nc.tensor.matmul(ps[u][:, j * P:(j + 1) * P], oh_src[u][:, k, j * P:(j + 1) * P],
                                                        oh_dst[u][:, k, :], start=k == 0 and j % 4 == 0,
                                                        stop=k == 1 and (j % 4 == 3 or j == NT - 1), skip_group_check=True)
                        last.then_inc(S("pair_counted"), 1)


def split_chunks(nc, S, c, tag, jobs, before=0):
    st = [c.enter_context(nc.sbuf_tensor(f"{tag}_stage{u}_{before}", [P, 1024], F32)) for u in range(2)]

    def view(k):
        n = jobs[k][0].shape[1]
        return st[k % 2][:].rearrange("p (n m) -> p n m", n=n)

    def load(eng):
        for k, (src, hi, lo) in enumerate(jobs):
            if k >= 2:
                eng.wait_ge(S(f"{tag}_lo"), before + k - 1)
            eng.dma_start(view(k), src).then_inc(S(f"{tag}_in{k % 2}"), 16)

    def high(eng):
        for k, (src, hi, lo) in enumerate(jobs):
            eng.wait_ge(S(f"{tag}_in{k % 2}"), 16 * (before // 2 + k // 2 + 1))
            nc.scalar.copy(hi, view(k)).then_inc(S(f"{tag}_hi"), 1)

    def low(eng, alu, ks=None):
        for k in ks or range(len(jobs)):
            src, hi, lo = jobs[k]
            eng.wait_ge(S(f"{tag}_hi"), before + k + 1)
            alu.tensor_tensor(lo, view(k), r32(hi), ALU.subtract).then_inc(S(f"{tag}_lo"), 1)

    return load, high, low


def rows(ap, n):
    return ap.rearrange("(n p) m -> p n m", p=P)


def aggregate(nc, S, K, T, A, W, l):
    with ExitStack() as c:
        sb = lambda n, s, d=F32: c.enter_context(nc.sbuf_tensor(f"{n}_{l}", s, d))
        xc = [sb(f"xc{u}", [P, NT, P]) for u in range(2)]
        m, e, em = (sb(n, [P, NT, P]) for n in ("m", "e", "em"))
        eh, el, mh, ml = ([sb(f"{n}{u}", [P, NT, P], F32R) for u in range(2)] for n in ("eh", "el", "mh", "ml"))
        pmax, top, dg = sb("pmax", [P, P]), sb("top", [P, 1]), sb("dg", [P, P])
        rden = sb("rden", [P, 512])
        tcol = sb("tcol", [P, 1])
        psd, psn, psx = ([c.enter_context(nc.psum_tensor(f"{n}{u}_{l}", [P, 512], F32)) for u in range(2)] for n in ("psd", "psn", "psx"))
        psk = c.enter_context(nc.psum_tensor(f"psk_{l}", [P, P], F32))
        psb = c.enter_context(nc.psum_tensor(f"psb_{l}", [P, P], F32))
        w1 = A[f"L0_gnn_mw1_{l}"]
        load, high, low = split_chunks(nc, S, c, "w1", [
            (rows(w1, KC)[:, k:k + 1, :], W["w1h"][:, k:k + 1, :], W["w1l"][:, k:k + 1, :]) for k in range(KC)], KC * l)
        n, kb, ib = S, KC * l, 3 * KC * l
        row = lambda name: A[name].partition_broadcast(P)
        with nc.Block() as block:
            @block.sync
            def _(sp):
                sp.dma_start(tcol[:], row(f"L0_gnn_t{l}")).then_inc(n("t_in"), 16)
                for k in range(KC):
                    if k >= 2:
                        sp.wait_ge(n("x_turned"), kb + k - 1)
                        sp.wait_ge(n("m_set"), kb + k - 1)
                    sp.dma_start(xc[k % 2][:], T["x"][l].rearrange("(j p) d -> p j d", p=P)[:, :, k * P:(k + 1) * P]).then_inc(n(f"xc_in{k % 2}"), 16)
                    if k == 1:
                        load(sp)
                sp.dma_start(W["b1"][:], row(f"L0_gnn_mb1_{l}")).then_inc(n("rows_in"), 16)
                sp.dma_start(W["b2"][:], row(f"L0_gnn_mb2_{l}")).then_inc(n("rows_in"), 16)
                sp.dma_start(W["g1"][:], A[f"L0_gnn_mlg_{l}"].rearrange("(k p) -> p k", p=P), allow_slow_non_contiguous=True).then_inc(n("rows_in"), 16)
                sp.dma_start(W["a1"][:], A[f"L0_gnn_mlb_{l}"].rearrange("(k p) -> p k", p=P), allow_slow_non_contiguous=True).then_inc(n("rows_in"), 16)
                if l:
                    sp.dma_start(W["g2"][:], row(f"L0_gnn_lng_{l}")).then_inc(n("rows_in"), 16)
                    sp.dma_start(W["a2"][:], row(f"L0_gnn_lnb_{l}")).then_inc(n("rows_in"), 16)
                sp.wait_ge(n("rows_in"), [64, 160, 256][l])

            def prepare(dve, k):
                v = nc.vector
                dve.wait_ge(n(f"xc_in{k % 2}"), 16 * (2 * l + k // 2 + 1))
                if k:
                    dve.wait_ge(n("em_set"), kb + k)
                    dve.wait_ge(n("e_hi"), kb + k)
                    dve.wait_ge(n("e_lo"), kb + k)
                v.tensor_scalar(m[:], xc[k % 2][:], 0.0, EPS, ALU.max, ALU.add).then_inc(n("m_set"), 1)
                dve.wait_ge(n("m_set"), kb + k + 1)
                v.tensor_scalar(e[:], m[:], tcol[:], None, ALU.mult).then_inc(n("z_set"), 1)
                dve.wait_ge(n("z_set"), kb + k + 1)
                v.tensor_reduce(pmax[:], e[:].rearrange("p j c -> p c j"), AX.X, ALU.max).then_inc(n("pmax_set"), 1)
                dve.wait_ge(n("max_turned"), kb + k + 1)
                v.tensor_reduce(top[:], psk[:], AX.X, ALU.max).then_inc(n("top_set"), 1)
                dve.wait_ge(n("top_set"), kb + k + 1)
                v.tensor_scalar(dg[:], K["ident"][:], top[:], None, ALU.mult).then_inc(n("dg_set"), 1)
                dve.wait_ge(n("max_spread"), kb + k + 1)
                v.tensor_tensor(e[:], e[:], psb[:].unsqueeze(1).to_broadcast([P, NT, P]), ALU.subtract).then_inc(n("z_low"), 1)

            def weigh(dve, k):
                v = nc.vector
                dve.wait_ge(n("e_set"), kb + k + 1)
                if k:
                    dve.wait_ge(n("m_lo"), kb + k)
                v.tensor_tensor(em[:], e[:], m[:], ALU.mult).then_inc(n("em_set"), 1)

            def finish(dve, k, b):
                v = nc.vector
                c0, w = NB[b]
                i, u = 3 * k + b, (3 * k + b) % 2
                dve.wait_ge(n("bank_ready"), ib + i + 1)
                if i:
                    dve.wait_ge(n("h_set"), ib + i)
                v.tensor_scalar(rden[:, 0:w], psd[u][:, 0:w], TINY, None, ALU.add).then_inc(n("den_set"), 1)
                dve.wait_ge(n("den_set"), ib + i + 1)
                v.reciprocal(rden[:, 0:w], rden[:, 0:w]).then_inc(n("rden_set"), 1)
                dve.wait_ge(n("rden_set"), ib + i + 1)
                h = W["hT"][:, k, c0:c0 + w]
                v.tensor_tensor(h, rden[:, 0:w], psn[u][:, 0:w], ALU.mult).then_inc(n("agg_set"), 1)
                dve.wait_ge(n("agg_set"), ib + i + 1)
                v.tensor_tensor(h, h, psx[u][:, 0:w], ALU.add).then_inc(n("h_set"), 1)

            @block.vector
            def _(dve):
                dve.wait_ge(n("t_in"), 16 * (l + 1))
                prepare(dve, 0)
                weigh(dve, 0)
                for k in range(KC):
                    if k + 1 < KC:
                        prepare(dve, k + 1)
                        weigh(dve, k + 1)
                    for b in range(3):
                        finish(dve, k, b)

            @block.scalar
            def _(act):
                s = nc.scalar
                s.preload_act_table_set(EXP_AND_LOG)
                for k in range(KC):
                    act.wait_ge(n("z_low"), kb + k + 1)
                    s.activation(e[:], e[:], ACT.Exp).then_inc(n("e_set"), 1)
                    if k >= 2:
                        act.wait_ge(n("bank_ready"), ib + 3 * (k - 1))
                    act.wait_ge(n("e_set"), kb + k + 1)
                    s.copy(eh[k % 2][:], e[:]).then_inc(n("e_hi"), 1)
                    act.wait_ge(n("em_set"), kb + k + 1)
                    s.copy(mh[k % 2][:], em[:]).then_inc(n("m_hi"), 1)
                    if k == 0:
                        high(act)

            @block.gpsimd
            def _(pool):
                g = nc.gpsimd
                for k in range(KC):
                    pool.wait_ge(n("e_hi"), kb + k + 1)
                    g.tensor_tensor(el[k % 2][:], e[:], r32(eh[k % 2][:]), ALU.subtract).then_inc(n("e_lo"), 1)
                    pool.wait_ge(n("m_hi"), kb + k + 1)
                    g.tensor_tensor(ml[k % 2][:], em[:], r32(mh[k % 2][:]), ALU.subtract).then_inc(n("m_lo"), 1)
                    if k == 0:
                        low(pool, g)

            @block.tensor
            def _(pe):
                t = nc.tensor

                def spread_max(k):
                    pe.wait_ge(n("pmax_set"), kb + k + 1)
                    if k:
                        pe.wait_ge(n("top_set"), kb + k)
                    t.transpose(psk[:], pmax[:], K["ident"][:]).then_inc(n("max_turned"), 1)
                    pe.wait_ge(n("dg_set"), kb + k + 1)
                    if k:
                        pe.wait_ge(n("z_low"), kb + k)
                    t.matmul(psb[:], K["ones"][:], dg[:], start=True, stop=True).then_inc(n("max_spread"), 1)

                spread_max(0)
                for k in range(KC):
                    if k + 1 < KC:
                        spread_max(k + 1)
                    pe.wait_ge(n("e_lo"), kb + k + 1)
                    pe.wait_ge(n("m_lo"), kb + k + 1)
                    for b, (c0, w) in enumerate(NB):
                        i, u = 3 * k + b, (3 * k + b) % 2
                        if i >= 2:
                            pe.wait_ge(n("h_set"), ib + i - 1)
                        for jj in range(w // P):
                            last = t.matmul(psx[u][:, jj * P:(jj + 1) * P], xc[k % 2][:, c0 // P + jj, :], K["ident"][:],
                                            is_transpose=True, start=jj == 0, stop=jj == w // P - 1, skip_group_check=True)
                        if b == 2:
                            last.then_inc(n("x_turned"), 1)
                        for ps, his, los in ((psd, eh, el), (psn, mh, ml)):
                            for j in range(NT):
                                t.matmul(ps[u][:, 0:w], his[k % 2][:, j, :], K["counts"][:, j, c0:c0 + w], start=j == 0, stop=False)
                                last = t.matmul(ps[u][:, 0:w], los[k % 2][:, j, :], K["counts"][:, j, c0:c0 + w], start=False, stop=j == NT - 1)
                        last.then_inc(n("bank_ready"), 1)


def three(t, ps, hi, lo, wh, wl, n, lhs):
    for k in range(n):
        t.matmul(ps, lhs(hi, k), wh(k), start=k == 0, stop=False)
        t.matmul(ps, lhs(hi, k), wl(k), start=False, stop=False)
        last = t.matmul(ps, lhs(lo, k), wh(k), start=False, stop=k == n - 1)
    return last


def turn_tile(t, ps, x, n, ident):
    for k in range(n):
        last = t.matmul(ps[:, k * P:(k + 1) * P], x[:, k * P:(k + 1) * P], ident, is_transpose=True,
                        start=k % 4 == 0, stop=k % 4 == 3 or k == n - 1, skip_group_check=True)
    return last


def mean_var(nc, eng, x, n, st, mv, S, i, stat, own):
    v = nc.vector
    for h in range(n):
        last = v.bn_stats(st[:, 6 * h:6 * h + 6], x[:, h * 512:(h + 1) * 512])
    last.then_inc(S(own), 1)
    eng.wait_ge(S(own), at(i + 1))
    carry(eng, S)
    v.bn_aggr(mv, st[:, 0:6 * n]).then_inc(S(stat), 1)


def rstd(nc, eng, K, mv, S, i, stat, log, done):
    eng.wait_ge(S(stat), at(i + 1))
    nc.scalar.activation(mv[:, 1:2], mv[:, 1:2], ACT.Ln, bias=K["ln_eps"][:]).then_inc(S(log), 1)
    eng.wait_ge(S(log), at(i + 1))
    nc.scalar.activation(mv[:, 1:2], mv[:, 1:2], ACT.Exp, scale=-0.5).then_inc(S(done), 1)


def feed_forward(nc, S, K, T, A, W, l):
    with ExitStack() as c:
        sb = lambda n, s, d=F32: c.enter_context(nc.sbuf_tensor(f"{n}_f{l}", s, d))
        w2h, w2l = sb("w2h", [P, K2, H], F32R), sb("w2l", [P, K2, H], F32R)
        hh, hl = ([sb(f"{n}{u}", [P, KC, P], F32R) for u in range(2)] for n in ("hh", "hl"))
        uu = sb("uu", [P, H2])
        gg = [sb(f"gg{u}", [P, H2]) for u in range(2)]
        gr = sb("gr", [P, H2])
        gh, gl = sb("gh", [P, H2], F32R), sb("gl", [P, H2], F32R)
        xn = [sb(f"xn{u}", [P, H]) for u in range(2)]
        xr = sb("xr", [P, H])
        old = [sb(f"old{u}", [P, H]) for u in range(2)]
        st1, st2 = sb("st1", [P, 12]), sb("st2", [P, 6])
        mv1, mv2 = ([sb(f"{n}{u}", [P, 2]) for u in range(2)] for n in ("mv1", "mv2"))
        psu = [c.enter_context(nc.psum_tensor(f"psu{u}_f{l}", [P, H2], F32)) for u in range(2)]
        psg = c.enter_context(nc.psum_tensor(f"psg_f{l}", [P, H2], F32))
        psx = [c.enter_context(nc.psum_tensor(f"psx{u}_f{l}", [P, H], F32)) for u in range(2)]
        w2 = rows(A[f"L0_gnn_mw2_{l}"], K2)
        load, high, low = split_chunks(nc, S, c, "w2", [
            (w2[:, 2 * k:2 * k + 2, :], w2h[:, 2 * k:2 * k + 2, :], w2l[:, 2 * k:2 * k + 2, :]) for k in range(KC)], KC * l)
        B = NT * l
        xin = T["x"][l].rearrange("(j p) d -> p j d", p=P)
        xout = T["x"][l + 1].rearrange("(j p) d -> p j d", p=P)
        BR = NT * max(l - 1, 0)
        with nc.Block() as block:
            @block.sync
            def _(sp):
                load(sp)

                def tile(i, u, half):
                    if l:
                        sp.wait_ge(S("x_out"), at(B + i - 1))
                        sp.dma_start(old[u][:], xin[:, bass.ds(i, 1), :]).then_inc(S(f"old_in{u}"), 16)
                    sp.wait_ge(S("x_out"), at(B + i + 1))
                    sp.dma_start(xout[:, bass.ds(i, 1), :], xn[u][:]).then_inc(S(f"x_stored{u}"), 16)

                with sp.Fori(0, NT // 2) as it:
                    for u in range(2):
                        tile(2 * it + u, u, it)
                for u in range(2):
                    sp.wait_ge(S(f"x_stored{u}"), dma_at((B + NT) // 2))

            @block.scalar
            def _(act):
                s = nc.scalar
                s.preload_act_table_set(EXP_AND_LOG)

                def split_h(i, u):
                    act.wait_ge(S("u_psum"), at(B + i - 1))
                    s.copy(hh[u][:], W["hT"][:, :, bass.ds(i * P, P)]).then_inc(S("h_hi"), 1)

                def norm1(i, u):
                    rstd(nc, act, K, mv1[u], S, B + i, "stat1", "log1", "rstd1")

                def relu_g(i, u):
                    act.wait_ge(S("g_turned"), at(B + i + 1))
                    act.wait_ge(S("g_lo"), at(B + i))
                    act.wait_ge(S("g_hi"), at(B + i))
                    for k in range(K2):
                        last = s.activation(gr[:, k * P:(k + 1) * P], psg[:, k * P:(k + 1) * P], ACT.Relu,
                                            bias=W["a1"][:, k:k + 1], scale=W["g1"][:, k:k + 1])
                    last.then_inc(S("g_relu"), 1)
                    act.wait_ge(S("g_relu"), at(B + i + 1))
                    act.wait_ge(S("x_psum"), at(B + i))
                    s.copy(gh[:], gr[:]).then_inc(S("g_hi"), 1)

                def norm2(i, u):
                    if l:
                        rstd(nc, act, K, mv2[u], S, BR + i, "stat2", "log2", "rstd2")

                split_h(0, 0)
                split_h(1, 1)
                high(act)
                norm1(0, 0)
                with act.Fori(0, NT // 2 - 1) as it:
                    for u in range(2):
                        i = 2 * it + u
                        relu_g(i, u)
                        split_h(i + 2, u)
                        norm1(i + 1, 1 - u)
                        norm2(i, u)
                relu_g(NT - 2, 0)
                norm1(NT - 1, 1)
                norm2(NT - 2, 0)
                relu_g(NT - 1, 1)
                norm2(NT - 1, 1)

            @block.gpsimd
            def _(pool):
                g = nc.gpsimd

                def low_h(i, u):
                    pool.wait_ge(S("h_hi"), at(B + i + 1))
                    pool.wait_ge(S("u_psum"), at(B + i - 1))
                    g.tensor_tensor(hl[u][:], W["hT"][:, :, bass.ds(i * P, P)], r32(hh[u][:]), ALU.subtract).then_inc(S("h_lo"), 1)

                def low_g(i, u):
                    pool.wait_ge(S("g_hi"), at(B + i + 1))
                    pool.wait_ge(S("x_psum"), at(B + i))
                    g.tensor_tensor(gl[:], gr[:], r32(gh[:]), ALU.subtract).then_inc(S("g_lo"), 1)

                low_h(0, 0)
                low_h(1, 1)
                low(pool, g)
                with pool.Fori(0, NT // 2 - 1) as it:
                    for u in range(2):
                        low_g(2 * it + u, u)
                        low_h(2 * it + u + 2, u)
                low_g(NT - 2, 0)
                low_g(NT - 1, 1)

            @block.vector
            def _(dve):
                v = nc.vector

                def first(i, u):
                    dve.wait_ge(S("u_psum"), at(B + i + 1))
                    dve.wait_ge(S("normed"), at(B + i))
                    v.tensor_tensor(uu[:], psu[u][:], W["b1"][:], ALU.add).then_inc(S("u_added"), 1)
                    dve.wait_ge(S("u_added"), at(B + i + 1))
                    dve.wait_ge(S("stat1"), at(B + i))
                    mean_var(nc, dve, uu, 2, st1, mv1[u][:], S, B + i, "stat1", "parts1")
                    dve.wait_ge(S("rstd1"), at(B + i + 1))
                    dve.wait_ge(S("g_turned"), at(B + i - 1))
                    v.tensor_scalar(gg[u][:], uu[:], mv1[u][:, 0:1], mv1[u][:, 1:2], ALU.subtract, ALU.mult).then_inc(S("normed"), 1)

                def second(i, u, half):
                    dve.wait_ge(S("x_psum"), at(B + i + 1))
                    dve.wait_ge(S("x_out"), at(B + i))
                    dve.wait_ge(S(f"x_stored{u}"), dma_at(B // 2 + half))
                    if l == 0:
                        v.tensor_tensor(xn[u][:], psx[u][:], W["b2"][:], ALU.add).then_inc(S("x_out"), 1)
                        return
                    q = BR + i
                    v.tensor_tensor(xr[:], psx[u][:], W["b2"][:], ALU.add).then_inc(S("x_added"), 1)
                    dve.wait_ge(S("x_added"), at(q + 1))
                    dve.wait_ge(S("stat2"), at(q))
                    mean_var(nc, dve, xr, 1, st2, mv2[u][:], S, q, "stat2", "parts2")
                    dve.wait_ge(S("rstd2"), at(q + 1))
                    v.tensor_scalar(xr[:], xr[:], mv2[u][:, 0:1], mv2[u][:, 1:2], ALU.subtract, ALU.mult).then_inc(S("x_normed"), 1)
                    dve.wait_ge(S("x_normed"), at(q + 1))
                    v.tensor_tensor(xr[:], xr[:], W["g2"][:], ALU.mult).then_inc(S("x_scaled"), 1)
                    dve.wait_ge(S("x_scaled"), at(q + 1))
                    v.tensor_tensor(xr[:], xr[:], W["a2"][:], ALU.add).then_inc(S("x_shifted"), 1)
                    dve.wait_ge(S("x_shifted"), at(q + 1))
                    dve.wait_ge(S(f"old_in{u}"), dma_at(BR // 2 + half + 1))
                    v.scalar_tensor_tensor(xn[u][:], xr[:], 0.0, old[u][:], ALU.max, ALU.add).then_inc(S("x_out"), 1)

                first(0, 0)
                with dve.Fori(0, NT // 2 - 1) as it:
                    first(2 * it + 1, 1)
                    second(2 * it, 0, it)
                    first(2 * it + 2, 0)
                    second(2 * it + 1, 1, it)
                first(NT - 1, 1)
                second(NT - 2, 0, NT // 2 - 1)
                second(NT - 1, 1, NT // 2 - 1)

            @block.tensor
            def _(pe):
                t = nc.tensor

                def up(i, u):
                    pe.wait_ge(S("h_lo"), at(B + i + 1))
                    pe.wait_ge(S("u_added"), at(B + i - 1))
                    for h in range(2):
                        last = three(t, psu[u][:, h * 512:(h + 1) * 512], hh[u], hl[u],
                                     lambda k: W["w1h"][:, k, h * 512:(h + 1) * 512],
                                     lambda k: W["w1l"][:, k, h * 512:(h + 1) * 512], KC, lambda a, k: a[:, k, :])
                    last.then_inc(S("u_psum"), 1)

                def down(i, u):
                    pe.wait_ge(S("normed"), at(B + i + 1))
                    pe.wait_ge(S("g_relu"), at(B + i))
                    turn_tile(t, psg, gg[u], K2, K["ident"][:]).then_inc(S("g_turned"), 1)
                    pe.wait_ge(S("g_lo"), at(B + i + 1))
                    pe.wait_ge(S("x_out"), at(B + i - 1))
                    three(t, psx[u][:], gh, gl, lambda k: w2h[:, k, :], lambda k: w2l[:, k, :], K2,
                          lambda a, k: a[:, k * P:(k + 1) * P]).then_inc(S("x_psum"), 1)

                up(0, 0)
                pe.wait_ge(S("w2_lo"), KC * (l + 1))
                with pe.Fori(0, NT // 2 - 1) as it:
                    for u in range(2):
                        up(2 * it + u + 1, 1 - u)
                        down(2 * it + u, u)
                up(NT - 1, 1)
                down(NT - 2, 0)
                down(NT - 1, 1)


def join_layers(nc, S, K, T, A, W):
    with ExitStack() as c:
        sb = lambda n, s, d=F32: c.enter_context(nc.sbuf_tensor(f"{n}_j", s, d))
        CC = 3 * KC
        cwh, cwl = sb("cwh", [P, CC, H], F32R), sb("cwl", [P, CC, H], F32R)
        abh, abl = sb("abh", [P, K2, H], F32R), sb("abl", [P, K2, H], F32R)
        cat = sb("cat", [P, 4, H])
        ch, cl = sb("ch", [P, 3 * H], F32R), sb("cl", [P, 3 * H], F32R)
        nh, nl = sb("nh", [P, H], F32R), sb("nl", [P, H], F32R)
        yy, xt = sb("yy", [P, H]), sb("xt", [P, H])
        st, mv = sb("st", [P, 6]), sb("mv", [P, 2])
        pt, qt = sb("pt", [P, H]), sb("qt", [P, H])
        cb, b1 = sb("cb", [P, H]), sb("b1", [P, H])
        psc = c.enter_context(nc.psum_tensor("psc_j", [P, 3 * H], F32))
        psy = c.enter_context(nc.psum_tensor("psy_j", [P, H], F32))
        psn = c.enter_context(nc.psum_tensor("psn_j", [P, H], F32))
        psp = c.enter_context(nc.psum_tensor("psp_j", [P, H], F32))
        psq = c.enter_context(nc.psum_tensor("psq_j", [P, H], F32))
        cw, w1 = rows(A["L0_gnn_cw"], CC), rows(A["L1_gnn_W1"][0:H2, :], K2)
        load, high, low = split_chunks(nc, S, c, "join", [
            (cw[:, 2 * k:2 * k + 2, :], cwh[:, 2 * k:2 * k + 2, :], cwl[:, 2 * k:2 * k + 2, :]) for k in range(CC // 2)] + [
            (w1[:, 2 * k:2 * k + 2, :], abh[:, 2 * k:2 * k + 2, :], abl[:, 2 * k:2 * k + 2, :]) for k in range(KC)])
        CHUNKS = CC // 2 + KC
        tiles = lambda x: x.rearrange("(j p) d -> p j d", p=P)
        with nc.Block() as block:
            @block.sync
            def _(sp):
                def bring(i):
                    sp.wait_ge(S("cat_turned"), at(i))
                    sp.wait_ge(S("y_added"), at(i))
                    for l in range(4):
                        sp.dma_start(cat[:, l, :], tiles(T["x"][l])[:, bass.ds(i, 1), :]).then_inc(S("cat_in"), 16)

                S.give_credit(sp, CREDITED_2, CREDITED_DMA_2)
                bring(0)
                load(sp)
                sp.dma_start(cb[:], A["L0_gnn_cb"].partition_broadcast(P)).then_inc(S("join_rows"), 16)
                sp.dma_start(b1[:], A["L1_gnn_b1"].partition_broadcast(P)).then_inc(S("join_rows"), 16)
                with sp.Fori(1, NT) as i:
                    bring(i)

            @block.scalar
            def _(act):
                s = nc.scalar
                s.preload_act_table_set(EXP_AND_LOG)

                def cat_high(i):
                    act.wait_ge(S("cat_turned"), at(i + 1))
                    act.wait_ge(S("y_psum"), at(i))
                    s.copy(ch[:], psc[:]).then_inc(S("cat_hi"), 1)

                def norm(i):
                    rstd(nc, act, K, mv, S, i, "y_stat", "y_log", "y_rstd")

                def x_high(i):
                    act.wait_ge(S("n_turned"), at(i + 1))
                    act.wait_ge(S("pq_psum"), at(i))
                    s.copy(nh[:], psn[:]).then_inc(S("n_hi"), 1)

                def store_p(i):
                    act.wait_ge(S("pq_psum"), at(i + 1))
                    act.wait_ge(S("p_stored"), dma_at(i))
                    s.copy(pt[:], psp[:]).then_inc(S("p_out"), 1)
                    act.wait_ge(S("p_out"), at(i + 1))
                    act.dma_start(tiles(T["src_part"])[:, bass.ds(i, 1), :], pt[:]).then_inc(S("p_stored"), 16)
                    act.wait_ge(S("q_out"), at(i + 1))
                    act.dma_start(tiles(T["dst_part"])[:, bass.ds(i, 1), :], qt[:]).then_inc(S("q_stored"), 16)

                high(act)
                cat_high(0)
                norm(0)
                with act.Fori(1, NT) as i:
                    cat_high(i)
                    x_high(i - 1)
                    norm(i)
                    store_p(i - 1)
                x_high(NT - 1)
                store_p(NT - 1)
                act.wait_ge(S("p_stored"), dma_at(NT))
                act.wait_ge(S("q_stored"), dma_at(NT))

            @block.vector
            def _(dve):
                v = nc.vector

                def cat_low(i):
                    dve.wait_ge(S("cat_hi"), at(i + 1))
                    v.tensor_tensor(cl[:], psc[:], r32(ch[:]), ALU.subtract).then_inc(S("cat_lo"), 1)

                def norm(i):
                    dve.wait_ge(S("y_psum"), at(i + 1))
                    dve.wait_ge(S("y_norm"), at(i))
                    v.tensor_tensor(yy[:], psy[:], cb[:], ALU.add).then_inc(S("y_biased"), 1)
                    dve.wait_ge(S("y_biased"), at(i + 1))
                    v.tensor_tensor(yy[:], yy[:], cat[:, 0, :], ALU.add).then_inc(S("y_added"), 1)
                    dve.wait_ge(S("y_added"), at(i + 1))
                    dve.wait_ge(S("y_stat"), at(i))
                    mean_var(nc, dve, yy, 1, st, mv[:], S, i, "y_stat", "y_parts")
                    dve.wait_ge(S("y_rstd"), at(i + 1))
                    dve.wait_ge(S("n_turned"), at(i))
                    dve.wait_ge(S("x_kept"), at(i))
                    v.tensor_scalar(xt[:], yy[:], mv[:, 0:1], mv[:, 1:2], ALU.subtract, ALU.mult).then_inc(S("y_norm"), 1)

                def x_low(i):
                    dve.wait_ge(S("n_hi"), at(i + 1))
                    v.tensor_tensor(nl[:], psn[:], r32(nh[:]), ALU.subtract).then_inc(S("n_lo"), 1)

                def store_q(i):
                    dve.wait_ge(S("pq_psum"), at(i + 1))
                    dve.wait_ge(S("q_stored"), dma_at(i))
                    v.tensor_tensor(qt[:], psq[:], b1[:], ALU.add).then_inc(S("q_out"), 1)

                low(dve, v)
                dve.wait_ge(S("join_rows"), 32)
                cat_low(0)
                dve.wait_ge(S("cat_in"), dma_at(4))
                norm(0)
                with dve.Fori(1, NT) as i:
                    cat_low(i)
                    x_low(i - 1)
                    norm(i)
                    store_q(i - 1)
                x_low(NT - 1)
                store_q(NT - 1)

            @block.gpsimd
            def _(pool):
                with pool.Fori(0, NT) as i:
                    pool.wait_ge(S("y_norm"), at(i + 1))
                    carry(pool, S)
                    nc.gpsimd.tensor_copy(W["X"][:, bass.ds(i, 1), :], xt[:]).then_inc(S("x_kept"), 1)

            @block.tensor
            def _(pe):
                t = nc.tensor

                def turn_cat(i):
                    pe.wait_ge(S("cat_in"), dma_at(4 * i + 4))
                    pe.wait_ge(S("cat_lo"), at(i))
                    turn_tile(t, psc, cat[:, 1:4, :].rearrange("p l d -> p (l d)"), CC, K["ident"][:]).then_inc(S("cat_turned"), 1)

                def product(i):
                    pe.wait_ge(S("cat_lo"), at(i + 1))
                    pe.wait_ge(S("y_biased"), at(i))
                    three(t, psy[:], ch, cl, lambda k: cwh[:, k, :], lambda k: cwl[:, k, :], CC,
                          lambda a, k: a[:, k * P:(k + 1) * P]).then_inc(S("y_psum"), 1)

                def turn_x(i):
                    pe.wait_ge(S("y_norm"), at(i + 1))
                    pe.wait_ge(S("n_lo"), at(i))
                    turn_tile(t, psn, xt, KC, K["ident"][:]).then_inc(S("n_turned"), 1)

                def parts(i):
                    pe.wait_ge(S("n_lo"), at(i + 1))
                    pe.wait_ge(S("p_out"), at(i))
                    pe.wait_ge(S("q_out"), at(i))
                    three(t, psp[:], nh, nl, lambda k: abh[:, k, :], lambda k: abl[:, k, :], KC,
                          lambda a, k: a[:, k * P:(k + 1) * P])
                    three(t, psq[:], nh, nl, lambda k: abh[:, KC + k, :], lambda k: abl[:, KC + k, :], KC,
                          lambda a, k: a[:, k * P:(k + 1) * P]).then_inc(S("pq_psum"), 1)

                pe.wait_ge(S("join_lo"), CHUNKS)
                turn_cat(0)
                product(0)
                with pe.Fori(1, NT) as i:
                    turn_cat(i)
                    turn_x(i - 1)
                    product(i)
                    parts(i - 1)
                turn_x(NT - 1)
                parts(NT - 1)


def mish_square(v, w):
    return v.scalar_tensor_tensor(w, w, 2.0, w, ALU.add, ALU.mult)


def edge_messages(nc, S, K, T, A, W):
    with ExitStack() as c:
        sb = lambda n, s, d=F32: c.enter_context(nc.sbuf_tensor(f"{n}_e", s, d))
        w2h, w2l = sb("w2h", [P, KC, H], F32R), sb("w2l", [P, KC, H], F32R)
        wc = sb("wc", [ED, H])
        wch2 = sb("wch2", [P, H], F32R)
        wcl = sb("wcl", [ED, H], F32R)
        at_rows = [sb(f"at_rows{u}", [P, 4, P]) for u in range(2)]
        attr = sb("attr", [P, 4 * P], F32R)
        G = [sb(f"G{u}", [P, 4, H]) for u in range(2)]
        GI = [sb(f"GI{u}", [P, 4, 2], I32) for u in range(2)]
        zw = [sb(f"zw{u}", [P, H2]) for u in range(2)]
        zh = [sb(f"zh{u}", [P, H2]) for u in range(2)]
        hh, hl = ([sb(f"{n}{u}", [P, KC, 512], F32R) for u in range(2)] for n in ("hh", "hl"))
        mw = [sb(f"mw{u}", [P, H2]) for u in range(2)]
        mx = [sb(f"mx{u}", [P, H2]) for u in range(2)]
        hot = [sb(f"hot{u}", [P, 4, P]) for u in range(2)]
        b2 = sb("b2", [P, H])
        psa = c.enter_context(nc.psum_tensor("psa_e", [P, 512], F32))
        psz = [c.enter_context(nc.psum_tensor(f"psz{u}_e", [P, H2], F32)) for u in range(2)]
        psm = c.enter_context(nc.psum_tensor("psm_e", [P, H2], F32))
        pss = c.enter_context(nc.psum_tensor("pss_e", [P, H], F32))
        w2 = rows(A["L1_gnn_W2"], KC)
        load, high, low = split_chunks(nc, S, c, "edge", [
            (w2[:, 2 * k:2 * k + 2, :], w2h[:, 2 * k:2 * k + 2, :], w2l[:, 2 * k:2 * k + 2, :]) for k in range(2)])
        table = T["table"].rearrange("(t p) f -> p t f", p=P)
        with nc.Block() as block:
            @block.sync
            def _(sp):
                sp.dma_start(wc[:], A["L1_gnn_W1"][H2:H2 + ED, :]).then_inc(S("wc_in"), 16)
                sp.dma_start(b2[:], A["L1_gnn_b2"].partition_broadcast(P)).then_inc(S("edge_b2_in"), 16)
                load(sp)
                with sp.Fori(0, QUADS // 2) as it:
                    for u in range(2):
                        q = 2 * it + u
                        sp.wait_ge(S("attr_turned"), at(q - 1))
                        sp.dma_start(at_rows[u][:, :, 0:ED], table[:, bass.ds(4 * q, 4), 0:ED]).then_inc(S(f"attr_in{u}"), 16)

            def both(eng, body):
                body(0, 0, False, True, True)
                body(1, 1, True, True, True)
                with eng.Fori(1, QUADS // 2 - 1) as it:
                    for u in range(2):
                        body(2 * it + u, u, True, True, True)
                body(QUADS - 2, 0, True, False, True)
                body(QUADS - 1, 1, True, False, False)

            @block.gpsimd
            def _(pool):
                g = nc.gpsimd

                def index(q, u):
                    pool.wait_ge(S("z_ready"), at(2 * q - 2))
                    carry(pool, S)
                    g.tensor_copy(GI[u][:], K["src_dst"][:, bass.ds(4 * q, 4), :]).then_inc(S("index_copied"), 1)
                    pool.wait_ge(S("index_copied"), at(q + 1))
                    carry(pool, S)
                    for k in range(4):
                        g.indirect_dma_start(out=G[u][:, k, :], out_offset=None, in_=T["src_part"],
                                             in_offset=bass.IndirectOffsetOnAxis(ap=GI[u][:, k, 0:1], axis=0)).then_inc(S(f"src_rows{u}"), 16)

                def add_dst(q, u, it):
                    pool.wait_ge(S(f"src_rows{u}"), 64 * it + 64)
                    carry(pool, S)
                    for k in range(4):
                        g.indirect_dma_start(out=G[u][:, k, :], out_offset=None, in_=T["dst_part"],
                                             in_offset=bass.IndirectOffsetOnAxis(ap=GI[u][:, k, 1:2], axis=0),
                                             compute_op=ALU.add).then_inc(S(f"dst_rows{u}"), 16)

                def low_h(q, u):
                    for f in range(2):
                        n = 2 * q + f
                        pool.wait_ge(S("z_hi"), at(n + 1))
                        pool.wait_ge(S("m_ready"), at(2 * q - 2))
                        g.tensor_tensor(hl[u][:, 2 * f:2 * f + 2, :], zh[f][:].rearrange("p (a b) -> p a b", a=2),
                                        r32(hh[u][:, 2 * f:2 * f + 2, :]), ALU.subtract).then_inc(S("z_lo"), 1)

                for u in range(2):
                    g.memset(at_rows[u][:, :, ED:P], 0.0).then_inc(S("attr_zero"), 1)
                index(0, 0)
                add_dst(0, 0, 0)
                index(1, 1)
                low_h(0, 0)
                add_dst(1, 1, 0)
                with pool.Fori(0, QUADS // 2 - 1) as it:
                    for u in range(2):
                        q = 2 * it + u
                        index(q + 2, u)
                        low_h(q + 1, 1 - u)
                        add_dst(q + 2, u, it + 1)
                low_h(QUADS - 1, 1)

            @block.tensor
            def _(pe):
                t = nc.tensor

                def turn_attr(q, u, it):
                    pe.wait_ge(S(f"attr_in{u}"), dma_at(it + 1))
                    pe.wait_ge(S("attr_lo"), at(q))
                    for k in range(4):
                        last = t.matmul(psa[:, k * P:(k + 1) * P], at_rows[u][:, k, :], K["ident"][:], is_transpose=True,
                                        start=k == 0, stop=k == 3, skip_group_check=True)
                    last.then_inc(S("attr_turned"), 1)

                def layer1(q, u, it):
                    pe.wait_ge(S(f"dst_rows{u}"), 64 * it + 64)
                    for f in range(2):
                        pe.wait_ge(S("z_h"), at(2 * q + f - 1))
                        for a in range(2):
                            j = 2 * f + a
                            for k in range(4):
                                t.matmul(psz[f][:, a * 512 + k * P:a * 512 + (k + 1) * P], G[u][:, k, j * P:(j + 1) * P], K["ident"][:],
                                         is_transpose=True, start=k == 0, stop=False, skip_group_check=True)
                        if f == 0:
                            pe.wait_ge(S("attr_lo"), at(q + 1))
                        for a in range(2):
                            j = 2 * f + a
                            out = psz[f][:, a * 512:(a + 1) * 512]
                            t.matmul(out, wch2[:, j * P:(j + 1) * P], attr[:], start=False, stop=False, skip_group_check=True)
                            last = t.matmul(out, wcl[:, j * P:(j + 1) * P], attr[0:ED, :], start=False, stop=True, skip_group_check=True)
                        last.then_inc(S("z_ready"), 1)

                def layer2(q, u, f):
                    n = 2 * q + f
                    if f == 0:
                        pe.wait_ge(S("z_lo"), at(2 * q + 2))
                    pe.wait_ge(S("m_x"), at(n))
                    for a in range(2):
                        e0 = (2 * f + a) * P
                        last = three(t, psm[:, a * 512:(a + 1) * 512], hh[u], hl[u], lambda k: w2h[:, k, :], lambda k: w2l[:, k, :],
                                     KC, lambda x, k: x[:, k, e0:e0 + P])
                    last.then_inc(S("m_ready"), 1)

                def sum_up(q, u, f):
                    n = 2 * q + f
                    pe.wait_ge(S("m_msg"), at(n + 1))
                    pe.wait_ge(S("onehot"), at(q + 1))
                    pe.wait_ge(S("seg_added"), at(n))
                    t.matmul(pss[:], hot[u][:, 2 * f, :], mw[f][:, 0:512], start=True, stop=False)
                    t.matmul(pss[:], hot[u][:, 2 * f + 1, :], mw[f][:, 512:1024], start=False, stop=True).then_inc(S("seg_ready"), 1)

                pe.wait_ge(S("wc_split"), 3)
                pe.wait_ge(S("attr_zero"), 2)
                turn_attr(0, 0, 0)
                layer1(0, 0, 0)
                turn_attr(1, 1, 0)
                layer1(1, 1, 0)
                pe.wait_ge(S("edge_lo"), 2)
                layer2(0, 0, 0)
                layer2(0, 0, 1)
                with pe.Fori(0, QUADS // 2 - 1) as it:
                    for u in range(2):
                        q = 2 * it + u
                        turn_attr(q + 2, u, it + 1)
                        sum_up(q, u, 0)
                        layer1(q + 2, u, it + 1)
                        layer2(q + 1, 1 - u, 0)
                        sum_up(q, u, 1)
                        layer2(q + 1, 1 - u, 1)
                sum_up(QUADS - 2, 0, 0)
                layer2(QUADS - 1, 1, 0)
                sum_up(QUADS - 2, 0, 1)
                layer2(QUADS - 1, 1, 1)
                sum_up(QUADS - 1, 1, 0)
                sum_up(QUADS - 1, 1, 1)

            @block.scalar
            def _(act):
                s = nc.scalar
                s.preload_act_table_set(EXP_AND_LOG)

                def z_exp(q, f):
                    n = 2 * q + f
                    act.wait_ge(S("z_ready"), at(n + 1))
                    act.wait_ge(S("z_h"), at(n - 1))
                    s.activation(zw[f][:], psz[f][:], ACT.Exp).then_inc(S("z_exp"), 1)

                def z_r(q, f):
                    n = 2 * q + f
                    act.wait_ge(S("z_u"), at(n + 1))
                    s.activation(zw[f][:], zw[f][:], ACT.Ln, scale=0.5, bias=1.0).then_inc(S("z_ln"), 1)
                    act.wait_ge(S("z_ln"), at(n + 1))
                    s.activation(zw[f][:], zw[f][:], ACT.Exp, scale=-1.0).then_inc(S("z_r"), 1)

                def z_hi(q, u, f):
                    n = 2 * q + f
                    act.wait_ge(S("z_h"), at(n + 1))
                    act.wait_ge(S("m_ready"), at(2 * q - 2))
                    s.copy(hh[u][:, 2 * f:2 * f + 2, :], zh[f][:].rearrange("p (a b) -> p a b", a=2)).then_inc(S("z_hi"), 1)

                def m_exp(q, f):
                    n = 2 * q + f
                    act.wait_ge(S("m_x"), at(n + 1))
                    act.wait_ge(S("seg_ready"), at(n - 1))
                    s.activation(mw[f][:], mx[f][:], ACT.Exp).then_inc(S("m_exp"), 1)

                def m_r(q, f):
                    n = 2 * q + f
                    act.wait_ge(S("m_u"), at(n + 1))
                    s.activation(mw[f][:], mw[f][:], ACT.Ln, scale=0.5, bias=1.0).then_inc(S("m_ln"), 1)
                    act.wait_ge(S("m_ln"), at(n + 1))
                    s.activation(mw[f][:], mw[f][:], ACT.Exp, scale=-1.0).then_inc(S("m_r"), 1)

                def attr_high(q):
                    act.wait_ge(S("attr_turned"), at(q + 1))
                    act.wait_ge(S("z_ready"), at(2 * q))
                    s.copy(attr[0:ED, :], psa[0:ED, :]).then_inc(S("attr_hi"), 1)

                def hidden(q, u):
                    z_exp(q, 0)
                    z_exp(q, 1)
                    z_r(q, 0)
                    z_r(q, 1)
                    z_hi(q, u, 0)
                    z_hi(q, u, 1)

                act.wait_ge(S("wc_in"), 16)
                s.copy(wch2[0:ED, :], wc[:]).then_inc(S("wc_split"), 1)
                s.copy(wch2[ED:P, :], wc[:]).then_inc(S("wc_split"), 1)
                attr_high(0)
                attr_high(1)
                high(act)
                hidden(0, 0)

                def body(q, u, back, attrs, more):
                    if more:
                        z_exp(q + 1, 0)
                        z_exp(q + 1, 1)
                        z_r(q + 1, 0)
                    m_exp(q, 0)
                    if more:
                        z_r(q + 1, 1)
                        z_hi(q + 1, 1 - u, 0)
                    m_r(q, 0)
                    if more:
                        z_hi(q + 1, 1 - u, 1)
                    m_exp(q, 1)
                    if attrs:
                        attr_high(q + 2)
                    m_r(q, 1)

                both(act, body)

            @block.vector
            def _(dve):
                v = nc.vector

                def z_u(q, f):
                    n = 2 * q + f
                    dve.wait_ge(S("z_exp"), at(n + 1))
                    v.tensor_scalar(zw[f][:], zw[f][:], CAP, None, ALU.min).then_inc(S("z_min"), 1)
                    dve.wait_ge(S("z_min"), at(n + 1))
                    mish_square(v, zw[f][:]).then_inc(S("z_u"), 1)

                def z_h(q, f):
                    n = 2 * q + f
                    dve.wait_ge(S("z_r"), at(n + 1))
                    dve.wait_ge(S("z_lo"), at(n - 1))
                    v.scalar_tensor_tensor(zh[f][:], zw[f][:], 1.0, psz[f][:], ALU.subtract, ALU.mult).then_inc(S("z_h"), 1)

                def m_u(q, f):
                    n = 2 * q + f
                    dve.wait_ge(S("m_exp"), at(n + 1))
                    v.tensor_scalar(mw[f][:], mw[f][:], CAP, None, ALU.min).then_inc(S("m_min"), 1)
                    dve.wait_ge(S("m_min"), at(n + 1))
                    mish_square(v, mw[f][:]).then_inc(S("m_u"), 1)

                def m_x(q, f):
                    n = 2 * q + f
                    dve.wait_ge(S("m_ready"), at(n + 1))
                    dve.wait_ge(S("m_msg"), at(n - 1))
                    v.tensor_tensor(mx[f][:].rearrange("p (a b) -> p a b", a=2), b2[:].unsqueeze(1).to_broadcast([P, 2, H]),
                                    psm[:].rearrange("p (a b) -> p a b", a=2), ALU.subtract).then_inc(S("m_x"), 1)

                def m_msg(q, f):
                    n = 2 * q + f
                    dve.wait_ge(S("m_r"), at(n + 1))
                    v.scalar_tensor_tensor(mw[f][:], mw[f][:], 1.0, mx[f][:], ALU.subtract, ALU.mult).then_inc(S("m_msg"), 1)

                def attr_low(q):
                    dve.wait_ge(S("attr_hi"), at(q + 1))
                    v.tensor_tensor(attr[ED:P, :], psa[0:ED, :], r32(attr[0:ED, :]), ALU.subtract).then_inc(S("attr_lo"), 1)

                def onehots(q, u):
                    dve.wait_ge(S("seg_ready"), at(2 * q - 2))
                    for k in range(4):
                        last = v.tensor_scalar(hot[u][:, k, :], K["iota"][:], K["meta"][:, bass.ds(4 * q + k, 1), 2], None, ALU.is_equal)
                    last.then_inc(S("onehot"), 1)

                def add_sums(q, f):
                    n = 2 * q + f
                    tile = dve.value_load(K["pair_tile"][0:1, bass.ds(n, 1)], min_val=0, max_val=NT - 1)
                    dve.wait_ge(S("seg_ready"), at(n + 1))
                    agg = W["agg"][:, bass.ds(tile, 1), :]
                    dve.wait_ge(S("seg_added"), at(n))
                    v.tensor_tensor(agg, agg, pss[:], ALU.add).then_inc(S("seg_added"), 1)

                def hidden(q):
                    z_u(q, 0)
                    z_u(q, 1)
                    z_h(q, 0)
                    z_h(q, 1)

                v.memset(W["agg"][:], 0.0).then_inc(S("agg_zero"), 1)
                dve.wait_ge(S("agg_zero"), 1)
                dve.wait_ge(S("wc_split"), 1)
                v.tensor_tensor(wcl[:], wc[:], r32(wch2[0:ED, :]), ALU.subtract).then_inc(S("wc_split"), 1)
                attr_low(0)
                attr_low(1)
                low(dve, v)
                hidden(0)
                dve.wait_ge(S("edge_b2_in"), 16)

                def body(q, u, back, attrs, more):
                    onehots(q, u)
                    if more:
                        z_u(q + 1, 0)
                    m_x(q, 0)
                    if more:
                        z_u(q + 1, 1)
                        z_h(q + 1, 0)
                    m_u(q, 0)
                    if more:
                        z_h(q + 1, 1)
                    if back:
                        add_sums(q - 1, 1)
                    m_x(q, 1)
                    m_msg(q, 0)
                    if attrs:
                        attr_low(q + 2)
                    m_u(q, 1)
                    m_msg(q, 1)
                    add_sums(q, 0)

                both(dve, body)
                add_sums(QUADS - 1, 1)


def update_nodes(nc, S, K, T, A, W, out):
    with ExitStack() as c:
        sb = lambda n, s, d=F32: c.enter_context(nc.sbuf_tensor(f"{n}_u", s, d))
        w3h, w3l = sb("w3h", [P, K2, H], F32R), sb("w3l", [P, K2, H], F32R)
        w4h, w4l = sb("w4h", [P, KC, H], F32R), sb("w4l", [P, KC, H], F32R)
        xa = [sb(f"xa{u}", [P, H2]) for u in range(2)]
        oh, ol = sb("oh", [P, H2], F32R), sb("ol", [P, H2], F32R)
        vx, vw, vo = sb("vx", [P, H]), sb("vw", [P, H]), sb("vo", [P, H])
        vh, vl = sb("vh", [P, H], F32R), sb("vl", [P, H], F32R)
        yy = sb("yy", [P, H])
        ft = [sb(f"ft{u}", [P, H]) for u in range(2)]
        st, mv = sb("st", [P, 6]), sb("mv", [P, 2])
        sf, mf = sb("sf", [P, 6]), sb("mf", [P, 2])
        b3, b4, ga, be = (sb(n, [P, H]) for n in ("b3", "b4", "ga", "be"))
        pso = c.enter_context(nc.psum_tensor("pso_u", [P, H2], F32))
        psv = c.enter_context(nc.psum_tensor("psv_u", [P, H], F32))
        pst = c.enter_context(nc.psum_tensor("pst_u", [P, H], F32))
        psw = c.enter_context(nc.psum_tensor("psw_u", [P, H], F32))
        w3, w4 = rows(A["L1_gnn_W3"], K2), rows(A["L1_gnn_W4"], KC)
        load, high, low = split_chunks(nc, S, c, "upd", [
            (w3[:, 2 * k:2 * k + 2, :], w3h[:, 2 * k:2 * k + 2, :], w3l[:, 2 * k:2 * k + 2, :]) for k in range(KC)] + [
            (w4[:, 2 * k:2 * k + 2, :], w4h[:, 2 * k:2 * k + 2, :], w4l[:, 2 * k:2 * k + 2, :]) for k in range(2)])

        def skewed(eng, first, second):
            first(0, 0)
            with eng.Fori(0, NT // 2 - 1) as it:
                first(2 * it + 1, 1)
                second(2 * it, 0, it)
                first(2 * it + 2, 0)
                second(2 * it + 1, 1, it)
            first(NT - 1, 1)
            second(NT - 2, 0, NT // 2 - 1)
            second(NT - 1, 1, NT // 2 - 1)

        with nc.Block() as block:
            @block.sync
            def _(sp):
                load(sp)
                for tile, name in ((b3, "b3"), (b4, "b4"), (ga, "gamma"), (be, "beta")):
                    sp.dma_start(tile[:], A[f"L1_gnn_{name}"].partition_broadcast(P)).then_inc(S("upd_rows"), 16)
                whole = out[0:(NT - 1) * P, :].rearrange("(j p) d -> p j d", p=P)

                def store(i, u):
                    sp.wait_ge(S("f_out"), at(i + 1))
                    sp.dma_start(whole[:, bass.ds(i, 1), :], ft[u][:]).then_inc(S(f"f_stored{u}"), 16)

                with sp.Fori(0, NT // 2 - 1) as it:
                    for u in range(2):
                        store(2 * it + u, u)
                store(NT - 2, 0)
                sp.wait_ge(S("f_out"), at(NT))
                sp.dma_start(out[(NT - 1) * P:N, :], ft[1][0:LAST, :]).then_inc(S("f_stored1"), 16)
                for u in range(2):
                    sp.wait_ge(S(f"f_stored{u}"), dma_at(NT // 2))

            @block.gpsimd
            def _(pool):
                g = nc.gpsimd

                def keep(i, u):
                    pool.wait_ge(S("f_sum"), at(i - 1))
                    carry(pool, S)
                    g.tensor_copy(xa[u][:, 0:H], W["X"][:, bass.ds(i, 1), :]).then_inc(S("o_kept"), 1)
                    g.tensor_copy(xa[u][:, H:H2], W["agg"][:, bass.ds(i, 1), :]).then_inc(S("o_agg"), 1)

                with pool.Fori(0, NT // 2) as it:
                    for u in range(2):
                        keep(2 * it + u, u)

            @block.tensor
            def _(pe):
                t = nc.tensor

                def first(i, u):
                    pe.wait_ge(S("o_agg"), at(i + 1))
                    pe.wait_ge(S("o_lo"), at(i))
                    turn_tile(t, pso, xa[u], K2, K["ident"][:]).then_inc(S("o_turned"), 1)
                    pe.wait_ge(S("o_lo"), at(i + 1))
                    pe.wait_ge(S("v_x"), at(i))
                    three(t, psv[:], oh, ol, lambda k: w3h[:, k, :], lambda k: w3l[:, k, :], K2,
                          lambda a, k: a[:, k * P:(k + 1) * P]).then_inc(S("v_psum"), 1)

                def second(i, u, half):
                    pe.wait_ge(S("v_out"), at(i + 1))
                    pe.wait_ge(S("v_lo"), at(i))
                    turn_tile(t, pst, vo, KC, K["ident"][:]).then_inc(S("v_turned"), 1)
                    pe.wait_ge(S("v_lo"), at(i + 1))
                    pe.wait_ge(S("f_y"), at(i))
                    three(t, psw[:], vh, vl, lambda k: w4h[:, k, :], lambda k: w4l[:, k, :], KC,
                          lambda a, k: a[:, k * P:(k + 1) * P]).then_inc(S("w_psum"), 1)

                pe.wait_ge(S("upd_lo"), KC + 2)
                skewed(pe, first, second)

            @block.scalar
            def _(act):
                s = nc.scalar
                s.preload_act_table_set(EXP_AND_LOG)

                def first(i, u):
                    act.wait_ge(S("o_turned"), at(i + 1))
                    act.wait_ge(S("v_psum"), at(i))
                    s.copy(oh[:, 0:H], pso[:, 0:H])
                    s.mul(oh[:, H:H2], pso[:, H:H2], -1.0).then_inc(S("o_hi"), 1)
                    act.wait_ge(S("v_x"), at(i + 1))
                    act.wait_ge(S("v_out"), at(i))
                    s.activation(vw[:], vx[:], ACT.Exp).then_inc(S("v_exp"), 1)
                    act.wait_ge(S("v_u"), at(i + 1))
                    s.activation(vw[:], vw[:], ACT.Ln, scale=0.5, bias=1.0).then_inc(S("v_ln"), 1)
                    act.wait_ge(S("v_ln"), at(i + 1))
                    s.activation(vw[:], vw[:], ACT.Exp, scale=-1.0).then_inc(S("v_r"), 1)

                def second(i, u, half):
                    act.wait_ge(S("v_turned"), at(i + 1))
                    act.wait_ge(S("w_psum"), at(i))
                    s.copy(vh[:], pst[:]).then_inc(S("v_hi"), 1)
                    rstd(nc, act, K, mv, S, i, "f_stat1", "f_log1", "f_rstd1")
                    rstd(nc, act, K, mf, S, i, "f_stat2", "f_log2", "f_rstd2")

                high(act)
                skewed(act, first, second)

            @block.vector
            def _(dve):
                v = nc.vector

                def first(i, u):
                    dve.wait_ge(S("o_hi"), at(i + 1))
                    v.tensor_tensor(ol[:, 0:H], pso[:, 0:H], r32(oh[:, 0:H]), ALU.subtract)
                    v.scalar_tensor_tensor(ol[:, H:H2], pso[:, H:H2], -1.0, r32(oh[:, H:H2]), ALU.mult, ALU.subtract).then_inc(S("o_lo"), 1)
                    dve.wait_ge(S("v_psum"), at(i + 1))
                    dve.wait_ge(S("v_out"), at(i))
                    v.tensor_tensor(vx[:], psv[:], b3[:], ALU.add).then_inc(S("v_x"), 1)
                    dve.wait_ge(S("v_exp"), at(i + 1))
                    v.tensor_scalar(vw[:], vw[:], CAP, None, ALU.min).then_inc(S("v_min"), 1)
                    dve.wait_ge(S("v_min"), at(i + 1))
                    mish_square(v, vw[:]).then_inc(S("v_u"), 1)
                    dve.wait_ge(S("v_r"), at(i + 1))
                    dve.wait_ge(S("v_turned"), at(i))
                    v.scalar_tensor_tensor(vo[:], vw[:], 1.0, vx[:], ALU.subtract, ALU.mult).then_inc(S("v_out"), 1)

                def second(i, u, half):
                    dve.wait_ge(S("v_hi"), at(i + 1))
                    v.tensor_tensor(vl[:], pst[:], r32(vh[:]), ALU.subtract).then_inc(S("v_lo"), 1)
                    dve.wait_ge(S("f_sum"), at(i))
                    dve.wait_ge(S("f_out"), at(i))
                    v.tensor_tensor(yy[:], xa[u][:, 0:H], b4[:], ALU.add).then_inc(S("f_base"), 1)
                    dve.wait_ge(S("w_psum"), at(i + 1))
                    dve.wait_ge(S("f_base"), at(i + 1))
                    v.tensor_tensor(yy[:], yy[:], psw[:], ALU.subtract).then_inc(S("f_y"), 1)
                    dve.wait_ge(S("f_y"), at(i + 1))
                    mean_var(nc, dve, yy, 1, st, mv[:], S, i, "f_stat1", "f_parts1")
                    dve.wait_ge(S("f_rstd1"), at(i + 1))
                    v.tensor_scalar(yy[:], yy[:], mv[:, 0:1], mv[:, 1:2], ALU.subtract, ALU.mult).then_inc(S("f_norm1"), 1)
                    dve.wait_ge(S("f_norm1"), at(i + 1))
                    v.tensor_tensor(yy[:], yy[:], ga[:], ALU.mult).then_inc(S("f_scaled"), 1)
                    dve.wait_ge(S("f_scaled"), at(i + 1))
                    v.tensor_tensor(yy[:], yy[:], be[:], ALU.add).then_inc(S("f_shifted"), 1)
                    dve.wait_ge(S("f_shifted"), at(i + 1))
                    v.tensor_tensor(yy[:], yy[:], xa[u][:, 0:H], ALU.add).then_inc(S("f_sum"), 1)
                    dve.wait_ge(S("f_sum"), at(i + 1))
                    mean_var(nc, dve, yy, 1, sf, mf[:], S, i, "f_stat2", "f_parts2")
                    dve.wait_ge(S("f_rstd2"), at(i + 1))
                    dve.wait_ge(S(f"f_stored{u}"), dma_at(half))
                    v.tensor_scalar(ft[u][:], yy[:], mf[:, 0:1], mf[:, 1:2], ALU.subtract, ALU.mult).then_inc(S("f_out"), 1)

                low(dve, v)
                dve.wait_ge(S("upd_rows"), 64)
                skewed(dve, first, second)


def program(nc, A, out):
    ctx = ExitStack()
    with ctx:
        S = Sems(nc, 1)
        sb = lambda n, s, d=F32: ctx.enter_context(nc.sbuf_tensor(n, s, d))
        dram = lambda n, s: nc.dram_tensor(n, s, F32, kind="Internal").ap()
        K = {"ident": sb("ident", [P, P]), "ones": sb("ones", [P, P]), "zeros": sb("zeros", [P, H]),
             "iota": sb("iota", [P, P]), "iota_n": sb("iota_n", [P, NP], F16), "ln_eps": sb("ln_eps", [P, 1]),
             "pair_tile": sb("pair_tile", [P, PAIRS], I32), "meta": sb("meta", [P, TILES, 4]),
             "src_dst": sb("src_dst", [P, TILES, 2], I32)}
        T = {"table": dram("table", (ROWS, ROW)), "x": [dram(f"x{l}", (NP, H)) for l in range(4)],
             "src_part": dram("src_part", (NP, H)), "dst_part": dram("dst_part", (NP, H))}
        with ExitStack() as first:
            s0 = lambda n, s, d=F32: first.enter_context(nc.sbuf_tensor(n, s, d))
            K["counts"] = s0("counts", [P, NT, NP], F32R)
            sort_edges(nc, S, K, T, A)
            count_edges(nc, S, K, T)
            W = {"hT": s0("hT", [P, KC, NP]), "w1h": s0("w1h", [P, KC, H2], F32R), "w1l": s0("w1l", [P, KC, H2], F32R),
                 "b1": s0("b1", [P, H2]), "b2": s0("b2", [P, H]), "g1": s0("g1", [P, K2]), "a1": s0("a1", [P, K2]),
                 "g2": s0("g2", [P, H]), "a2": s0("a2", [P, H])}
            for l in range(3):
                aggregate(nc, S, K, T, A, W, l)
                feed_forward(nc, S, K, T, A, W, l)
        S.close()
        S = Sems(nc, 2)
        W = {"X": sb("X", [P, NT, H]), "agg": sb("agg", [P, NT, H])}
        join_layers(nc, S, K, T, A, W)
        edge_messages(nc, S, K, T, A, W)
        update_nodes(nc, S, K, T, A, W, out)


_OUT = (N, H)


def kernel(**inputs):
    import numpy as np
    import concourse.bacc as bacc
    from concourse.bass_utils import run_bass_kernel_spmd as run

    nc = bacc.Bacc("TRN2", target_bir_lowering=False, num_devices=1)
    arrays, A = {}, {}
    for name, value in inputs.items():
        a = np.ascontiguousarray(value)
        arrays[f"in_{name}"] = a
        A[name] = nc.dram_tensor(f"in_{name}", a.shape, mybir.dt.from_np(a.dtype), kind="ExternalInput").ap()
    out = nc.dram_tensor("out", _OUT, F32, kind="ExternalOutput").ap()
    program(nc, A, out)
    return run(nc, [arrays], core_ids=[0]).results[0]["out"]
```

```python
import concourse.bass as bass
from concourse import mybir
from contextlib import ExitStack

F32 = mybir.dt.float32
F32R = mybir.dt.float32r
BF16 = mybir.dt.bfloat16
F16 = mybir.dt.float16
I32 = mybir.dt.int32
ALU = mybir.AluOpType
ACT = mybir.ActivationFunctionType
AX = mybir.AxisListType

P = 128
N, H, E, ED = 1250, 512, 21250, 64
NT = (N + P - 1) // P
NP = NT * P
LAST = N - (NT - 1) * P
KC = H // P
H2 = 2 * H
K2 = H2 // P
EP, EJ = 125, E // 125
PAIRS = (E + NT * 255) // 256
QUADS = PAIRS // 2
TILES = 2 * PAIRS
ROWS = TILES * P
ROW = ED + 4
SC = 10
PARTS = (0, 2, 6, EJ // SC)
EPS = 1e-7
LN_EPS = 1e-5
TINY = 1e-16
EXP_AND_LOG = "natural_log_exp_and_others"
CAP = float(2 ** 24)
NB = [(0, 512), (512, 512), (1024, 256)]


def carry(eng, S):
    eng.sem_inc(S("carried"), 1)


def r32(ap):
    return ap.bitcast(F32)


CREDIT, DMA_CREDIT = 2, 32
CREDITED_1 = ("onehots pair_counted pair_added h_hi h_lo u_psum u_added parts1 stat1 log1 rstd1 normed g_turned g_relu g_hi g_lo "
              "x_psum x_added parts2 stat2 log2 rstd2 x_normed x_scaled x_shifted x_out").split()
CREDITED_DMA_1 = "old_in0 old_in1 x_stored0 x_stored1".split()
CREDITED_2 = ("cat_turned cat_hi cat_lo y_psum y_biased y_added y_parts y_stat y_log y_rstd y_norm x_kept n_turned n_hi n_lo pq_psum p_out q_out "
              "index_copied attr_turned attr_hi attr_lo z_ready z_exp z_min z_u z_ln z_r z_h z_hi z_lo "
              "m_ready m_x m_exp m_min m_u m_ln m_r m_msg onehot seg_ready seg_added "
              "o_kept o_turned o_hi o_lo v_psum v_x v_exp v_min v_u v_ln v_r v_out v_turned v_hi v_lo w_psum "
              "f_y f_parts1 f_stat1 f_log1 f_rstd1 f_scaled f_sum f_parts2 f_stat2 f_log2 f_rstd2 f_out").split()
CREDITED_DMA_2 = "cat_in0 cat_in1 p_stored q_stored attr_in0 attr_in1 f_stored0 f_stored1".split()


def at(n):
    return n + CREDIT


def dma_at(n):
    return 16 * n + DMA_CREDIT


class Sems:

    def __init__(self, nc, half):
        self.nc, self.half, self.made = nc, half, {}

    def __call__(self, name):
        if name not in self.made:
            self.made[name] = self.nc.alloc_semaphore(name=f"{name}.{self.half}")
        return self.made[name]

    def give_credit(self, eng, compute, dma):
        for name in compute:
            eng.sem_inc(self(name), CREDIT)
        for name in dma:
            eng.sem_inc(self(name), DMA_CREDIT)

    def close(self):
        self.nc.clear_and_free_semaphores(list(self.made.values()))
        self.nc.all_engine_barrier()


def sort_edges(nc, S, K, T, A):
    with ExitStack() as c:
        sb = lambda n, s, d=F32: c.enter_context(nc.sbuf_tensor(n, s, d))
        src_i, dst_i = sb("src_i", [EP, EJ], I32), sb("dst_i", [EP, EJ], I32)
        bkt_i = sb("bkt_i", [EP, EJ], I32)
        src_f, dst_f, bkt_f = sb("src_f", [EP, EJ]), sb("dst_f", [EP, EJ]), sb("bkt_f", [EP, EJ])
        oh, cum = sb("oh", [EP, NT, EJ]), sb("cum", [EP, NT, EJ])
        ones_e = sb("ones_e", [EP, EJ])
        pos, tmp = sb("pos", [EP, EJ]), sb("tmp", [EP, EJ])
        pos_i = sb("pos_i", [EP, EJ], I32)
        pay = sb("pay", [EP, EJ, ROW])
        payb = [sb(f"payb{u}", [EP, SC, ROW]) for u in range(2)]
        posb = [sb(f"posb{u}", [EP, SC], I32) for u in range(2)]
        dum = sb("dum", [P, ROW])
        below = sb("below", [EP, EP])
        tot, npair, incl, excl = (sb(n, [P, NT]) for n in ("tot", "npair", "incl", "excl"))
        tot_i = sb("tot_i", [P, NT], I32)
        base = sb("base", [EP, NT])
        qi, qd, qs = sb("qi", [P, PAIRS]), sb("qd", [P, PAIRS]), sb("qs", [P, PAIRS])
        pc = c.enter_context(nc.psum_tensor("pc", [P, 512], F32))
        table_rows = T["table"]
        BATCHES = EJ // SC
        with nc.Block() as block:
            @block.sync
            def _(sp):
                S.give_credit(sp, CREDITED_1, CREDITED_DMA_1)
                sp.dma_start(dst_i[:], A["dst"].rearrange("(p j) -> p j", p=EP)).then_inc(S("dst_in"), 16)
                sp.dma_start(src_i[:], A["src"].rearrange("(p j) -> p j", p=EP)).then_inc(S("src_in"), 16)
                sp.wait_ge(S("dummy_set"), 2)
                sp.dma_start(table_rows.rearrange("(p r) f -> p r f", p=P),
                             dum[:].unsqueeze(1).to_broadcast([P, ROWS // P, ROW])).then_inc(S("table_filled"), 16)
                attr = A["edge_attr_64"].rearrange("(p j) f -> p j f", p=EP)
                for k, (a, b) in enumerate(zip(PARTS, PARTS[1:])):
                    sp.dma_start(pay[:, a * SC:b * SC, 0:ED], attr[:, a * SC:b * SC, :]).then_inc(S(f"attr_in{k}"), 16)
                sp.dma_start(T["x"][0][0:N, :], A["x"]).then_inc(S("x_padded"), 16)
                sp.wait_ge(S("zero_set"), 1)
                sp.dma_start(T["x"][0][N:NP, :], K["zeros"][0:NP - N, :]).then_inc(S("x_padded"), 16)
                sp.wait_ge(S("x_padded"), 32)
                sp.wait_ge(S("table_filled"), 16)

            @block.gpsimd
            def _(pool):
                g = nc.gpsimd
                g.memset(K["ident"][:], 0.0).then_inc(S("ident_0"), 1)
                g.memset(K["zeros"][:], 0.0).then_inc(S("zero_set"), 1)
                g.memset(below[:], 1.0).then_inc(S("below_1"), 1)
                g.memset(K["ones"][:], 1.0).then_inc(S("const_ready"), 1)
                g.iota(K["iota"][:], [[1, P]], base=0, channel_multiplier=0,
                       allow_small_or_imprecise_dtypes=True).then_inc(S("const_ready"), 1)
                g.iota(K["iota_n"][:], [[1, NP]], base=0, channel_multiplier=0,
                       allow_small_or_imprecise_dtypes=True).then_inc(S("const_ready"), 1)
                g.iota(qi[:], [[1, PAIRS]], base=0, channel_multiplier=0,
                       allow_small_or_imprecise_dtypes=True).then_inc(S("const_ready"), 1)
                pool.wait_ge(S("below_1"), 1)
                g.affine_select(out=below[:], in_=below[:], compare_op=ALU.is_gt, fill=0.0, base=0,
                                pattern=[[1, EP]], channel_multiplier=-1).then_inc(S("const_ready"), 1)
                pool.wait_ge(S("ident_0"), 1)
                g.affine_select(out=K["ident"][:], in_=K["ident"][:], compare_op=ALU.not_equal, fill=1.0, base=0,
                                pattern=[[-1, P]], channel_multiplier=1).then_inc(S("const_ready"), 1)
                pool.wait_ge(S("table_filled"), 16)

                def scatter(n, u):
                    pool.wait_ge(S("batch_ready"), 2 * n + 2)
                    carry(pool, S)
                    for s in range(SC):
                        g.indirect_dma_start(out=table_rows, out_offset=bass.IndirectOffsetOnAxis(ap=posb[u][:, s:s + 1], axis=0),
                                             in_=payb[u][:, s, :], in_offset=None).then_inc(S(f"scattered{u}"), 16)

                with pool.Fori(0, BATCHES // 2) as it:
                    for u in range(2):
                        scatter(2 * it + u, u)
                scatter(BATCHES - 1, 0)
                pool.wait_ge(S("scattered0"), 16 * SC * (BATCHES // 2 + 1))
                pool.wait_ge(S("scattered1"), 16 * SC * (BATCHES // 2))

            @block.tensor
            def _(pe):
                pe.wait_ge(S("const_ready"), 6)
                pe.wait_ge(S("counted"), NT)
                counts = cum[:, :, EJ - 1]
                nc.tensor.matmul(pc[0:EP, 0:NT], below[:], counts, start=True, stop=True)
                nc.tensor.matmul(pc[:, 64:64 + NT], K["ones"][0:EP, :], counts, start=True, stop=True).then_inc(S("count_sums"), 1)

            @block.vector
            def _(dve):
                v = nc.vector
                done = [0]

                def step(ins):
                    done[0] += 1
                    ins.then_inc(S("sort_steps"), 1)
                    dve.wait_ge(S("sort_steps"), done[0])

                v.memset(dum[:], 0.0).then_inc(S("dummy_set"), 1)
                dve.wait_ge(S("dummy_set"), 1)
                v.memset(dum[:, ED + 2:ED + 3], -1.0).then_inc(S("dummy_set"), 1)
                step(v.memset(ones_e[:], 1.0))
                dve.wait_ge(S("dst_in"), 16)
                v.tensor_copy(dst_f[:], dst_i[:])
                step(v.tensor_single_scalar(bkt_i[:], dst_i[:], 7, ALU.arith_shift_right))
                step(v.tensor_copy(bkt_f[:], bkt_i[:]))
                for b in range(NT):
                    step(v.tensor_single_scalar(oh[:, b, :], bkt_f[:], float(b), ALU.is_equal))
                    v.tensor_tensor_scan(cum[:, b, :], ones_e[:], oh[:, b, :], 0.0, ALU.mult, ALU.add).then_inc(S("counted"), 1)
                dve.wait_ge(S("src_in"), 16)
                v.tensor_copy(src_f[:], src_i[:])
                dve.wait_ge(S("count_sums"), 1)
                step(v.tensor_copy(tot[:], pc[:, 64:64 + NT]))
                step(v.tensor_scalar(tot[:], tot[:], 255.0, None, ALU.add))
                step(v.tensor_copy(tot_i[:], tot[:]))
                step(v.tensor_single_scalar(tot_i[:], tot_i[:], 8, ALU.arith_shift_right))
                step(v.tensor_copy(npair[:], tot_i[:]))
                step(v.tensor_tensor_scan(incl[:], ones_e[0:P, 0:NT] if EP >= P else K["ones"][:, 0:NT], npair[:], 0.0, ALU.mult, ALU.add))
                step(v.tensor_tensor(excl[:], incl[:], npair[:], ALU.subtract))
                step(v.tensor_scalar(base[:], excl[0:EP, :], 256.0, -1.0, ALU.mult, ALU.add))
                step(v.tensor_tensor(base[:], base[:], pc[0:EP, 0:NT], ALU.add))
                step(v.memset(pos[:], 0.0))
                for b in range(NT):
                    step(v.scalar_tensor_tensor(tmp[:], cum[:, b, :], base[:, b:b + 1], oh[:, b, :], ALU.add, ALU.mult))
                    step(v.tensor_tensor(pos[:], pos[:], tmp[:], ALU.add))
                step(v.tensor_copy(pos_i[:], pos[:]))
                v.tensor_copy(pay[:, :, ED], src_f[:])
                v.tensor_copy(pay[:, :, ED + 1], dst_f[:])
                v.memset(pay[:, :, ED + 3], 0.0)
                step(v.scalar_tensor_tensor(pay[:, :, ED + 2], bkt_f[:], -float(P), dst_f[:], ALU.mult, ALU.add))

                def batch(n, u):
                    v.tensor_copy(payb[u][:], pay[:, bass.ds(n * SC, SC), :]).then_inc(S("batch_ready"), 1)
                    v.tensor_copy(posb[u][:], pos_i[:, bass.ds(n * SC, SC)]).then_inc(S("batch_ready"), 1)

                dve.wait_ge(S("attr_in0"), 16)
                for u in range(2):
                    batch(u, u)
                dve.wait_ge(S("const_ready"), 6)
                step(v.memset(qd[:], -1.0))
                for b in range(NT):
                    step(v.tensor_scalar(qs[:], qi[:], excl[:, b:b + 1], None, ALU.is_ge))
                    step(v.tensor_tensor(qd[:], qd[:], qs[:], ALU.add))
                step(v.tensor_copy(K["pair_tile"][:], qd[:]))
                v.memset(K["counts"][:].bitcast(F32), 0.0).then_inc(S("counts_zero"), 1)
                v.memset(K["ln_eps"][:], LN_EPS).then_inc(S("counts_zero"), 1)
                for k in (1, 2):
                    dve.wait_ge(S(f"attr_in{k}"), 16)
                    with dve.Fori(PARTS[k] // 2, PARTS[k + 1] // 2) as it:
                        dve.wait_ge(S("scattered0"), 16 * SC * it)
                        batch(2 * it, 0)
                        dve.wait_ge(S("scattered1"), 16 * SC * it)
                        batch(2 * it + 1, 1)
                dve.wait_ge(S("scattered0"), 16 * SC * (BATCHES // 2))
                batch(BATCHES - 1, 0)


def count_edges(nc, S, K, T):
    with ExitStack() as c:
        sb = lambda n, s, d=F32: c.enter_context(nc.sbuf_tensor(n, s, d))
        oh_src = [sb(f"oh_src{u}", [P, 2, NP], BF16) for u in range(2)]
        oh_dst = [sb(f"oh_dst{u}", [P, 2, P], BF16) for u in range(2)]
        ps = [c.enter_context(nc.psum_tensor(f"pcount{u}", [P, 3 * 512], F32)) for u in range(2)]
        meta, counts = K["meta"], K["counts"]
        PART = TILES // 4
        with nc.Block() as block:
            @block.sync
            def _(sp):
                for k in range(4):
                    sp.dma_start(meta[:, k * PART:(k + 1) * PART, :],
                                 T["table"].rearrange("(t p) f -> p t f", p=P)[:, k * PART:(k + 1) * PART, ED:ROW]).then_inc(S(f"meta_in{k}"), 16)

            def pair(eng, q, u):
                v = nc.vector
                eng.wait_ge(S("pair_counted"), at(q - 1))
                for k in range(2):
                    v.tensor_scalar(oh_dst[u][:, k, :], K["iota"][:], meta[:, bass.ds(2 * q + k, 1), 2], None, ALU.is_equal)
                    last = v.tensor_scalar(oh_src[u][:, k, :], K["iota_n"][:], meta[:, bass.ds(2 * q + k, 1), 0], None, ALU.is_equal)
                last.then_inc(S("onehots"), 1)

            def add(eng, q, u):
                v = nc.vector
                tile = eng.value_load(K["pair_tile"][0:1, bass.ds(q, 1)], min_val=0, max_val=NT - 1)
                eng.wait_ge(S("pair_counted"), at(q + 1))
                dst = counts[:, :, bass.ds(tile * P, P)]
                eng.wait_ge(S("pair_added"), at(q))
                v.tensor_tensor(dst, r32(dst), ps[u][:, 0:NP].rearrange("p (j d) -> p j d", j=NT), ALU.add).then_inc(S("pair_added"), 1)

            @block.vector
            def _(dve):
                for k in range(4):
                    dve.wait_ge(S(f"meta_in{k}"), 16)
                nc.vector.tensor_copy(K["src_dst"][:], meta[:, :, 0:2]).then_inc(S("index_ready"), 1)
                pair(dve, 0, 0)
                with dve.Fori(0, PAIRS // 2 - 1) as it:
                    for u in range(2):
                        pair(dve, 2 * it + u + 1, 1 - u)
                        add(dve, 2 * it + u, u)
                pair(dve, PAIRS - 1, 1)
                add(dve, PAIRS - 2, 0)
                add(dve, PAIRS - 1, 1)

            @block.tensor
            def _(pe):
                with pe.Fori(0, PAIRS // 2) as it:
                    for u in range(2):
                        q = 2 * it + u
                        pe.wait_ge(S("onehots"), at(q + 1))
                        pe.wait_ge(S("pair_added"), at(q - 1))
                        for k in range(2):
                            for j in range(NT):
                                last = nc.tensor.matmul(ps[u][:, j * P:(j + 1) * P], oh_src[u][:, k, j * P:(j + 1) * P],
                                                        oh_dst[u][:, k, :], start=k == 0 and j % 4 == 0,
                                                        stop=k == 1 and (j % 4 == 3 or j == NT - 1), skip_group_check=True)
                        last.then_inc(S("pair_counted"), 1)


def split_chunks(nc, S, c, tag, jobs, before=0):
    st = [c.enter_context(nc.sbuf_tensor(f"{tag}_stage{u}_{before}", [P, 1024], F32)) for u in range(2)]

    def view(k):
        n = jobs[k][0].shape[1]
        return st[k % 2][:].rearrange("p (n m) -> p n m", n=n)

    def load(eng):
        for k, (src, hi, lo) in enumerate(jobs):
            if k >= 2:
                eng.wait_ge(S(f"{tag}_lo"), before + k - 1)
            eng.dma_start(view(k), src).then_inc(S(f"{tag}_in{k % 2}"), 16)

    def high(eng):
        for k, (src, hi, lo) in enumerate(jobs):
            eng.wait_ge(S(f"{tag}_in{k % 2}"), 16 * (before // 2 + k // 2 + 1))
            nc.scalar.copy(hi, view(k)).then_inc(S(f"{tag}_hi"), 1)

    def low(eng, alu, ks=None):
        for k in ks or range(len(jobs)):
            src, hi, lo = jobs[k]
            eng.wait_ge(S(f"{tag}_hi"), before + k + 1)
            alu.tensor_tensor(lo, view(k), r32(hi), ALU.subtract).then_inc(S(f"{tag}_lo"), 1)

    return load, high, low


def rows(ap, n):
    return ap.rearrange("(n p) m -> p n m", p=P)


def aggregate(nc, S, K, T, A, W, l):
    with ExitStack() as c:
        sb = lambda n, s, d=F32: c.enter_context(nc.sbuf_tensor(f"{n}_{l}", s, d))
        xc = [sb(f"xc{u}", [P, NT, P]) for u in range(2)]
        m, e, em = (sb(n, [P, NT, P]) for n in ("m", "e", "em"))
        eh, el, mh, ml = ([sb(f"{n}{u}", [P, NT, P], F32R) for u in range(2)] for n in ("eh", "el", "mh", "ml"))
        pmax, top, dg = sb("pmax", [P, P]), sb("top", [P, 1]), sb("dg", [P, P])
        rden = sb("rden", [P, 512])
        tcol = sb("tcol", [P, 1])
        psd, psn, psx = ([c.enter_context(nc.psum_tensor(f"{n}{u}_{l}", [P, 512], F32)) for u in range(2)] for n in ("psd", "psn", "psx"))
        psk = c.enter_context(nc.psum_tensor(f"psk_{l}", [P, P], F32))
        psb = c.enter_context(nc.psum_tensor(f"psb_{l}", [P, P], F32))
        w1 = A[f"L0_gnn_mw1_{l}"]
        load, high, low = split_chunks(nc, S, c, "w1", [
            (rows(w1, KC)[:, k:k + 1, :], W["w1h"][:, k:k + 1, :], W["w1l"][:, k:k + 1, :]) for k in range(KC)], KC * l)
        n, kb, ib = S, KC * l, 3 * KC * l
        row = lambda name: A[name].partition_broadcast(P)
        with nc.Block() as block:
            @block.sync
            def _(sp):
                sp.dma_start(tcol[:], row(f"L0_gnn_t{l}")).then_inc(n("t_in"), 16)
                for k in range(KC):
                    if k >= 2:
                        sp.wait_ge(n("x_turned"), kb + k - 1)
                        sp.wait_ge(n("m_set"), kb + k - 1)
                    sp.dma_start(xc[k % 2][:], T["x"][l].rearrange("(j p) d -> p j d", p=P)[:, :, k * P:(k + 1) * P]).then_inc(n(f"xc_in{k % 2}"), 16)
                    if k == 1:
                        load(sp)
                sp.dma_start(W["b1"][:], row(f"L0_gnn_mb1_{l}")).then_inc(n("rows_in"), 16)
                sp.dma_start(W["b2"][:], row(f"L0_gnn_mb2_{l}")).then_inc(n("rows_in"), 16)
                sp.dma_start(W["g1"][:], A[f"L0_gnn_mlg_{l}"].rearrange("(k p) -> p k", p=P), allow_slow_non_contiguous=True).then_inc(n("rows_in"), 16)
                sp.dma_start(W["a1"][:], A[f"L0_gnn_mlb_{l}"].rearrange("(k p) -> p k", p=P), allow_slow_non_contiguous=True).then_inc(n("rows_in"), 16)
                if l:
                    sp.dma_start(W["g2"][:], row(f"L0_gnn_lng_{l}")).then_inc(n("rows_in"), 16)
                    sp.dma_start(W["a2"][:], row(f"L0_gnn_lnb_{l}")).then_inc(n("rows_in"), 16)
                sp.wait_ge(n("rows_in"), [64, 160, 256][l])

            def prepare(dve, k):
                v = nc.vector
                dve.wait_ge(n(f"xc_in{k % 2}"), 16 * (2 * l + k // 2 + 1))
                if k:
                    dve.wait_ge(n("em_set"), kb + k)
                    dve.wait_ge(n("e_hi"), kb + k)
                    dve.wait_ge(n("e_lo"), kb + k)
                v.tensor_scalar(m[:], xc[k % 2][:], 0.0, EPS, ALU.max, ALU.add).then_inc(n("m_set"), 1)
                dve.wait_ge(n("m_set"), kb + k + 1)
                v.tensor_scalar(e[:], m[:], tcol[:], None, ALU.mult).then_inc(n("z_set"), 1)
                dve.wait_ge(n("z_set"), kb + k + 1)
                v.tensor_reduce(pmax[:], e[:].rearrange("p j c -> p c j"), AX.X, ALU.max).then_inc(n("pmax_set"), 1)
                dve.wait_ge(n("max_turned"), kb + k + 1)
                v.tensor_reduce(top[:], psk[:], AX.X, ALU.max).then_inc(n("top_set"), 1)
                dve.wait_ge(n("top_set"), kb + k + 1)
                v.tensor_scalar(dg[:], K["ident"][:], top[:], None, ALU.mult).then_inc(n("dg_set"), 1)
                dve.wait_ge(n("max_spread"), kb + k + 1)
                v.tensor_tensor(e[:], e[:], psb[:].unsqueeze(1).to_broadcast([P, NT, P]), ALU.subtract).then_inc(n("z_low"), 1)

            def weigh(dve, k):
                v = nc.vector
                dve.wait_ge(n("e_set"), kb + k + 1)
                if k:
                    dve.wait_ge(n("m_lo"), kb + k)
                v.tensor_tensor(em[:], e[:], m[:], ALU.mult).then_inc(n("em_set"), 1)

            def finish(dve, k, b):
                v = nc.vector
                c0, w = NB[b]
                i, u = 3 * k + b, (3 * k + b) % 2
                dve.wait_ge(n("bank_ready"), ib + i + 1)
                if i:
                    dve.wait_ge(n("h_set"), ib + i)
                v.tensor_scalar(rden[:, 0:w], psd[u][:, 0:w], TINY, None, ALU.add).then_inc(n("den_set"), 1)
                dve.wait_ge(n("den_set"), ib + i + 1)
                v.reciprocal(rden[:, 0:w], rden[:, 0:w]).then_inc(n("rden_set"), 1)
                dve.wait_ge(n("rden_set"), ib + i + 1)
                h = W["hT"][:, k, c0:c0 + w]
                v.tensor_tensor(h, rden[:, 0:w], psn[u][:, 0:w], ALU.mult).then_inc(n("agg_set"), 1)
                dve.wait_ge(n("agg_set"), ib + i + 1)
                v.tensor_tensor(h, h, psx[u][:, 0:w], ALU.add).then_inc(n("h_set"), 1)

            @block.vector
            def _(dve):
                dve.wait_ge(n("t_in"), 16 * (l + 1))
                prepare(dve, 0)
                weigh(dve, 0)
                for k in range(KC):
                    if k + 1 < KC:
                        prepare(dve, k + 1)
                    finish(dve, k, 0)
                    if k + 1 < KC:
                        weigh(dve, k + 1)
                    finish(dve, k, 1)
                    finish(dve, k, 2)

            @block.scalar
            def _(act):
                s = nc.scalar
                s.preload_act_table_set(EXP_AND_LOG)
                for k in range(KC):
                    act.wait_ge(n("z_low"), kb + k + 1)
                    s.activation(e[:], e[:], ACT.Exp).then_inc(n("e_set"), 1)
                    if k >= 2:
                        act.wait_ge(n("bank_ready"), ib + 3 * (k - 1))
                    act.wait_ge(n("e_set"), kb + k + 1)
                    s.copy(eh[k % 2][:], e[:]).then_inc(n("e_hi"), 1)
                    act.wait_ge(n("em_set"), kb + k + 1)
                    s.copy(mh[k % 2][:], em[:]).then_inc(n("m_hi"), 1)
                    if k == 0:
                        high(act)

            @block.gpsimd
            def _(pool):
                g = nc.gpsimd
                for k in range(KC):
                    pool.wait_ge(n("e_hi"), kb + k + 1)
                    g.tensor_tensor(el[k % 2][:], e[:], r32(eh[k % 2][:]), ALU.subtract).then_inc(n("e_lo"), 1)
                    pool.wait_ge(n("m_hi"), kb + k + 1)
                    g.tensor_tensor(ml[k % 2][:], em[:], r32(mh[k % 2][:]), ALU.subtract).then_inc(n("m_lo"), 1)
                    if k == 0:
                        low(pool, g)

            @block.tensor
            def _(pe):
                t = nc.tensor

                def spread_max(k):
                    pe.wait_ge(n("pmax_set"), kb + k + 1)
                    if k:
                        pe.wait_ge(n("top_set"), kb + k)
                    t.transpose(psk[:], pmax[:], K["ident"][:]).then_inc(n("max_turned"), 1)
                    pe.wait_ge(n("dg_set"), kb + k + 1)
                    if k:
                        pe.wait_ge(n("z_low"), kb + k)
                    t.matmul(psb[:], K["ones"][:], dg[:], start=True, stop=True).then_inc(n("max_spread"), 1)

                spread_max(0)
                for k in range(KC):
                    for b, (c0, w) in enumerate(NB):
                        i, u = 3 * k + b, (3 * k + b) % 2
                        if i >= 2:
                            pe.wait_ge(n("h_set"), ib + i - 1)
                        for jj in range(w // P):
                            last = t.matmul(psx[u][:, jj * P:(jj + 1) * P], xc[k % 2][:, c0 // P + jj, :], K["ident"][:],
                                            is_transpose=True, start=jj == 0, stop=jj == w // P - 1, skip_group_check=True)
                        if b == 2:
                            last.then_inc(n("x_turned"), 1)
                        for ps, his, los, low_part in ((psd, eh, el, "e_lo"), (psn, mh, ml, "m_lo")):
                            pe.wait_ge(n(low_part), kb + k + 1)
                            for j in range(NT):
                                t.matmul(ps[u][:, 0:w], his[k % 2][:, j, :], K["counts"][:, j, c0:c0 + w], start=j == 0, stop=False)
                                last = t.matmul(ps[u][:, 0:w], los[k % 2][:, j, :], K["counts"][:, j, c0:c0 + w], start=False, stop=j == NT - 1)
                        last.then_inc(n("bank_ready"), 1)
                        if b == 0 and k + 1 < KC:
                            spread_max(k + 1)


def three(t, ps, hi, lo, wh, wl, n, lhs):
    for k in range(n):
        t.matmul(ps, lhs(hi, k), wh(k), start=k == 0, stop=False)
        t.matmul(ps, lhs(hi, k), wl(k), start=False, stop=False)
        last = t.matmul(ps, lhs(lo, k), wh(k), start=False, stop=k == n - 1)
    return last


def turn_tile(t, ps, x, n, ident):
    for k in range(n):
        last = t.matmul(ps[:, k * P:(k + 1) * P], x[:, k * P:(k + 1) * P], ident, is_transpose=True,
                        start=k % 4 == 0, stop=k % 4 == 3 or k == n - 1, skip_group_check=True)
    return last


def mean_var(nc, eng, x, n, st, mv, S, i, stat, own):
    v = nc.vector
    for h in range(n):
        last = v.bn_stats(st[:, 6 * h:6 * h + 6], x[:, h * 512:(h + 1) * 512])
    last.then_inc(S(own), 1)
    eng.wait_ge(S(own), at(i + 1))
    carry(eng, S)
    v.bn_aggr(mv, st[:, 0:6 * n]).then_inc(S(stat), 1)


def rstd(nc, eng, K, mv, S, i, stat, log, done):
    eng.wait_ge(S(stat), at(i + 1))
    nc.scalar.activation(mv[:, 1:2], mv[:, 1:2], ACT.Ln, bias=K["ln_eps"][:]).then_inc(S(log), 1)
    eng.wait_ge(S(log), at(i + 1))
    nc.scalar.activation(mv[:, 1:2], mv[:, 1:2], ACT.Exp, scale=-0.5).then_inc(S(done), 1)


def pipeline(eng, lo, hi, last, body):
    def straight(s):
        body(s, lambda o: (s + o) % 2, lambda o: (s + o) // 2, lambda o: 0 <= s + o < NT)

    for s in range(-1, lo):
        straight(s)
    with eng.Fori(0, (hi - lo) // 2) as it:
        for k in range(2):
            body(lo + k + 2 * it, lambda o: (lo + k + o) % 2, lambda o: it + (lo + k + o) // 2, lambda o: True)
    for s in range(hi, last + 1):
        straight(s)


def feed_forward(nc, S, K, T, A, W, l):
    with ExitStack() as c:
        sb = lambda n, s, d=F32: c.enter_context(nc.sbuf_tensor(f"{n}_f{l}", s, d))
        w2h, w2l = sb("w2h", [P, K2, H], F32R), sb("w2l", [P, K2, H], F32R)
        hh, hl = ([sb(f"{n}{u}", [P, KC, P], F32R) for u in range(2)] for n in ("hh", "hl"))
        gg = [sb(f"gg{u}", [P, H2]) for u in range(2)]
        gr = sb("gr", [P, H2])
        gh, gl = ([sb(f"{n}{u}", [P, H2], F32R) for u in range(2)] for n in ("gh", "gl"))
        xn = [sb(f"xn{u}", [P, H]) for u in range(2)]
        old = [sb(f"old{u}", [P, H]) for u in range(2)]
        st1, st2 = sb("st1", [P, 12]), sb("st2", [P, 6])
        mv1, mv2 = ([sb(f"{n}{u}", [P, 2]) for u in range(2)] for n in ("mv1", "mv2"))
        psu = [c.enter_context(nc.psum_tensor(f"psu{u}_f{l}", [P, H2], F32)) for u in range(2)]
        psg = c.enter_context(nc.psum_tensor(f"psg_f{l}", [P, H2], F32))
        psx = [c.enter_context(nc.psum_tensor(f"psx{u}_f{l}", [P, H], F32)) for u in range(2)]
        w2 = rows(A[f"L0_gnn_mw2_{l}"], K2)
        load, high, low = split_chunks(nc, S, c, "w2", [
            (w2[:, 2 * k:2 * k + 2, :], w2h[:, 2 * k:2 * k + 2, :], w2l[:, 2 * k:2 * k + 2, :]) for k in range(KC)], KC * l)
        B = NT * l
        xin = T["x"][l].rearrange("(j p) d -> p j d", p=P)
        xout = T["x"][l + 1].rearrange("(j p) d -> p j d", p=P)
        BR = NT * max(l - 1, 0)
        steps = lambda eng, body: pipeline(eng, 2, NT - 2, NT + 1, body)
        with nc.Block() as block:
            @block.sync
            def _(sp):
                load(sp)

                def fetch(i, u):
                    if l:
                        sp.wait_ge(S("x_out"), at(B + i - 1))
                        sp.dma_start(old[u][:], xin[:, bass.ds(i, 1), :]).then_inc(S(f"old_in{u}"), 16)

                def store(i, u):
                    sp.wait_ge(S("x_out"), at(B + i + 1))
                    sp.dma_start(xout[:, bass.ds(i, 1), :], xn[u][:]).then_inc(S(f"x_stored{u}"), 16)

                fetch(0, 0)
                with sp.Fori(0, NT // 2 - 1) as it:
                    for u in range(2):
                        fetch(2 * it + u + 1, 1 - u)
                        store(2 * it + u, u)
                fetch(NT - 1, 1)
                store(NT - 2, 0)
                store(NT - 1, 1)
                for u in range(2):
                    sp.wait_ge(S(f"x_stored{u}"), dma_at((B + NT) // 2))

            @block.scalar
            def _(act):
                s = nc.scalar
                s.preload_act_table_set(EXP_AND_LOG)

                def split_h(i, u):
                    act.wait_ge(S("u_psum"), at(B + i - 1))
                    s.copy(hh[u][:], W["hT"][:, :, bass.ds(i * P, P)]).then_inc(S("h_hi"), 1)

                def norm1(i, u):
                    rstd(nc, act, K, mv1[u], S, B + i, "stat1", "log1", "rstd1")

                def relu_g(i, u):
                    act.wait_ge(S("g_turned"), at(B + i + 1))
                    act.wait_ge(S("g_lo"), at(B + i))
                    act.wait_ge(S("g_hi"), at(B + i))
                    for k in range(K2):
                        last = s.activation(gr[:, k * P:(k + 1) * P], psg[:, k * P:(k + 1) * P], ACT.Relu,
                                            bias=W["a1"][:, k:k + 1], scale=W["g1"][:, k:k + 1])
                    last.then_inc(S("g_relu"), 1)
                    act.wait_ge(S("g_relu"), at(B + i + 1))
                    act.wait_ge(S("x_psum"), at(B + i - 1))
                    s.copy(gh[u][:], gr[:]).then_inc(S("g_hi"), 1)

                def norm2(i, u):
                    if l:
                        rstd(nc, act, K, mv2[u], S, BR + i, "stat2", "log2", "rstd2")

                def body(s, par, half, has):
                    if has(-2):
                        norm2(s - 2, par(-2))
                    if has(0) and has(2):
                        split_h(s + 2, par(2))
                    if has(0):
                        relu_g(s, par(0))
                    if has(1):
                        norm1(s + 1, par(1))
                        if not has(0):
                            high(act)

                for u in range(2):
                    split_h(u, u)
                steps(act, body)

            @block.gpsimd
            def _(pool):
                g = nc.gpsimd

                def low_h(i, u):
                    pool.wait_ge(S("h_hi"), at(B + i + 1))
                    pool.wait_ge(S("u_psum"), at(B + i - 1))
                    g.tensor_tensor(hl[u][:], W["hT"][:, :, bass.ds(i * P, P)], r32(hh[u][:]), ALU.subtract).then_inc(S("h_lo"), 1)

                def low_g(i, u):
                    pool.wait_ge(S("g_hi"), at(B + i + 1))
                    pool.wait_ge(S("x_psum"), at(B + i - 1))
                    g.tensor_tensor(gl[u][:], gr[:], r32(gh[u][:]), ALU.subtract).then_inc(S("g_lo"), 1)

                low_h(0, 0)
                low_h(1, 1)
                low(pool, g)
                with pool.Fori(0, NT // 2 - 1) as it:
                    for u in range(2):
                        low_h(2 * it + u + 2, u)
                        low_g(2 * it + u, u)
                low_g(NT - 2, 0)
                low_g(NT - 1, 1)

            @block.vector
            def _(dve):
                v = nc.vector

                def first(i, u):
                    dve.wait_ge(S("u_psum"), at(B + i + 1))
                    dve.wait_ge(S("normed"), at(B + i))
                    dve.wait_ge(S("g_turned"), at(B + i - 1))
                    v.tensor_tensor(gg[u][:], psu[u][:], W["b1"][:], ALU.add).then_inc(S("u_added"), 1)
                    dve.wait_ge(S("u_added"), at(B + i + 1))
                    dve.wait_ge(S("stat1"), at(B + i))
                    mean_var(nc, dve, gg[u], 2, st1, mv1[u][:], S, B + i, "stat1", "parts1")
                    dve.wait_ge(S("rstd1"), at(B + i + 1))
                    v.tensor_scalar(gg[u][:], gg[u][:], mv1[u][:, 0:1], mv1[u][:, 1:2], ALU.subtract, ALU.mult).then_inc(S("normed"), 1)

                def second(i, u, half):
                    dve.wait_ge(S("x_psum"), at(B + i + 1))
                    dve.wait_ge(S("x_out"), at(B + i))
                    dve.wait_ge(S(f"x_stored{u}"), dma_at(B // 2 + half))
                    if l == 0:
                        v.tensor_tensor(xn[u][:], psx[u][:], W["b2"][:], ALU.add).then_inc(S("x_out"), 1)
                        return
                    q = BR + i
                    v.tensor_tensor(xn[u][:], psx[u][:], W["b2"][:], ALU.add).then_inc(S("x_added"), 1)
                    dve.wait_ge(S("x_added"), at(q + 1))
                    dve.wait_ge(S("stat2"), at(q))
                    mean_var(nc, dve, xn[u], 1, st2, mv2[u][:], S, q, "stat2", "parts2")
                    dve.wait_ge(S("rstd2"), at(q + 1))
                    v.tensor_scalar(xn[u][:], xn[u][:], mv2[u][:, 0:1], mv2[u][:, 1:2], ALU.subtract, ALU.mult).then_inc(S("x_normed"), 1)
                    dve.wait_ge(S("x_normed"), at(q + 1))
                    v.tensor_tensor(xn[u][:], xn[u][:], W["g2"][:], ALU.mult).then_inc(S("x_scaled"), 1)
                    dve.wait_ge(S("x_scaled"), at(q + 1))
                    v.tensor_tensor(xn[u][:], xn[u][:], W["a2"][:], ALU.add).then_inc(S("x_shifted"), 1)
                    dve.wait_ge(S("x_shifted"), at(q + 1))
                    dve.wait_ge(S(f"old_in{u}"), dma_at(BR // 2 + half + 1))
                    v.scalar_tensor_tensor(xn[u][:], xn[u][:], 0.0, old[u][:], ALU.max, ALU.add).then_inc(S("x_out"), 1)

                def body(s, par, half, has):
                    if has(-2):
                        second(s - 2, par(-2), half(-2))
                    if has(1):
                        first(s + 1, par(1))

                steps(dve, body)

            @block.tensor
            def _(pe):
                t = nc.tensor

                def up(i, u):
                    pe.wait_ge(S("h_lo"), at(B + i + 1))
                    pe.wait_ge(S("u_added"), at(B + i - 1))
                    for h in range(2):
                        last = three(t, psu[u][:, h * 512:(h + 1) * 512], hh[u], hl[u],
                                     lambda k: W["w1h"][:, k, h * 512:(h + 1) * 512],
                                     lambda k: W["w1l"][:, k, h * 512:(h + 1) * 512], KC, lambda a, k: a[:, k, :])
                    last.then_inc(S("u_psum"), 1)

                def turn_g(i, u):
                    pe.wait_ge(S("normed"), at(B + i + 1))
                    pe.wait_ge(S("g_relu"), at(B + i))
                    turn_tile(t, psg, gg[u], K2, K["ident"][:]).then_inc(S("g_turned"), 1)

                def down(i, u):
                    pe.wait_ge(S("g_lo"), at(B + i + 1))
                    pe.wait_ge(S("x_out"), at(B + i - 1))
                    three(t, psx[u][:], gh[u], gl[u], lambda k: w2h[:, k, :], lambda k: w2l[:, k, :], K2,
                          lambda a, k: a[:, k * P:(k + 1) * P]).then_inc(S("x_psum"), 1)

                def body(s, par, half, has):
                    if has(1):
                        up(s + 1, par(1))
                    if has(0):
                        turn_g(s, par(0))
                        if not has(-1):
                            pe.wait_ge(S("w2_lo"), KC * (l + 1))
                    if has(-1):
                        down(s - 1, par(-1))

                steps(pe, body)


def join_layers(nc, S, K, T, A, W):
    with ExitStack() as c:
        sb = lambda n, s, d=F32: c.enter_context(nc.sbuf_tensor(f"{n}_j", s, d))
        CC = 3 * KC
        cwh, cwl = sb("cwh", [P, CC, H], F32R), sb("cwl", [P, CC, H], F32R)
        abh, abl = sb("abh", [P, K2, H], F32R), sb("abl", [P, K2, H], F32R)
        cat = [sb(f"cat{u}", [P, 4, H]) for u in range(2)]
        ch, cl = ([sb(f"{n}{u}", [P, 3 * H], F32R) for u in range(2)] for n in ("ch", "cl"))
        nh, nl = sb("nh", [P, H], F32R), sb("nl", [P, H], F32R)
        yy, xt = sb("yy", [P, H]), sb("xt", [P, H])
        st, mv = sb("st", [P, 6]), sb("mv", [P, 2])
        pt, qt = sb("pt", [P, H]), sb("qt", [P, H])
        cb, b1 = sb("cb", [P, H]), sb("b1", [P, H])
        psc = c.enter_context(nc.psum_tensor("psc_j", [P, 3 * H], F32))
        psy = c.enter_context(nc.psum_tensor("psy_j", [P, H], F32))
        psn = c.enter_context(nc.psum_tensor("psn_j", [P, H], F32))
        psp = c.enter_context(nc.psum_tensor("psp_j", [P, H], F32))
        psq = c.enter_context(nc.psum_tensor("psq_j", [P, H], F32))
        cw, w1 = rows(A["L0_gnn_cw"], CC), rows(A["L1_gnn_W1"][0:H2, :], K2)
        load, high, low = split_chunks(nc, S, c, "join", [
            (cw[:, 2 * k:2 * k + 2, :], cwh[:, 2 * k:2 * k + 2, :], cwl[:, 2 * k:2 * k + 2, :]) for k in range(CC // 2)] + [
            (w1[:, 2 * k:2 * k + 2, :], abh[:, 2 * k:2 * k + 2, :], abl[:, 2 * k:2 * k + 2, :]) for k in range(KC)])
        CHUNKS = CC // 2 + KC
        tiles = lambda x: x.rearrange("(j p) d -> p j d", p=P)
        steps = lambda eng, body: pipeline(eng, 1, NT - 1, NT, body)
        with nc.Block() as block:
            @block.sync
            def _(sp):
                def bring(i, u):
                    sp.wait_ge(S("cat_turned"), at(i - 1))
                    sp.wait_ge(S("y_added"), at(i - 1))
                    for l in range(4):
                        sp.dma_start(cat[u][:, l, :], tiles(T["x"][l])[:, bass.ds(i, 1), :]).then_inc(S(f"cat_in{u}"), 16)

                S.give_credit(sp, CREDITED_2, CREDITED_DMA_2)
                for u in range(2):
                    bring(u, u)
                sp.dma_start(cb[:], A["L0_gnn_cb"].partition_broadcast(P)).then_inc(S("join_rows"), 16)
                sp.dma_start(b1[:], A["L1_gnn_b1"].partition_broadcast(P)).then_inc(S("join_rows"), 16)
                load(sp)
                with sp.Fori(1, NT // 2) as it:
                    for u in range(2):
                        bring(2 * it + u, u)

            @block.scalar
            def _(act):
                s = nc.scalar
                s.preload_act_table_set(EXP_AND_LOG)

                def cat_high(i, u):
                    act.wait_ge(S("cat_turned"), at(i + 1))
                    act.wait_ge(S("y_psum"), at(i - 1))
                    s.copy(ch[u][:], psc[:]).then_inc(S("cat_hi"), 1)

                def x_high(i):
                    act.wait_ge(S("n_turned"), at(i + 1))
                    act.wait_ge(S("pq_psum"), at(i))
                    s.copy(nh[:], psn[:]).then_inc(S("n_hi"), 1)

                def store(i):
                    act.wait_ge(S("pq_psum"), at(i + 1))
                    act.wait_ge(S("p_stored"), dma_at(i))
                    s.copy(pt[:], psp[:]).then_inc(S("p_out"), 1)
                    act.wait_ge(S("p_out"), at(i + 1))
                    act.dma_start(tiles(T["src_part"])[:, bass.ds(i, 1), :], pt[:]).then_inc(S("p_stored"), 16)
                    act.wait_ge(S("q_out"), at(i + 1))
                    act.dma_start(tiles(T["dst_part"])[:, bass.ds(i, 1), :], qt[:]).then_inc(S("q_stored"), 16)

                def body(s, par, half, has):
                    if has(1):
                        cat_high(s + 1, par(1))
                        if not has(0):
                            high(act)
                    if has(-1):
                        x_high(s - 1)
                    if has(0):
                        rstd(nc, act, K, mv, S, s, "y_stat", "y_log", "y_rstd")
                    if has(-1):
                        store(s - 1)

                steps(act, body)
                act.wait_ge(S("p_stored"), dma_at(NT))
                act.wait_ge(S("q_stored"), dma_at(NT))

            @block.vector
            def _(dve):
                v = nc.vector

                def cat_low(i, u):
                    dve.wait_ge(S("cat_hi"), at(i + 1))
                    v.tensor_tensor(cl[u][:], psc[:], r32(ch[u][:]), ALU.subtract).then_inc(S("cat_lo"), 1)

                def norm(i, u, half):
                    dve.wait_ge(S(f"cat_in{u}"), dma_at(4 * half + 4))
                    dve.wait_ge(S("y_psum"), at(i + 1))
                    dve.wait_ge(S("y_norm"), at(i))
                    v.tensor_tensor(yy[:], psy[:], cb[:], ALU.add).then_inc(S("y_biased"), 1)
                    dve.wait_ge(S("y_biased"), at(i + 1))
                    v.tensor_tensor(yy[:], yy[:], cat[u][:, 0, :], ALU.add).then_inc(S("y_added"), 1)
                    dve.wait_ge(S("y_added"), at(i + 1))
                    dve.wait_ge(S("y_stat"), at(i))
                    mean_var(nc, dve, yy, 1, st, mv[:], S, i, "y_stat", "y_parts")
                    dve.wait_ge(S("y_rstd"), at(i + 1))
                    dve.wait_ge(S("n_turned"), at(i))
                    dve.wait_ge(S("x_kept"), at(i))
                    v.tensor_scalar(xt[:], yy[:], mv[:, 0:1], mv[:, 1:2], ALU.subtract, ALU.mult).then_inc(S("y_norm"), 1)

                def x_low(i):
                    dve.wait_ge(S("n_hi"), at(i + 1))
                    v.tensor_tensor(nl[:], psn[:], r32(nh[:]), ALU.subtract).then_inc(S("n_lo"), 1)

                def dst_part(i):
                    dve.wait_ge(S("pq_psum"), at(i + 1))
                    dve.wait_ge(S("q_stored"), dma_at(i))
                    v.tensor_tensor(qt[:], psq[:], b1[:], ALU.add).then_inc(S("q_out"), 1)

                def body(s, par, half, has):
                    if has(1):
                        cat_low(s + 1, par(1))
                        if not has(0):
                            low(dve, v)
                    if has(-1):
                        x_low(s - 1)
                    if has(0):
                        norm(s, par(0), half(0))
                    if has(-1):
                        dst_part(s - 1)

                dve.wait_ge(S("join_rows"), 32)
                steps(dve, body)

            @block.gpsimd
            def _(pool):
                with pool.Fori(0, NT) as i:
                    pool.wait_ge(S("y_norm"), at(i + 1))
                    carry(pool, S)
                    nc.gpsimd.tensor_copy(W["X"][:, bass.ds(i, 1), :], xt[:]).then_inc(S("x_kept"), 1)

            @block.tensor
            def _(pe):
                t = nc.tensor

                def turn_cat(i, u, half):
                    pe.wait_ge(S(f"cat_in{u}"), dma_at(4 * half + 4))
                    pe.wait_ge(S("cat_lo"), at(i))
                    turn_tile(t, psc, cat[u][:, 1:4, :].rearrange("p l d -> p (l d)"), CC, K["ident"][:]).then_inc(S("cat_turned"), 1)

                def product(i, u):
                    pe.wait_ge(S("cat_lo"), at(i + 1))
                    pe.wait_ge(S("y_biased"), at(i))
                    three(t, psy[:], ch[u], cl[u], lambda k: cwh[:, k, :], lambda k: cwl[:, k, :], CC,
                          lambda a, k: a[:, k * P:(k + 1) * P]).then_inc(S("y_psum"), 1)

                def turn_x(i):
                    pe.wait_ge(S("y_norm"), at(i + 1))
                    pe.wait_ge(S("n_lo"), at(i))
                    turn_tile(t, psn, xt, KC, K["ident"][:]).then_inc(S("n_turned"), 1)

                def parts(i):
                    pe.wait_ge(S("n_lo"), at(i + 1))
                    pe.wait_ge(S("p_out"), at(i))
                    pe.wait_ge(S("q_out"), at(i))
                    three(t, psp[:], nh, nl, lambda k: abh[:, k, :], lambda k: abl[:, k, :], KC,
                          lambda a, k: a[:, k * P:(k + 1) * P])
                    three(t, psq[:], nh, nl, lambda k: abh[:, KC + k, :], lambda k: abl[:, KC + k, :], KC,
                          lambda a, k: a[:, k * P:(k + 1) * P]).then_inc(S("pq_psum"), 1)

                def body(s, par, half, has):
                    if has(1):
                        turn_cat(s + 1, par(1), half(1))
                    if has(-1):
                        turn_x(s - 1)
                    if has(0):
                        if not has(-1):
                            pe.wait_ge(S("join_lo"), CC // 2)
                        product(s, par(0))
                        if not has(-1):
                            pe.wait_ge(S("join_lo"), CHUNKS)
                    if has(-1):
                        parts(s - 1)

                steps(pe, body)


def mish_square(v, w):
    return v.scalar_tensor_tensor(w, w, 2.0, w, ALU.add, ALU.mult)


def edge_messages(nc, S, K, T, A, W):
    with ExitStack() as c:
        sb = lambda n, s, d=F32: c.enter_context(nc.sbuf_tensor(f"{n}_e", s, d))
        w2h, w2l = sb("w2h", [P, KC, H], F32R), sb("w2l", [P, KC, H], F32R)
        wc = sb("wc", [ED, H])
        wch2 = sb("wch2", [P, H], F32R)
        wcl = sb("wcl", [ED, H], F32R)
        at_rows = [sb(f"at_rows{u}", [P, 4, P]) for u in range(2)]
        attr = sb("attr", [P, 4 * P], F32R)
        G = [sb(f"G{u}", [P, 4, H]) for u in range(2)]
        GI = [sb(f"GI{u}", [P, 4, 2], I32) for u in range(2)]
        zw = [sb(f"zw{u}", [P, H2]) for u in range(2)]
        zh = [sb(f"zh{u}", [P, H2]) for u in range(2)]
        hh, hl = ([sb(f"{n}{u}", [P, KC, 512], F32R) for u in range(2)] for n in ("hh", "hl"))
        mw = [sb(f"mw{u}", [P, H2]) for u in range(2)]
        mx = [sb(f"mx{u}", [P, H2]) for u in range(2)]
        hot = [sb(f"hot{u}", [P, 4, P]) for u in range(2)]
        b2 = sb("b2", [P, H])
        psa = c.enter_context(nc.psum_tensor("psa_e", [P, 512], F32))
        psz = [c.enter_context(nc.psum_tensor(f"psz{u}_e", [P, H2], F32)) for u in range(2)]
        psm = c.enter_context(nc.psum_tensor("psm_e", [P, H2], F32))
        pss = c.enter_context(nc.psum_tensor("pss_e", [P, H], F32))
        w2 = rows(A["L1_gnn_W2"], KC)
        load, high, low = split_chunks(nc, S, c, "edge", [
            (w2[:, 2 * k:2 * k + 2, :], w2h[:, 2 * k:2 * k + 2, :], w2l[:, 2 * k:2 * k + 2, :]) for k in range(2)])
        table = T["table"].rearrange("(t p) f -> p t f", p=P)
        with nc.Block() as block:
            @block.sync
            def _(sp):
                sp.dma_start(wc[:], A["L1_gnn_W1"][H2:H2 + ED, :]).then_inc(S("wc_in"), 16)
                sp.dma_start(b2[:], A["L1_gnn_b2"].partition_broadcast(P)).then_inc(S("edge_b2_in"), 16)
                load(sp)
                with sp.Fori(0, QUADS // 2) as it:
                    for u in range(2):
                        q = 2 * it + u
                        sp.wait_ge(S("attr_turned"), at(q - 1))
                        sp.dma_start(at_rows[u][:, :, 0:ED], table[:, bass.ds(4 * q, 4), 0:ED]).then_inc(S(f"attr_in{u}"), 16)

            def both(eng, body):
                body(0, 0, 0, False, True, True)
                body(1, 1, 0, True, True, True)
                with eng.Fori(1, QUADS // 2 - 1) as it:
                    for u in range(2):
                        body(2 * it + u, u, it, True, True, True)
                body(QUADS - 2, 0, QUADS // 2 - 1, True, False, True)
                body(QUADS - 1, 1, QUADS // 2 - 1, True, False, False)

            @block.gpsimd
            def _(pool):
                g = nc.gpsimd

                def index(q, u):
                    pool.wait_ge(S("z_ready"), at(2 * q - 2))
                    carry(pool, S)
                    g.tensor_copy(GI[u][:], K["src_dst"][:, bass.ds(4 * q, 4), :]).then_inc(S("index_copied"), 1)
                    pool.wait_ge(S("index_copied"), at(q + 1))
                    carry(pool, S)
                    for k in range(4):
                        g.indirect_dma_start(out=G[u][:, k, :], out_offset=None, in_=T["src_part"],
                                             in_offset=bass.IndirectOffsetOnAxis(ap=GI[u][:, k, 0:1], axis=0)).then_inc(S(f"src_rows{u}"), 16)

                def add_dst(q, u, it):
                    pool.wait_ge(S(f"src_rows{u}"), 64 * it + 64)
                    carry(pool, S)
                    for k in range(4):
                        g.indirect_dma_start(out=G[u][:, k, :], out_offset=None, in_=T["dst_part"],
                                             in_offset=bass.IndirectOffsetOnAxis(ap=GI[u][:, k, 1:2], axis=0),
                                             compute_op=ALU.add).then_inc(S(f"dst_rows{u}"), 16)

                def low_h(q, u):
                    for f in range(2):
                        n = 2 * q + f
                        pool.wait_ge(S("z_hi"), at(n + 1))
                        pool.wait_ge(S("m_ready"), at(2 * q - 2))
                        g.tensor_tensor(hl[u][:, 2 * f:2 * f + 2, :], zh[f][:].rearrange("p (a b) -> p a b", a=2),
                                        r32(hh[u][:, 2 * f:2 * f + 2, :]), ALU.subtract).then_inc(S("z_lo"), 1)

                for u in range(2):
                    g.memset(at_rows[u][:, :, ED:P], 0.0).then_inc(S("attr_zero"), 1)
                index(0, 0)
                add_dst(0, 0, 0)
                index(1, 1)
                add_dst(1, 1, 0)
                with pool.Fori(0, QUADS // 2 - 1) as it:
                    for u in range(2):
                        q = 2 * it + u
                        index(q + 2, u)
                        low_h(q, u)
                        add_dst(q + 2, u, it + 1)
                low_h(QUADS - 2, 0)
                low_h(QUADS - 1, 1)

            @block.tensor
            def _(pe):
                t = nc.tensor

                def turn_attr(q, u, it):
                    pe.wait_ge(S(f"attr_in{u}"), dma_at(it + 1))
                    pe.wait_ge(S("attr_lo"), at(q))
                    for k in range(4):
                        last = t.matmul(psa[:, k * P:(k + 1) * P], at_rows[u][:, k, :], K["ident"][:], is_transpose=True,
                                        start=k == 0, stop=k == 3, skip_group_check=True)
                    last.then_inc(S("attr_turned"), 1)

                def layer1(q, u, it):
                    pe.wait_ge(S(f"dst_rows{u}"), 64 * it + 64)
                    for f in range(2):
                        pe.wait_ge(S("z_h"), at(2 * q + f - 1))
                        for a in range(2):
                            j = 2 * f + a
                            for k in range(4):
                                t.matmul(psz[f][:, a * 512 + k * P:a * 512 + (k + 1) * P], G[u][:, k, j * P:(j + 1) * P], K["ident"][:],
                                         is_transpose=True, start=k == 0, stop=False, skip_group_check=True)
                        if f == 0:
                            pe.wait_ge(S("attr_lo"), at(q + 1))
                        for a in range(2):
                            j = 2 * f + a
                            out = psz[f][:, a * 512:(a + 1) * 512]
                            t.matmul(out, wch2[:, j * P:(j + 1) * P], attr[:], start=False, stop=False, skip_group_check=True)
                            last = t.matmul(out, wcl[:, j * P:(j + 1) * P], attr[0:ED, :], start=False, stop=True, skip_group_check=True)
                        last.then_inc(S("z_ready"), 1)

                def layer2(q, u, f):
                    n = 2 * q + f
                    if f == 0:
                        pe.wait_ge(S("z_lo"), at(2 * q + 2))
                    pe.wait_ge(S("m_x"), at(n))
                    for a in range(2):
                        e0 = (2 * f + a) * P
                        last = three(t, psm[:, a * 512:(a + 1) * 512], hh[u], hl[u], lambda k: w2h[:, k, :], lambda k: w2l[:, k, :],
                                     KC, lambda x, k: x[:, k, e0:e0 + P])
                    last.then_inc(S("m_ready"), 1)

                def sum_up(q, u, f):
                    n = 2 * q + f
                    pe.wait_ge(S("m_msg"), at(n + 1))
                    pe.wait_ge(S("onehot"), at(q + 1))
                    pe.wait_ge(S("seg_added"), at(n))
                    t.matmul(pss[:], hot[u][:, 2 * f, :], mw[f][:, 0:512], start=True, stop=False)
                    t.matmul(pss[:], hot[u][:, 2 * f + 1, :], mw[f][:, 512:1024], start=False, stop=True).then_inc(S("seg_ready"), 1)

                pe.wait_ge(S("wc_split"), 3)
                pe.wait_ge(S("attr_zero"), 2)
                turn_attr(0, 0, 0)
                layer1(0, 0, 0)
                turn_attr(1, 1, 0)

                def body(q, u, it, back, attrs, more):
                    if more:
                        layer1(q + 1, 1 - u, it + u)
                    if back:
                        sum_up(q - 1, 1 - u, 0)
                    layer2(q, u, 0)
                    if back:
                        sum_up(q - 1, 1 - u, 1)
                    if attrs:
                        turn_attr(q + 2, u, it + 1)
                    layer2(q, u, 1)

                pe.wait_ge(S("edge_lo"), 2)
                both(pe, body)
                sum_up(QUADS - 1, 1, 0)
                sum_up(QUADS - 1, 1, 1)

            @block.scalar
            def _(act):
                s = nc.scalar
                s.preload_act_table_set(EXP_AND_LOG)

                def z_exp(q, f):
                    n = 2 * q + f
                    act.wait_ge(S("z_ready"), at(n + 1))
                    act.wait_ge(S("z_h"), at(n - 1))
                    s.activation(zw[f][:], psz[f][:], ACT.Exp).then_inc(S("z_exp"), 1)

                def z_r(q, f):
                    n = 2 * q + f
                    act.wait_ge(S("z_u"), at(n + 1))
                    s.activation(zw[f][:], zw[f][:], ACT.Ln, scale=0.5, bias=1.0).then_inc(S("z_ln"), 1)
                    act.wait_ge(S("z_ln"), at(n + 1))
                    s.activation(zw[f][:], zw[f][:], ACT.Exp, scale=-1.0).then_inc(S("z_r"), 1)

                def z_hi(q, u, f):
                    n = 2 * q + f
                    act.wait_ge(S("z_h"), at(n + 1))
                    act.wait_ge(S("m_ready"), at(2 * q - 2))
                    s.copy(hh[u][:, 2 * f:2 * f + 2, :], zh[f][:].rearrange("p (a b) -> p a b", a=2)).then_inc(S("z_hi"), 1)

                def m_exp(q, f):
                    n = 2 * q + f
                    act.wait_ge(S("m_x"), at(n + 1))
                    act.wait_ge(S("seg_ready"), at(n - 1))
                    s.activation(mw[f][:], mx[f][:], ACT.Exp).then_inc(S("m_exp"), 1)

                def m_r(q, f):
                    n = 2 * q + f
                    act.wait_ge(S("m_u"), at(n + 1))
                    s.activation(mw[f][:], mw[f][:], ACT.Ln, scale=0.5, bias=1.0).then_inc(S("m_ln"), 1)
                    act.wait_ge(S("m_ln"), at(n + 1))
                    s.activation(mw[f][:], mw[f][:], ACT.Exp, scale=-1.0).then_inc(S("m_r"), 1)

                def attr_high(q):
                    act.wait_ge(S("attr_turned"), at(q + 1))
                    act.wait_ge(S("z_ready"), at(2 * q))
                    s.copy(attr[0:ED, :], psa[0:ED, :]).then_inc(S("attr_hi"), 1)

                def hidden(q, u):
                    z_exp(q, 0)
                    z_exp(q, 1)
                    z_r(q, 0)
                    z_r(q, 1)
                    z_hi(q, u, 0)
                    z_hi(q, u, 1)

                act.wait_ge(S("wc_in"), 16)
                s.copy(wch2[0:ED, :], wc[:]).then_inc(S("wc_split"), 1)
                s.copy(wch2[ED:P, :], wc[:]).then_inc(S("wc_split"), 1)
                attr_high(0)
                attr_high(1)
                high(act)
                hidden(0, 0)

                def body(q, u, it, back, attrs, more):
                    if back:
                        m_exp(q - 1, 1)
                    if more:
                        z_exp(q + 1, 0)
                        z_exp(q + 1, 1)
                    if back:
                        m_r(q - 1, 1)
                    if more:
                        z_r(q + 1, 0)
                        z_r(q + 1, 1)
                        z_hi(q + 1, 1 - u, 0)
                        z_hi(q + 1, 1 - u, 1)
                    m_exp(q, 0)
                    if attrs:
                        attr_high(q + 2)
                    m_r(q, 0)

                both(act, body)
                m_exp(QUADS - 1, 1)
                m_r(QUADS - 1, 1)

            @block.vector
            def _(dve):
                v = nc.vector

                def z_u(q, f):
                    n = 2 * q + f
                    dve.wait_ge(S("z_exp"), at(n + 1))
                    v.tensor_scalar(zw[f][:], zw[f][:], CAP, None, ALU.min).then_inc(S("z_min"), 1)
                    dve.wait_ge(S("z_min"), at(n + 1))
                    mish_square(v, zw[f][:]).then_inc(S("z_u"), 1)

                def z_h(q, f):
                    n = 2 * q + f
                    dve.wait_ge(S("z_r"), at(n + 1))
                    dve.wait_ge(S("z_lo"), at(n - 1))
                    v.scalar_tensor_tensor(zh[f][:], zw[f][:], 1.0, psz[f][:], ALU.subtract, ALU.mult).then_inc(S("z_h"), 1)

                def m_u(q, f):
                    n = 2 * q + f
                    dve.wait_ge(S("m_exp"), at(n + 1))
                    v.tensor_scalar(mw[f][:], mw[f][:], CAP, None, ALU.min).then_inc(S("m_min"), 1)
                    dve.wait_ge(S("m_min"), at(n + 1))
                    mish_square(v, mw[f][:]).then_inc(S("m_u"), 1)

                def m_x(q, f):
                    n = 2 * q + f
                    dve.wait_ge(S("m_ready"), at(n + 1))
                    dve.wait_ge(S("m_msg"), at(n - 1))
                    v.tensor_tensor(mx[f][:].rearrange("p (a b) -> p a b", a=2), b2[:].unsqueeze(1).to_broadcast([P, 2, H]),
                                    psm[:].rearrange("p (a b) -> p a b", a=2), ALU.subtract).then_inc(S("m_x"), 1)

                def m_msg(q, f):
                    n = 2 * q + f
                    dve.wait_ge(S("m_r"), at(n + 1))
                    v.scalar_tensor_tensor(mw[f][:], mw[f][:], 1.0, mx[f][:], ALU.subtract, ALU.mult).then_inc(S("m_msg"), 1)

                def attr_low(q):
                    dve.wait_ge(S("attr_hi"), at(q + 1))
                    v.tensor_tensor(attr[ED:P, :], psa[0:ED, :], r32(attr[0:ED, :]), ALU.subtract).then_inc(S("attr_lo"), 1)

                def onehots(q, u):
                    dve.wait_ge(S("seg_ready"), at(2 * q - 2))
                    for k in range(4):
                        last = v.tensor_scalar(hot[u][:, k, :], K["iota"][:], K["meta"][:, bass.ds(4 * q + k, 1), 2], None, ALU.is_equal)
                    last.then_inc(S("onehot"), 1)

                def add_sums(q, f):
                    n = 2 * q + f
                    tile = dve.value_load(K["pair_tile"][0:1, bass.ds(n, 1)], min_val=0, max_val=NT - 1)
                    dve.wait_ge(S("seg_ready"), at(n + 1))
                    agg = W["agg"][:, bass.ds(tile, 1), :]
                    dve.wait_ge(S("seg_added"), at(n))
                    v.tensor_tensor(agg, agg, pss[:], ALU.add).then_inc(S("seg_added"), 1)

                def hidden(q):
                    z_u(q, 0)
                    z_u(q, 1)
                    z_h(q, 0)
                    z_h(q, 1)

                v.memset(W["agg"][:], 0.0).then_inc(S("agg_zero"), 1)
                dve.wait_ge(S("agg_zero"), 1)
                dve.wait_ge(S("wc_split"), 1)
                v.tensor_tensor(wcl[:], wc[:], r32(wch2[0:ED, :]), ALU.subtract).then_inc(S("wc_split"), 1)
                attr_low(0)
                attr_low(1)
                low(dve, v)
                hidden(0)
                dve.wait_ge(S("edge_b2_in"), 16)

                def body(q, u, it, back, attrs, more):
                    if back:
                        m_u(q - 1, 1)
                    if more:
                        z_u(q + 1, 0)
                        z_u(q + 1, 1)
                    if back:
                        m_msg(q - 1, 1)
                        add_sums(q - 1, 0)
                    if more:
                        z_h(q + 1, 0)
                        z_h(q + 1, 1)
                    m_x(q, 0)
                    if back:
                        add_sums(q - 1, 1)
                    onehots(q, u)
                    m_u(q, 0)
                    if attrs:
                        attr_low(q + 2)
                    m_msg(q, 0)
                    m_x(q, 1)

                both(dve, body)
                m_u(QUADS - 1, 1)
                m_msg(QUADS - 1, 1)
                add_sums(QUADS - 1, 0)
                add_sums(QUADS - 1, 1)


def update_nodes(nc, S, K, T, A, W, out):
    with ExitStack() as c:
        sb = lambda n, s, d=F32: c.enter_context(nc.sbuf_tensor(f"{n}_u", s, d))
        w3h, w3l = sb("w3h", [P, K2, H], F32R), sb("w3l", [P, K2, H], F32R)
        w4h, w4l = sb("w4h", [P, KC, H], F32R), sb("w4l", [P, KC, H], F32R)
        xa = [sb(f"xa{u}", [P, H2]) for u in range(2)]
        xb, xe = sb("xb", [P, NT, H]), sb("xe", [P, NT, H])
        oh, ol = ([sb(f"{n}{u}", [P, H2], F32R) for u in range(2)] for n in ("oh", "ol"))
        vx, vw, vo = sb("vx", [P, H]), sb("vw", [P, H]), sb("vo", [P, H])
        vh, vl = sb("vh", [P, H], F32R), sb("vl", [P, H], F32R)
        yy = sb("yy", [P, H])
        ft = [sb(f"ft{u}", [P, H]) for u in range(2)]
        st, mv = sb("st", [P, 6]), sb("mv", [P, 2])
        sf, mf = sb("sf", [P, 6]), sb("mf", [P, 2])
        b3, b4, ga, be = (sb(n, [P, H]) for n in ("b3", "b4", "ga", "be"))
        pso = c.enter_context(nc.psum_tensor("pso_u", [P, H2], F32))
        psv = [c.enter_context(nc.psum_tensor(f"psv{u}_u", [P, H], F32)) for u in range(2)]
        pst = c.enter_context(nc.psum_tensor("pst_u", [P, H], F32))
        psw = c.enter_context(nc.psum_tensor("psw_u", [P, H], F32))
        w3, w4 = rows(A["L1_gnn_W3"], K2), rows(A["L1_gnn_W4"], KC)
        load, high, low = split_chunks(nc, S, c, "upd", [
            (w3[:, 2 * k:2 * k + 2, :], w3h[:, 2 * k:2 * k + 2, :], w3l[:, 2 * k:2 * k + 2, :]) for k in range(KC)] + [
            (w4[:, 2 * k:2 * k + 2, :], w4h[:, 2 * k:2 * k + 2, :], w4l[:, 2 * k:2 * k + 2, :]) for k in range(2)])
        steps = lambda eng, body: pipeline(eng, 3, NT - 1, NT + 2, body)

        with nc.Block() as block:
            @block.sync
            def _(sp):
                for tile, name in ((b3, "b3"), (b4, "b4"), (ga, "gamma"), (be, "beta")):
                    sp.dma_start(tile[:], A[f"L1_gnn_{name}"].partition_broadcast(P)).then_inc(S("upd_rows"), 16)
                load(sp)
                whole = out[0:(NT - 1) * P, :].rearrange("(j p) d -> p j d", p=P)

                def store(i, u):
                    sp.wait_ge(S("f_out"), at(i + 1))
                    sp.dma_start(whole[:, bass.ds(i, 1), :], ft[u][:]).then_inc(S(f"f_stored{u}"), 16)

                with sp.Fori(0, NT // 2 - 1) as it:
                    for u in range(2):
                        store(2 * it + u, u)
                store(NT - 2, 0)
                sp.wait_ge(S("f_out"), at(NT))
                sp.dma_start(out[(NT - 1) * P:N, :], ft[1][0:LAST, :]).then_inc(S("f_stored1"), 16)
                for u in range(2):
                    sp.wait_ge(S(f"f_stored{u}"), dma_at(NT // 2))

            @block.gpsimd
            def _(pool):
                g = nc.gpsimd

                def keep(i, u):
                    pool.wait_ge(S("o_turned"), at(i - 1))
                    carry(pool, S)
                    g.tensor_copy(xa[u][:, 0:H], W["X"][:, bass.ds(i, 1), :]).then_inc(S("o_kept"), 1)
                    g.tensor_copy(xa[u][:, H:H2], W["agg"][:, bass.ds(i, 1), :]).then_inc(S("o_kept"), 1)

                for u in range(2):
                    keep(u, u)
                pool.wait_ge(S("upd_rows"), 64)
                g.tensor_tensor(xb[:], W["X"][:], b4[:].unsqueeze(1).to_broadcast([P, NT, H]), ALU.add).then_inc(S("bases"), 1)
                g.tensor_tensor(xe[:], W["X"][:], be[:].unsqueeze(1).to_broadcast([P, NT, H]), ALU.add).then_inc(S("bases"), 1)
                with pool.Fori(1, NT // 2) as it:
                    for u in range(2):
                        keep(2 * it + u, u)

            @block.tensor
            def _(pe):
                t = nc.tensor

                def turn_xa(i, u):
                    pe.wait_ge(S("o_kept"), at(2 * i + 2))
                    pe.wait_ge(S("o_lo"), at(i))
                    turn_tile(t, pso, xa[u], K2, K["ident"][:]).then_inc(S("o_turned"), 1)

                def product3(i, u):
                    pe.wait_ge(S("o_lo"), at(i + 1))
                    pe.wait_ge(S("v_x"), at(i - 1))
                    three(t, psv[u][:], oh[u], ol[u], lambda k: w3h[:, k, :], lambda k: w3l[:, k, :], K2,
                          lambda a, k: a[:, k * P:(k + 1) * P]).then_inc(S("v_psum"), 1)

                def turn_u(i):
                    pe.wait_ge(S("v_out"), at(i + 1))
                    pe.wait_ge(S("v_lo"), at(i))
                    turn_tile(t, pst, vo, KC, K["ident"][:]).then_inc(S("v_turned"), 1)

                def product4(i):
                    pe.wait_ge(S("v_lo"), at(i + 1))
                    pe.wait_ge(S("f_y"), at(i))
                    three(t, psw[:], vh, vl, lambda k: w4h[:, k, :], lambda k: w4l[:, k, :], KC,
                          lambda a, k: a[:, k * P:(k + 1) * P]).then_inc(S("w_psum"), 1)

                def body(s, par, half, has):
                    if has(1):
                        turn_xa(s + 1, par(1))
                    if has(-2):
                        turn_u(s - 2)
                    if has(0):
                        if not has(-1):
                            pe.wait_ge(S("upd_lo"), KC)
                        product3(s, par(0))
                        if not has(-1):
                            pe.wait_ge(S("upd_lo"), KC + 2)
                    if has(-2):
                        product4(s - 2)

                steps(pe, body)

            @block.scalar
            def _(act):
                s = nc.scalar
                s.preload_act_table_set(EXP_AND_LOG)

                def xa_high(i, u):
                    act.wait_ge(S("o_turned"), at(i + 1))
                    act.wait_ge(S("v_psum"), at(i - 1))
                    s.copy(oh[u][:, 0:H], pso[:, 0:H])
                    s.mul(oh[u][:, H:H2], pso[:, H:H2], -1.0).then_inc(S("o_hi"), 1)

                def mish_exp(i):
                    act.wait_ge(S("v_x"), at(i + 1))
                    act.wait_ge(S("v_out"), at(i))
                    s.activation(vw[:], vx[:], ACT.Exp).then_inc(S("v_exp"), 1)

                def mish_r(i):
                    act.wait_ge(S("v_u"), at(i + 1))
                    s.activation(vw[:], vw[:], ACT.Ln, scale=0.5, bias=1.0).then_inc(S("v_ln"), 1)
                    act.wait_ge(S("v_ln"), at(i + 1))
                    s.activation(vw[:], vw[:], ACT.Exp, scale=-1.0).then_inc(S("v_r"), 1)

                def u_high(i):
                    act.wait_ge(S("v_turned"), at(i + 1))
                    act.wait_ge(S("w_psum"), at(i))
                    s.copy(vh[:], pst[:]).then_inc(S("v_hi"), 1)

                def body(s, par, half, has):
                    if has(-1):
                        mish_exp(s - 1)
                    if has(-3):
                        rstd(nc, act, K, mv, S, s - 3, "f_stat1", "f_log1", "f_rstd1")
                    if has(1):
                        xa_high(s + 1, par(1))
                        if not has(0):
                            high(act)
                    if has(-1):
                        mish_r(s - 1)
                    if has(-2):
                        u_high(s - 2)
                    if has(-3):
                        rstd(nc, act, K, mf, S, s - 3, "f_stat2", "f_log2", "f_rstd2")

                steps(act, body)

            @block.vector
            def _(dve):
                v = nc.vector

                def xa_low(i, u):
                    dve.wait_ge(S("o_hi"), at(i + 1))
                    v.tensor_tensor(ol[u][:, 0:H], pso[:, 0:H], r32(oh[u][:, 0:H]), ALU.subtract)
                    v.scalar_tensor_tensor(ol[u][:, H:H2], pso[:, H:H2], -1.0, r32(oh[u][:, H:H2]), ALU.mult, ALU.subtract).then_inc(S("o_lo"), 1)

                def mish_x(i, u):
                    dve.wait_ge(S("v_psum"), at(i + 1))
                    dve.wait_ge(S("v_out"), at(i))
                    v.tensor_tensor(vx[:], psv[u][:], b3[:], ALU.add).then_inc(S("v_x"), 1)

                def mish_u(i):
                    dve.wait_ge(S("v_exp"), at(i + 1))
                    v.tensor_scalar(vw[:], vw[:], CAP, None, ALU.min).then_inc(S("v_min"), 1)
                    dve.wait_ge(S("v_min"), at(i + 1))
                    mish_square(v, vw[:]).then_inc(S("v_u"), 1)

                def mish_out(i):
                    dve.wait_ge(S("v_r"), at(i + 1))
                    dve.wait_ge(S("v_turned"), at(i))
                    v.scalar_tensor_tensor(vo[:], vw[:], 1.0, vx[:], ALU.subtract, ALU.mult).then_inc(S("v_out"), 1)

                def u_low(i):
                    dve.wait_ge(S("v_hi"), at(i + 1))
                    v.tensor_tensor(vl[:], pst[:], r32(vh[:]), ALU.subtract).then_inc(S("v_lo"), 1)

                def add_x(i):
                    dve.wait_ge(S("w_psum"), at(i + 1))
                    dve.wait_ge(S("f_sum"), at(i))
                    dve.wait_ge(S("f_out"), at(i))
                    v.tensor_tensor(yy[:].unsqueeze(1), xb[:, bass.ds(i, 1), :], psw[:].unsqueeze(1), ALU.subtract).then_inc(S("f_y"), 1)
                    dve.wait_ge(S("f_y"), at(i + 1))
                    mean_var(nc, dve, yy, 1, st, mv[:], S, i, "f_stat1", "f_parts1")

                def norm1(i):
                    dve.wait_ge(S("f_rstd1"), at(i + 1))
                    v.scalar_tensor_tensor(yy[:], yy[:], mv[:, 0:1], ga[:], ALU.subtract, ALU.mult).then_inc(S("f_scaled"), 1)
                    dve.wait_ge(S("f_scaled"), at(i + 1))
                    v.scalar_tensor_tensor(yy[:].unsqueeze(1), yy[:].unsqueeze(1), mv[:, 1:2], xe[:, bass.ds(i, 1), :], ALU.mult, ALU.add).then_inc(S("f_sum"), 1)
                    dve.wait_ge(S("f_sum"), at(i + 1))
                    mean_var(nc, dve, yy, 1, sf, mf[:], S, i, "f_stat2", "f_parts2")

                def norm2(i, u, half):
                    dve.wait_ge(S("f_rstd2"), at(i + 1))
                    dve.wait_ge(S(f"f_stored{u}"), dma_at(half))
                    v.tensor_scalar(ft[u][:], yy[:], mf[:, 0:1], mf[:, 1:2], ALU.subtract, ALU.mult).then_inc(S("f_out"), 1)

                def body(s, par, half, has):
                    if has(-1):
                        mish_x(s - 1, par(-1))
                    if has(-3):
                        add_x(s - 3)
                    if has(-1):
                        mish_u(s - 1)
                    if has(1):
                        xa_low(s + 1, par(1))
                        if not has(0):
                            low(dve, v)
                    if has(-3):
                        norm1(s - 3)
                    if has(-1):
                        mish_out(s - 1)
                    if has(-2):
                        u_low(s - 2)
                    if has(-3):
                        norm2(s - 3, par(-3), half(-3))

                dve.wait_ge(S("upd_rows"), 64)
                dve.wait_ge(S("bases"), 2)
                steps(dve, body)


def program(nc, A, out):
    ctx = ExitStack()
    with ctx:
        S = Sems(nc, 1)
        sb = lambda n, s, d=F32: ctx.enter_context(nc.sbuf_tensor(n, s, d))
        dram = lambda n, s: nc.dram_tensor(n, s, F32, kind="Internal").ap()
        K = {"ident": sb("ident", [P, P]), "ones": sb("ones", [P, P]), "zeros": sb("zeros", [P, H]),
             "iota": sb("iota", [P, P]), "iota_n": sb("iota_n", [P, NP], F16), "ln_eps": sb("ln_eps", [P, 1]),
             "pair_tile": sb("pair_tile", [P, PAIRS], I32), "meta": sb("meta", [P, TILES, 4]),
             "src_dst": sb("src_dst", [P, TILES, 2], I32)}
        T = {"table": dram("table", (ROWS, ROW)), "x": [dram(f"x{l}", (NP, H)) for l in range(4)],
             "src_part": dram("src_part", (NP, H)), "dst_part": dram("dst_part", (NP, H))}
        with ExitStack() as first:
            s0 = lambda n, s, d=F32: first.enter_context(nc.sbuf_tensor(n, s, d))
            K["counts"] = s0("counts", [P, NT, NP], F32R)
            sort_edges(nc, S, K, T, A)
            count_edges(nc, S, K, T)
            W = {"hT": s0("hT", [P, KC, NP]), "w1h": s0("w1h", [P, KC, H2], F32R), "w1l": s0("w1l", [P, KC, H2], F32R),
                 "b1": s0("b1", [P, H2]), "b2": s0("b2", [P, H]), "g1": s0("g1", [P, K2]), "a1": s0("a1", [P, K2]),
                 "g2": s0("g2", [P, H]), "a2": s0("a2", [P, H])}
            for l in range(3):
                aggregate(nc, S, K, T, A, W, l)
                feed_forward(nc, S, K, T, A, W, l)
        S.close()
        S = Sems(nc, 2)
        W = {"X": sb("X", [P, NT, H]), "agg": sb("agg", [P, NT, H])}
        join_layers(nc, S, K, T, A, W)
        edge_messages(nc, S, K, T, A, W)
        update_nodes(nc, S, K, T, A, W, out)


_OUT = (N, H)


def kernel(**inputs):
    import numpy as np
    import concourse.bacc as bacc
    from concourse.bass_utils import run_bass_kernel_spmd as run

    nc = bacc.Bacc("TRN2", target_bir_lowering=False, num_devices=1)
    arrays, A = {}, {}
    for name, value in inputs.items():
        a = np.ascontiguousarray(value)
        arrays[f"in_{name}"] = a
        A[name] = nc.dram_tensor(f"in_{name}", a.shape, mybir.dt.from_np(a.dtype), kind="ExternalInput").ap()
    out = nc.dram_tensor("out", _OUT, F32, kind="ExternalOutput").ap()
    program(nc, A, out)
    return run(nc, [arrays], core_ids=[0]).results[0]["out"]
```

```python
import concourse.bass as bass
from concourse import mybir
from contextlib import ExitStack

F32 = mybir.dt.float32
F32R = mybir.dt.float32r
BF16 = mybir.dt.bfloat16
F16 = mybir.dt.float16
I32 = mybir.dt.int32
ALU = mybir.AluOpType
ACT = mybir.ActivationFunctionType
AX = mybir.AxisListType

P = 128
N, H, E, ED = 1250, 512, 21250, 64
NT = (N + P - 1) // P
NP = NT * P
LAST = N - (NT - 1) * P
KC = H // P
H2 = 2 * H
K2 = H2 // P
EP, EJ = 125, E // 125
PAIRS = (E + NT * 255) // 256
QUADS = PAIRS // 2
TILES = 2 * PAIRS
ROWS = TILES * P
ROW = ED + 4
SC = 10
PARTS = (0, 2, 6, EJ // SC)
EPS = 1e-7
LN_EPS = 1e-5
TINY = 1e-35
EXP_AND_LOG = "natural_log_exp_and_others"
CAP = float(2 ** 24)
NB = [(0, 512), (512, 512), (1024, 256)]


def carry(eng, S):
    eng.sem_inc(S("carried"), 1)


def r32(ap):
    return ap.bitcast(F32)


CREDIT, DMA_CREDIT = 2, 32
CREDITED_1 = ("src_hot dst_apart dst_hot pair_counted even_added odd_staged odd_added h_hi h_lo u_psum u_added parts1 stat1 log1 rstd1 normed g_turned g_relu g_hi g_lo "
              "x_psum x_added parts2 stat2 log2 rstd2 x_normed x_scaled x_shifted x_out").split()
CREDITED_DMA_1 = "old_in0 old_in1 x_stored0 x_stored1".split()
CREDITED_2 = ("cat_turned cat_hi cat_lo y_psum y_biased y_added y_parts y_stat y_log y_rstd y_norm x_kept n_turned n_hi n_lo pq_psum p_out q_out "
              "index_copied attr_turned attr_hi attr_lo z_ready z_exp z_min z_u z_ln z_r z_h z_hi z_lo "
              "m_ready m_x m_exp m_min m_u m_ln m_r m_msg onehot seg_ready seg_added "
              "o_kept based bases o_turned o_hi o_lo v_psum v_x v_exp v_min v_u v_ln v_r v_out v_turned v_hi v_lo w_psum "
              "f_y f_parts1 f_stat1 f_log1 f_rstd1 f_scaled f_sum f_parts2 f_stat2 f_log2 f_rstd2 f_out").split()
CREDITED_DMA_2 = "cat_in0 cat_in1 p_stored q_stored attr_in0 attr_in1 f_stored0 f_stored1".split()


def at(n):
    return n + CREDIT


def dma_at(n):
    return 16 * n + DMA_CREDIT


class Sems:

    def __init__(self, nc, half):
        self.nc, self.half, self.made = nc, half, {}

    def __call__(self, name):
        if name not in self.made:
            self.made[name] = self.nc.alloc_semaphore(name=f"{name}.{self.half}")
        return self.made[name]

    def give_credit(self, eng, compute, dma):
        for name in compute:
            eng.sem_inc(self(name), CREDIT)
        for name in dma:
            eng.sem_inc(self(name), DMA_CREDIT)

    def close(self):
        self.nc.clear_and_free_semaphores(list(self.made.values()))
        self.nc.all_engine_barrier()


def sort_edges(nc, S, K, T, A):
    with ExitStack() as c:
        sb = lambda n, s, d=F32: c.enter_context(nc.sbuf_tensor(n, s, d))
        src_i, dst_i = sb("src_i", [EP, EJ], I32), sb("dst_i", [EP, EJ], I32)
        bkt_i = sb("bkt_i", [EP, EJ], I32)
        src_f, dst_f, bkt_f = sb("src_f", [EP, EJ]), sb("dst_f", [EP, EJ]), sb("bkt_f", [EP, EJ])
        oh, cum = sb("oh", [EP, NT, EJ]), sb("cum", [EP, NT, EJ])
        ones_e = sb("ones_e", [EP, EJ])
        pos, tmp = sb("pos", [EP, EJ]), sb("tmp", [EP, EJ])
        pos_i = sb("pos_i", [EP, EJ], I32)
        pay = sb("pay", [EP, EJ, ROW])
        payb = [sb(f"payb{u}", [EP, SC, ROW]) for u in range(2)]
        posb = [sb(f"posb{u}", [EP, SC], I32) for u in range(2)]
        dum = sb("dum", [P, ROW])
        below = sb("below", [EP, EP])
        tot, npair, incl, excl = (sb(n, [P, NT]) for n in ("tot", "npair", "incl", "excl"))
        tot_i = sb("tot_i", [P, NT], I32)
        base = sb("base", [EP, NT])
        qi, qd, qs = sb("qi", [P, PAIRS]), sb("qd", [P, PAIRS]), sb("qs", [P, PAIRS])
        pc = c.enter_context(nc.psum_tensor("pc", [P, 512], F32))
        table_rows = T["table"]
        BATCHES = EJ // SC
        with nc.Block() as block:
            @block.sync
            def _(sp):
                S.give_credit(sp, CREDITED_1, CREDITED_DMA_1)
                sp.dma_start(dst_i[:], A["dst"].rearrange("(p j) -> p j", p=EP)).then_inc(S("dst_in"), 16)
                sp.dma_start(src_i[:], A["src"].rearrange("(p j) -> p j", p=EP)).then_inc(S("src_in"), 16)
                sp.wait_ge(S("dummy_set"), 2)
                sp.dma_start(table_rows.rearrange("(p r) f -> p r f", p=P),
                             dum[:].unsqueeze(1).to_broadcast([P, ROWS // P, ROW])).then_inc(S("table_filled"), 16)
                attr = A["edge_attr_64"].rearrange("(p j) f -> p j f", p=EP)
                for k, (a, b) in enumerate(zip(PARTS, PARTS[1:])):
                    sp.dma_start(pay[:, a * SC:b * SC, 0:ED], attr[:, a * SC:b * SC, :]).then_inc(S(f"attr_in{k}"), 16)
                sp.wait_ge(S("zero_set"), 1)
                sp.wait_ge(S("table_filled"), 16)

            @block.gpsimd
            def _(pool):
                g = nc.gpsimd
                g.memset(K["ident"][:], 0.0).then_inc(S("ident_0"), 1)
                g.memset(K["zeros"][:], 0.0).then_inc(S("zero_set"), 1)
                g.memset(below[:], 1.0).then_inc(S("below_1"), 1)
                g.memset(K["ones"][:], 1.0).then_inc(S("const_ready"), 1)
                g.iota(K["iota"][:], [[1, P]], base=0, channel_multiplier=0,
                       allow_small_or_imprecise_dtypes=True).then_inc(S("const_ready"), 1)
                g.iota(K["iota_n"][:], [[1, NP]], base=0, channel_multiplier=0,
                       allow_small_or_imprecise_dtypes=True).then_inc(S("const_ready"), 1)
                g.iota(qi[:], [[1, PAIRS]], base=0, channel_multiplier=0,
                       allow_small_or_imprecise_dtypes=True).then_inc(S("const_ready"), 1)
                pool.wait_ge(S("below_1"), 1)
                g.affine_select(out=below[:], in_=below[:], compare_op=ALU.is_gt, fill=0.0, base=0,
                                pattern=[[1, EP]], channel_multiplier=-1).then_inc(S("const_ready"), 1)
                pool.wait_ge(S("ident_0"), 1)
                g.affine_select(out=K["ident"][:], in_=K["ident"][:], compare_op=ALU.not_equal, fill=1.0, base=0,
                                pattern=[[-1, P]], channel_multiplier=1).then_inc(S("const_ready"), 1)
                pool.wait_ge(S("table_filled"), 16)

                def scatter(n, u):
                    pool.wait_ge(S("batch_ready"), 2 * n + 2)
                    carry(pool, S)
                    for s in range(SC):
                        g.indirect_dma_start(out=table_rows, out_offset=bass.IndirectOffsetOnAxis(ap=posb[u][:, s:s + 1], axis=0),
                                             in_=payb[u][:, s, :], in_offset=None).then_inc(S(f"scattered{u}"), 16)

                with pool.Fori(0, BATCHES // 2) as it:
                    for u in range(2):
                        scatter(2 * it + u, u)
                scatter(BATCHES - 1, 0)
                pool.wait_ge(S("scattered0"), 16 * SC * (BATCHES // 2 + 1))
                pool.wait_ge(S("scattered1"), 16 * SC * (BATCHES // 2))

            @block.tensor
            def _(pe):
                pe.wait_ge(S("const_ready"), 6)
                pe.wait_ge(S("counted"), NT)
                counts = cum[:, :, EJ - 1]
                nc.tensor.matmul(pc[0:EP, 0:NT], below[:], counts, start=True, stop=True)
                nc.tensor.matmul(pc[:, 64:64 + NT], K["ones"][0:EP, :], counts, start=True, stop=True).then_inc(S("count_sums"), 1)

            @block.vector
            def _(dve):
                v = nc.vector
                done = [0]

                def step(ins):
                    done[0] += 1
                    ins.then_inc(S("sort_steps"), 1)
                    dve.wait_ge(S("sort_steps"), done[0])

                v.memset(dum[:], 0.0).then_inc(S("dummy_set"), 1)
                dve.wait_ge(S("dummy_set"), 1)
                v.memset(dum[:, ED + 2:ED + 3], -1.0).then_inc(S("dummy_set"), 1)
                step(v.memset(ones_e[:], 1.0))
                dve.wait_ge(S("dst_in"), 16)
                v.tensor_copy(dst_f[:], dst_i[:])
                step(v.tensor_single_scalar(bkt_i[:], dst_i[:], 7, ALU.arith_shift_right))
                step(v.tensor_copy(bkt_f[:], bkt_i[:]))
                for b in range(NT):
                    step(v.tensor_single_scalar(oh[:, b, :], bkt_f[:], float(b), ALU.is_equal))
                    v.tensor_tensor_scan(cum[:, b, :], ones_e[:], oh[:, b, :], 0.0, ALU.mult, ALU.add).then_inc(S("counted"), 1)
                dve.wait_ge(S("src_in"), 16)
                v.tensor_copy(src_f[:], src_i[:])
                dve.wait_ge(S("count_sums"), 1)
                step(v.tensor_copy(tot[:], pc[:, 64:64 + NT]))
                step(v.tensor_scalar(tot[:], tot[:], 255.0, None, ALU.add))
                step(v.tensor_copy(tot_i[:], tot[:]))
                step(v.tensor_single_scalar(tot_i[:], tot_i[:], 8, ALU.arith_shift_right))
                step(v.tensor_copy(npair[:], tot_i[:]))
                step(v.tensor_tensor_scan(incl[:], K["ones"][:, 0:NT], npair[:], 0.0, ALU.mult, ALU.add))
                step(v.tensor_tensor(excl[:], incl[:], npair[:], ALU.subtract))
                step(v.tensor_scalar(base[:], excl[0:EP, :], 256.0, -1.0, ALU.mult, ALU.add))
                step(v.tensor_tensor(base[:], base[:], pc[0:EP, 0:NT], ALU.add))
                step(v.memset(pos[:], 0.0))
                for b in range(NT):
                    step(v.scalar_tensor_tensor(tmp[:], cum[:, b, :], base[:, b:b + 1], oh[:, b, :], ALU.add, ALU.mult))
                    step(v.tensor_tensor(pos[:], pos[:], tmp[:], ALU.add))
                step(v.tensor_copy(pos_i[:], pos[:]))
                v.tensor_copy(pay[:, :, ED], src_f[:])
                v.tensor_copy(pay[:, :, ED + 1], dst_f[:])
                v.memset(pay[:, :, ED + 3], 0.0)
                step(v.scalar_tensor_tensor(pay[:, :, ED + 2], bkt_f[:], -float(P), dst_f[:], ALU.mult, ALU.add))

                def batch(n, u):
                    v.tensor_copy(payb[u][:], pay[:, bass.ds(n * SC, SC), :]).then_inc(S("batch_ready"), 1)
                    v.tensor_copy(posb[u][:], pos_i[:, bass.ds(n * SC, SC)]).then_inc(S("batch_ready"), 1)

                dve.wait_ge(S("attr_in0"), 16)
                for u in range(2):
                    batch(u, u)
                dve.wait_ge(S("const_ready"), 6)
                step(v.memset(qd[:], -1.0))
                for b in range(NT):
                    step(v.tensor_scalar(qs[:], qi[:], excl[:, b:b + 1], None, ALU.is_ge))
                    step(v.tensor_tensor(qd[:], qd[:], qs[:], ALU.add))
                step(v.tensor_copy(K["pair_tile"][:], qd[:]))
                v.memset(K["counts"][:].bitcast(F32), 0.0).then_inc(S("counts_zero"), 1)
                v.memset(K["ln_eps"][:], LN_EPS).then_inc(S("counts_zero"), 1)
                for k in (1, 2):
                    dve.wait_ge(S(f"attr_in{k}"), 16)
                    with dve.Fori(PARTS[k] // 2, PARTS[k + 1] // 2) as it:
                        dve.wait_ge(S("scattered0"), 16 * SC * it)
                        batch(2 * it, 0)
                        dve.wait_ge(S("scattered1"), 16 * SC * it)
                        batch(2 * it + 1, 1)
                dve.wait_ge(S("scattered0"), 16 * SC * (BATCHES // 2))
                batch(BATCHES - 1, 0)
                v.memset(K["odd_counts"][:], 0.0).then_inc(S("counts_zero"), 1)


def count_edges(nc, S, K, T, A):
    with ExitStack() as c:
        sb = lambda n, s, d=F32: c.enter_context(nc.sbuf_tensor(n, s, d))
        oh_src = [sb(f"oh_src{u}", [P, 2, NP], BF16) for u in range(4)]
        oh_dst = [sb(f"oh_dst{u}", [P, 2, P], BF16) for u in range(4)]
        apart = sb("apart", [P, 2, P])
        staged = [sb(f"staged{u}", [P, NT, P], BF16) for u in range(2)]
        ps = [c.enter_context(nc.psum_tensor(f"pcount{u}", [P, 3 * 512], F32)) for u in range(2)]
        meta, counts = K["meta"], K["counts"]
        PART = TILES // 4
        HALF = PAIRS // 2
        DVE_TILES = 7
        with nc.Block() as block:
            @block.sync
            def _(sp):
                for k in range(4):
                    sp.dma_start(meta[:, k * PART:(k + 1) * PART, :],
                                 T["table"].rearrange("(t p) f -> p t f", p=P)[:, k * PART:(k + 1) * PART, ED:ROW]).then_inc(S(f"meta_in{k}"), 16)
                sp.dma_start(T["x"][0][0:N, :], A["x"]).then_inc(S("x_padded"), 16)
                sp.dma_start(T["x"][0][N:NP, :], K["zeros"][0:NP - N, :]).then_inc(S("x_padded"), 16)
                sp.wait_ge(S("x_padded"), 32)

            def pair(dve, q, u, reused=True):
                if reused:
                    dve.wait_ge(S("pair_counted"), at(q - 3))
                for k in range(2):
                    last = nc.vector.tensor_scalar(oh_src[u][:, k, :], K["iota_n"][:], meta[:, bass.ds(2 * q + k, 1), 0], None, ALU.is_equal)
                last.then_inc(S("src_hot"), 1)

            @block.scalar
            def _(act):
                s = nc.scalar
                s.preload_act_table_set(EXP_AND_LOG)
                for k in range(4):
                    act.wait_ge(S(f"meta_in{k}"), 16)

                def dst_hot(q, u, reused=True):
                    if reused:
                        act.wait_ge(S("pair_counted"), at(q - 3))
                    act.wait_ge(S("dst_hot"), at(q))
                    for k in range(2):
                        last = s.activation(apart[:, k, :], K["iota"][:], ACT.Abs, scale=-1.0, bias=meta[:, bass.ds(2 * q + k, 1), 2])
                    last.then_inc(S("dst_apart"), 1)
                    act.wait_ge(S("dst_apart"), at(q + 1))
                    s.activation(oh_dst[u][:], apart[:], ACT.Relu, scale=-1.0, bias=1.0).then_inc(S("dst_hot"), 1)

                def stage(m, v):
                    act.wait_ge(S("pair_counted"), at(2 * m + 2))
                    act.wait_ge(S("odd_added"), at(m - 1))
                    s.copy(staged[v][:], ps[1][:, 0:NP].rearrange("p (j d) -> p j d", j=NT)).then_inc(S("odd_staged"), 1)

                for q in range(4):
                    dst_hot(q, q, reused=False)
                stage(0, 0)
                with act.Fori(0, HALF // 2 - 1) as it:
                    for v in range(2):
                        m = 2 * it + 1 + v
                        for k in range(2):
                            dst_hot(2 * m + 2 + k, 2 * v + k)
                        stage(m, 1 - v)
                stage(HALF - 1, 1)

            @block.gpsimd
            def _(pool):
                g = nc.gpsimd

                def add_odd(m, v):
                    tile = pool.value_load(K["pair_tile"][0:1, bass.ds(2 * m + 1, 1)], min_val=0, max_val=NT - 1)
                    dst = K["odd_counts"][:, :, bass.ds(tile * P, P)]
                    pool.wait_ge(S("odd_staged"), at(m + 1))
                    pool.wait_ge(S("odd_added"), at(m))
                    carry(pool, S)
                    g.tensor_tensor(dst, dst, staged[v][:], ALU.add).then_inc(S("odd_added"), 1)

                with pool.Fori(0, HALF // 2) as it:
                    for v in range(2):
                        add_odd(2 * it + v, v)
                pool.wait_ge(S("even_added"), at(HALF))
                pool.wait_ge(S("odd_added"), at(HALF))
                g.tensor_tensor(counts[:, DVE_TILES:NT, :], r32(counts[:, DVE_TILES:NT, :]), K["odd_counts"][:, DVE_TILES:NT, :],
                                ALU.add).then_inc(S("counts_done"), 1)

            @block.vector
            def _(dve):
                for k in range(4):
                    dve.wait_ge(S(f"meta_in{k}"), 16)
                nc.vector.tensor_copy(K["src_dst"][:], meta[:, :, 0:2]).then_inc(S("index_ready"), 1)

                def add_even(m):
                    tile = dve.value_load(K["pair_tile"][0:1, bass.ds(2 * m, 1)], min_val=0, max_val=NT - 1)
                    dst = counts[:, :, bass.ds(tile * P, P)]
                    dve.wait_ge(S("pair_counted"), at(2 * m + 1))
                    dve.wait_ge(S("even_added"), at(m))
                    nc.vector.tensor_tensor(dst, r32(dst), ps[0][:, 0:NP].rearrange("p (j d) -> p j d", j=NT), ALU.add).then_inc(S("even_added"), 1)

                for q in range(4):
                    pair(dve, q, q, reused=False)
                add_even(0)
                with dve.Fori(0, HALF // 2 - 1) as it:
                    for v in range(2):
                        m = 2 * it + 1 + v
                        for k in range(2):
                            pair(dve, 2 * m + 2 + k, 2 * v + k)
                        add_even(m)
                add_even(HALF - 1)
                dve.wait_ge(S("even_added"), at(HALF))
                dve.wait_ge(S("odd_added"), at(HALF))
                nc.vector.tensor_tensor(counts[:, 0:DVE_TILES, :], r32(counts[:, 0:DVE_TILES, :]), K["odd_counts"][:, 0:DVE_TILES, :],
                                        ALU.add).then_inc(S("counts_done"), 1)

            @block.tensor
            def _(pe):
                with pe.Fori(0, HALF // 2) as it:
                    for w in range(4):
                        q, m, u = 4 * it + w, 2 * it + w // 2, w % 2
                        for name in ("src_hot", "dst_hot"):
                            pe.wait_ge(S(name), at(q + 1))
                        pe.wait_ge(S(("even_added", "odd_staged")[u]), at(m))
                        for k in range(2):
                            for j in range(NT):
                                last = nc.tensor.matmul(ps[u][:, j * P:(j + 1) * P], oh_src[w][:, k, j * P:(j + 1) * P],
                                                        oh_dst[w][:, k, :], start=k == 0 and j % 4 == 0,
                                                        stop=k == 1 and (j % 4 == 3 or j == NT - 1), skip_group_check=True)
                        last.then_inc(S("pair_counted"), 1)


def split_chunks(nc, S, c, tag, jobs, before=0, stages=2):
    st = [c.enter_context(nc.sbuf_tensor(f"{tag}_stage{u}_{before}", [P, 1024], F32)) for u in range(stages)]

    def view(k):
        n = jobs[k][0].shape[1]
        return st[k % stages][:].rearrange("p (n m) -> p n m", n=n)

    def load(eng, ks=None):
        for k in (range(len(jobs)) if ks is None else ks):
            if k >= stages:
                eng.wait_ge(S(f"{tag}_lo"), before + k - stages + 1)
            eng.dma_start(view(k), jobs[k][0]).then_inc(S(f"{tag}_in{k % stages}"), 16)

    def high(eng, ks=None):
        for k in (range(len(jobs)) if ks is None else ks):
            src, hi, lo = jobs[k]
            eng.wait_ge(S(f"{tag}_in{k % stages}"), 16 * (before // stages + k // stages + 1))
            nc.scalar.copy(hi, view(k)).then_inc(S(f"{tag}_hi"), 1)

    def low(eng, alu, ks=None):
        for k in (range(len(jobs)) if ks is None else ks):
            src, hi, lo = jobs[k]
            eng.wait_ge(S(f"{tag}_hi"), before + k + 1)
            alu.tensor_tensor(lo, view(k), r32(hi), ALU.subtract).then_inc(S(f"{tag}_lo"), 1)

    return load, high, low, view


def split_alone(nc, S, c, tag, jobs):
    load, high, low, view = split_chunks(nc, S, c, tag, jobs)

    def alone(pool, ks):
        for k in ks:
            src, hi, lo = jobs[k]
            pool.wait_ge(S(f"{tag}_in{k % 2}"), 16 * (k // 2 + 1))
            nc.gpsimd.tensor_copy(hi, view(k)).then_inc(S(f"{tag}_hi"), 1)
            low(pool, nc.gpsimd, [k])

    return load, alone


def rows(ap, n):
    return ap.rearrange("(n p) m -> p n m", p=P)


def aggregate(nc, S, K, T, A, W, l):
    with ExitStack() as c:
        sb = lambda n, s, d=F32: c.enter_context(nc.sbuf_tensor(f"{n}_{l}", s, d))
        xc = [sb(f"xc{u}", [P, NT, P]) for u in range(2)]
        m, e, em = (sb(n, [P, NT, P]) for n in ("m", "e", "em"))
        eh, el, mh, ml = ([sb(f"{n}{u}", [P, NT, P], F32R) for u in range(2)] for n in ("eh", "el", "mh", "ml"))
        pmax, top, dg = sb("pmax", [P, P]), sb("top", [P, 1]), sb("dg", [P, P])
        rden = sb("rden", [P, 512])
        tcol = sb("tcol", [P, 1])
        psd, psn, psx = ([c.enter_context(nc.psum_tensor(f"{n}{u}_{l}", [P, 512], F32)) for u in range(2)] for n in ("psd", "psn", "psx"))
        psk = c.enter_context(nc.psum_tensor(f"psk_{l}", [P, P], F32))
        psb = c.enter_context(nc.psum_tensor(f"psb_{l}", [P, P], F32))
        w1, w2 = A[f"L0_gnn_mw1_{l}"], rows(A[f"L0_gnn_mw2_{l}"], K2)
        load, high, low, _ = split_chunks(nc, S, c, "w", [
            (rows(w1, KC)[:, k:k + 1, :], W["w1h"][:, k:k + 1, :], W["w1l"][:, k:k + 1, :]) for k in range(KC)] + [
            (w2[:, 2 * k:2 * k + 2, :], W["w2h"][:, 2 * k:2 * k + 2, :], W["w2l"][:, 2 * k:2 * k + 2, :]) for k in range(2)], (KC + 2) * l)
        CHUNKS = (range(2), range(2, 4), range(4, 5), range(5, 6))
        n, kb, ib = S, KC * l, 3 * KC * l
        row = lambda name: A[name].partition_broadcast(P)
        with nc.Block() as block:
            @block.sync
            def _(sp):
                sp.dma_start(tcol[:], row(f"L0_gnn_t{l}")).then_inc(n("t_in"), 16)
                for k in range(KC):
                    if k >= 2:
                        sp.wait_ge(n("x_turned"), kb + k - 1)
                        sp.wait_ge(n("m_set"), kb + k - 1)
                    sp.dma_start(xc[k % 2][:], T["x"][l].rearrange("(j p) d -> p j d", p=P)[:, :, k * P:(k + 1) * P]).then_inc(n(f"xc_in{k % 2}"), 16)
                    load(sp, [range(0), range(2), range(2, 4), range(4, 6)][k])

            def prepare(dve, k):
                v = nc.vector
                dve.wait_ge(n(f"xc_in{k % 2}"), 16 * (2 * l + k // 2 + 1))
                if k:
                    dve.wait_ge(n("em_set"), kb + k)
                    dve.wait_ge(n("e_hi"), kb + k)
                    dve.wait_ge(n("e_lo"), kb + k)
                v.tensor_scalar(m[:], xc[k % 2][:], 0.0, EPS, ALU.max, ALU.add).then_inc(n("m_set"), 1)
                dve.wait_ge(n("m_set"), kb + k + 1)
                v.tensor_scalar(e[:], m[:], tcol[:], None, ALU.mult).then_inc(n("z_set"), 1)
                dve.wait_ge(n("z_set"), kb + k + 1)
                v.tensor_reduce(pmax[:], e[:].rearrange("p j c -> p c j"), AX.X, ALU.max).then_inc(n("pmax_set"), 1)
                dve.wait_ge(n("max_turned"), kb + k + 1)
                v.tensor_reduce(top[:], psk[:], AX.X, ALU.max).then_inc(n("top_set"), 1)
                dve.wait_ge(n("top_set"), kb + k + 1)
                v.tensor_scalar(dg[:], K["ident"][:], top[:], None, ALU.mult).then_inc(n("dg_set"), 1)
                dve.wait_ge(n("max_spread"), kb + k + 1)
                v.tensor_tensor(e[:], e[:], psb[:].unsqueeze(1).to_broadcast([P, NT, P]), ALU.subtract).then_inc(n("z_low"), 1)

            def weigh(dve, k):
                v = nc.vector
                dve.wait_ge(n("e_set"), kb + k + 1)
                if k:
                    dve.wait_ge(n("m_lo"), kb + k)
                v.tensor_tensor(em[:], e[:], m[:], ALU.mult).then_inc(n("em_set"), 1)

            def finish(dve, k, b):
                v = nc.vector
                c0, w = NB[b]
                i, u = 3 * k + b, (3 * k + b) % 2
                dve.wait_ge(n("bank_ready"), ib + i + 1)
                if i:
                    dve.wait_ge(n("h_set"), ib + i)
                v.tensor_scalar(rden[:, 0:w], psd[u][:, 0:w], TINY, None, ALU.add).then_inc(n("den_set"), 1)
                dve.wait_ge(n("den_set"), ib + i + 1)
                v.reciprocal(rden[:, 0:w], rden[:, 0:w]).then_inc(n("rden_set"), 1)
                dve.wait_ge(n("rden_set"), ib + i + 1)
                h = W["hT"][:, k, c0:c0 + w]
                v.tensor_tensor(h, rden[:, 0:w], psn[u][:, 0:w], ALU.mult).then_inc(n("agg_set"), 1)
                dve.wait_ge(n("agg_set"), ib + i + 1)
                v.tensor_tensor(h, h, psx[u][:, 0:w], ALU.add).then_inc(n("h_set"), 1)

            @block.vector
            def _(dve):
                dve.wait_ge(n("t_in"), 16 * (l + 1))
                prepare(dve, 0)
                weigh(dve, 0)
                for k in range(KC):
                    if k + 1 < KC:
                        prepare(dve, k + 1)
                    finish(dve, k, 0)
                    if k + 1 < KC:
                        weigh(dve, k + 1)
                    finish(dve, k, 1)
                    finish(dve, k, 2)

            @block.scalar
            def _(act):
                s = nc.scalar
                s.preload_act_table_set(EXP_AND_LOG)
                for k in range(KC):
                    act.wait_ge(n("z_low"), kb + k + 1)
                    s.activation(e[:], e[:], ACT.Exp).then_inc(n("e_set"), 1)
                    if k >= 2:
                        act.wait_ge(n("bank_ready"), ib + 3 * (k - 1))
                    act.wait_ge(n("e_set"), kb + k + 1)
                    s.copy(eh[k % 2][:], e[:]).then_inc(n("e_hi"), 1)
                    act.wait_ge(n("em_set"), kb + k + 1)
                    s.copy(mh[k % 2][:], em[:]).then_inc(n("m_hi"), 1)
                    high(act, CHUNKS[k])

            @block.gpsimd
            def _(pool):
                g = nc.gpsimd
                for k in range(KC):
                    pool.wait_ge(n("e_hi"), kb + k + 1)
                    g.tensor_tensor(el[k % 2][:], e[:], r32(eh[k % 2][:]), ALU.subtract).then_inc(n("e_lo"), 1)
                    pool.wait_ge(n("m_hi"), kb + k + 1)
                    g.tensor_tensor(ml[k % 2][:], em[:], r32(mh[k % 2][:]), ALU.subtract).then_inc(n("m_lo"), 1)
                    low(pool, g, CHUNKS[k])

            @block.tensor
            def _(pe):
                t = nc.tensor

                def spread_max(k):
                    pe.wait_ge(n("pmax_set"), kb + k + 1)
                    if k:
                        pe.wait_ge(n("top_set"), kb + k)
                    t.transpose(psk[:], pmax[:], K["ident"][:]).then_inc(n("max_turned"), 1)
                    pe.wait_ge(n("dg_set"), kb + k + 1)
                    if k:
                        pe.wait_ge(n("z_low"), kb + k)
                    t.matmul(psb[:], K["ones"][:], dg[:], start=True, stop=True).then_inc(n("max_spread"), 1)

                spread_max(0)
                for k in range(KC):
                    for b, (c0, w) in enumerate(NB):
                        i, u = 3 * k + b, (3 * k + b) % 2
                        if i >= 2:
                            pe.wait_ge(n("h_set"), ib + i - 1)
                        for jj in range(w // P):
                            last = t.matmul(psx[u][:, jj * P:(jj + 1) * P], xc[k % 2][:, c0 // P + jj, :], K["ident"][:],
                                            is_transpose=True, start=jj == 0, stop=jj == w // P - 1, skip_group_check=True)
                        if b == 2:
                            last.then_inc(n("x_turned"), 1)
                        for ps, his, los, high_part, low_part in ((psd, eh, el, "e_hi", "e_lo"), (psn, mh, ml, "m_hi", "m_lo")):
                            pe.wait_ge(n(high_part), kb + k + 1)
                            for j in range(NT):
                                t.matmul(ps[u][:, 0:w], his[k % 2][:, j, :], K["counts"][:, j, c0:c0 + w], start=j == 0, stop=False)
                            pe.wait_ge(n(low_part), kb + k + 1)
                            for j in range(NT):
                                last = t.matmul(ps[u][:, 0:w], los[k % 2][:, j, :], K["counts"][:, j, c0:c0 + w], start=False, stop=j == NT - 1)
                        last.then_inc(n("bank_ready"), 1)
                        if b == 0 and k + 1 < KC:
                            spread_max(k + 1)


def three(t, ps, hi, lo, wh, wl, n, lhs):
    for k in range(n):
        t.matmul(ps, lhs(hi, k), wh(k), start=k == 0, stop=False)
        t.matmul(ps, lhs(hi, k), wl(k), start=False, stop=False)
        last = t.matmul(ps, lhs(lo, k), wh(k), start=False, stop=k == n - 1)
    return last


def turn_tile(t, ps, x, n, ident):
    for k in range(n):
        last = t.matmul(ps[:, k * P:(k + 1) * P], x[:, k * P:(k + 1) * P], ident, is_transpose=True,
                        start=k % 4 == 0, stop=k % 4 == 3 or k == n - 1, skip_group_check=True)
    return last


def mean_var(nc, eng, x, n, st, mv, S, i, stat, own):
    v = nc.vector
    for h in range(n):
        last = v.bn_stats(st[:, 6 * h:6 * h + 6], x[:, h * 512:(h + 1) * 512])
    last.then_inc(S(own), 1)
    eng.wait_ge(S(own), at(i + 1))
    carry(eng, S)
    v.bn_aggr(mv, st[:, 0:6 * n]).then_inc(S(stat), 1)


def rstd(nc, eng, K, mv, S, i, stat, log, done):
    eng.wait_ge(S(stat), at(i + 1))
    nc.scalar.activation(mv[:, 1:2], mv[:, 1:2], ACT.Ln, bias=K["ln_eps"][:]).then_inc(S(log), 1)
    eng.wait_ge(S(log), at(i + 1))
    nc.scalar.activation(mv[:, 1:2], mv[:, 1:2], ACT.Exp, scale=-0.5).then_inc(S(done), 1)


def pipeline(eng, lo, hi, last, body):
    def straight(s):
        body(s, lambda o: (s + o) % 2, lambda o: (s + o) // 2, lambda o: 0 <= s + o < NT)

    for s in range(-1, lo):
        straight(s)
    with eng.Fori(0, (hi - lo) // 2) as it:
        for k in range(2):
            body(lo + k + 2 * it, lambda o: (lo + k + o) % 2, lambda o: it + (lo + k + o) // 2, lambda o: True)
    for s in range(hi, last + 1):
        straight(s)


def feed_forward(nc, S, K, T, A, W, l):
    with ExitStack() as c:
        sb = lambda n, s, d=F32: c.enter_context(nc.sbuf_tensor(f"{n}_f{l}", s, d))
        b1, b2, g1, a1 = (sb(n, [P, w]) for n, w in (("b1", H2), ("b2", H), ("g1", K2), ("a1", K2)))
        g2, a2 = sb("g2", [P, H]), sb("a2", [P, H])
        hh, hl = ([sb(f"{n}{u}", [P, KC, P], F32R) for u in range(2)] for n in ("hh", "hl"))
        gg = [sb(f"gg{u}", [P, H2]) for u in range(2)]
        gr = sb("gr", [P, H2])
        gh, gl = ([sb(f"{n}{u}", [P, H2], F32R) for u in range(2)] for n in ("gh", "gl"))
        xn = [sb(f"xn{u}", [P, H]) for u in range(2)]
        old = [sb(f"old{u}", [P, H]) for u in range(2)]
        st1, st2 = sb("st1", [P, 12]), sb("st2", [P, 6])
        mv1, mv2 = ([sb(f"{n}{u}", [P, 2]) for u in range(2)] for n in ("mv1", "mv2"))
        psu = [c.enter_context(nc.psum_tensor(f"psu{u}_f{l}", [P, H2], F32)) for u in range(2)]
        psg = c.enter_context(nc.psum_tensor(f"psg_f{l}", [P, H2], F32))
        psx = [c.enter_context(nc.psum_tensor(f"psx{u}_f{l}", [P, H], F32)) for u in range(2)]
        w2h, w2l = sb("w2h", [P, KC, H], F32R), sb("w2l", [P, KC, H], F32R)
        w2 = rows(A[f"L0_gnn_mw2_{l}"], K2)
        load, high, low, _ = split_chunks(nc, S, c, "w2", [
            (w2[:, KC + 2 * k:KC + 2 * k + 2, :], w2h[:, 2 * k:2 * k + 2, :], w2l[:, 2 * k:2 * k + 2, :]) for k in range(2)], 2 * l)
        half2 = lambda first, second: lambda k: first[:, k, :] if k < KC else second[:, k - KC, :]
        row = lambda name: A[name].partition_broadcast(P)
        ROWS_IN = (64, 160, 256)[l]
        B = NT * l
        xin = T["x"][l].rearrange("(j p) d -> p j d", p=P)
        xout = T["x"][l + 1].rearrange("(j p) d -> p j d", p=P)
        BR = NT * max(l - 1, 0)
        steps = lambda eng, body: pipeline(eng, 2, NT - 2, NT + 1, body)
        with nc.Block() as block:
            @block.sync
            def _(sp):
                load(sp)
                sp.dma_start(b1[:], row(f"L0_gnn_mb1_{l}")).then_inc(S("rows_in"), 16)
                sp.dma_start(b2[:], row(f"L0_gnn_mb2_{l}")).then_inc(S("rows_in"), 16)
                sp.dma_start(g1[:], A[f"L0_gnn_mlg_{l}"].rearrange("(k p) -> p k", p=P), allow_slow_non_contiguous=True).then_inc(S("rows_in"), 16)
                sp.dma_start(a1[:], A[f"L0_gnn_mlb_{l}"].rearrange("(k p) -> p k", p=P), allow_slow_non_contiguous=True).then_inc(S("rows_in"), 16)
                if l:
                    sp.dma_start(g2[:], row(f"L0_gnn_lng_{l}")).then_inc(S("rows_in"), 16)
                    sp.dma_start(a2[:], row(f"L0_gnn_lnb_{l}")).then_inc(S("rows_in"), 16)

                def fetch(i, u):
                    if l:
                        sp.wait_ge(S("x_out"), at(B + i - 1))
                        sp.dma_start(old[u][:], xin[:, bass.ds(i, 1), :]).then_inc(S(f"old_in{u}"), 16)

                def store(i, u):
                    sp.wait_ge(S("x_out"), at(B + i + 1))
                    sp.dma_start(xout[:, bass.ds(i, 1), :], xn[u][:]).then_inc(S(f"x_stored{u}"), 16)

                fetch(0, 0)
                with sp.Fori(0, NT // 2 - 1) as it:
                    for u in range(2):
                        fetch(2 * it + u + 1, 1 - u)
                        store(2 * it + u, u)
                fetch(NT - 1, 1)
                store(NT - 2, 0)
                store(NT - 1, 1)
                for u in range(2):
                    sp.wait_ge(S(f"x_stored{u}"), dma_at((B + NT) // 2))

            @block.scalar
            def _(act):
                s = nc.scalar
                s.preload_act_table_set(EXP_AND_LOG)

                def split_h(i, u):
                    act.wait_ge(S("u_psum"), at(B + i - 1))
                    s.copy(hh[u][:], W["hT"][:, :, bass.ds(i * P, P)]).then_inc(S("h_hi"), 1)

                def norm1(i, u):
                    rstd(nc, act, K, mv1[u], S, B + i, "stat1", "log1", "rstd1")

                def relu_g(i, u):
                    act.wait_ge(S("g_turned"), at(B + i + 1))
                    act.wait_ge(S("g_lo"), at(B + i))
                    act.wait_ge(S("g_hi"), at(B + i))
                    for k in range(K2):
                        last = s.activation(gr[:, k * P:(k + 1) * P], psg[:, k * P:(k + 1) * P], ACT.Relu,
                                            bias=a1[:, k:k + 1], scale=g1[:, k:k + 1])
                    last.then_inc(S("g_relu"), 1)
                    act.wait_ge(S("g_relu"), at(B + i + 1))
                    act.wait_ge(S("x_psum"), at(B + i - 1))
                    s.copy(gh[u][:], gr[:]).then_inc(S("g_hi"), 1)

                def norm2(i, u):
                    if l:
                        rstd(nc, act, K, mv2[u], S, BR + i, "stat2", "log2", "rstd2")

                def body(s, par, half, has):
                    if has(-2):
                        norm2(s - 2, par(-2))
                    if has(0) and has(2):
                        split_h(s + 2, par(2))
                    if has(0):
                        relu_g(s, par(0))
                    if has(1):
                        norm1(s + 1, par(1))

                for u in range(2):
                    split_h(u, u)
                act.wait_ge(S("rows_in"), ROWS_IN)
                high(act)
                steps(act, body)

            @block.gpsimd
            def _(pool):
                g = nc.gpsimd

                def low_h(i, u):
                    pool.wait_ge(S("h_hi"), at(B + i + 1))
                    pool.wait_ge(S("u_psum"), at(B + i - 1))
                    g.tensor_tensor(hl[u][:], W["hT"][:, :, bass.ds(i * P, P)], r32(hh[u][:]), ALU.subtract).then_inc(S("h_lo"), 1)

                def low_g(i, u):
                    pool.wait_ge(S("g_hi"), at(B + i + 1))
                    pool.wait_ge(S("x_psum"), at(B + i - 1))
                    g.tensor_tensor(gl[u][:], gr[:], r32(gh[u][:]), ALU.subtract).then_inc(S("g_lo"), 1)

                low_h(0, 0)
                low_h(1, 1)
                low(pool, g)
                with pool.Fori(0, NT // 2 - 1) as it:
                    for u in range(2):
                        low_h(2 * it + u + 2, u)
                        low_g(2 * it + u, u)
                low_g(NT - 2, 0)
                low_g(NT - 1, 1)

            @block.vector
            def _(dve):
                v = nc.vector

                def first(i, u):
                    dve.wait_ge(S("u_psum"), at(B + i + 1))
                    dve.wait_ge(S("normed"), at(B + i))
                    dve.wait_ge(S("g_turned"), at(B + i - 1))
                    v.tensor_tensor(gg[u][:], psu[u][:], b1[:], ALU.add).then_inc(S("u_added"), 1)
                    dve.wait_ge(S("u_added"), at(B + i + 1))
                    dve.wait_ge(S("stat1"), at(B + i))
                    mean_var(nc, dve, gg[u], 2, st1, mv1[u][:], S, B + i, "stat1", "parts1")
                    dve.wait_ge(S("rstd1"), at(B + i + 1))
                    v.tensor_scalar(gg[u][:], gg[u][:], mv1[u][:, 0:1], mv1[u][:, 1:2], ALU.subtract, ALU.mult).then_inc(S("normed"), 1)

                def second(i, u, half):
                    dve.wait_ge(S("x_psum"), at(B + i + 1))
                    dve.wait_ge(S("x_out"), at(B + i))
                    dve.wait_ge(S(f"x_stored{u}"), dma_at(B // 2 + half))
                    if l == 0:
                        v.tensor_tensor(xn[u][:], psx[u][:], b2[:], ALU.add).then_inc(S("x_out"), 1)
                        return
                    q = BR + i
                    v.tensor_tensor(xn[u][:], psx[u][:], b2[:], ALU.add).then_inc(S("x_added"), 1)
                    dve.wait_ge(S("x_added"), at(q + 1))
                    dve.wait_ge(S("stat2"), at(q))
                    mean_var(nc, dve, xn[u], 1, st2, mv2[u][:], S, q, "stat2", "parts2")
                    dve.wait_ge(S("rstd2"), at(q + 1))
                    v.tensor_scalar(xn[u][:], xn[u][:], mv2[u][:, 0:1], mv2[u][:, 1:2], ALU.subtract, ALU.mult).then_inc(S("x_normed"), 1)
                    dve.wait_ge(S("x_normed"), at(q + 1))
                    v.tensor_tensor(xn[u][:], xn[u][:], g2[:], ALU.mult).then_inc(S("x_scaled"), 1)
                    dve.wait_ge(S("x_scaled"), at(q + 1))
                    v.tensor_tensor(xn[u][:], xn[u][:], a2[:], ALU.add).then_inc(S("x_shifted"), 1)
                    dve.wait_ge(S("x_shifted"), at(q + 1))
                    dve.wait_ge(S(f"old_in{u}"), dma_at(BR // 2 + half + 1))
                    v.scalar_tensor_tensor(xn[u][:], xn[u][:], 0.0, old[u][:], ALU.max, ALU.add).then_inc(S("x_out"), 1)

                def body(s, par, half, has):
                    if has(-2):
                        second(s - 2, par(-2), half(-2))
                    if has(1):
                        first(s + 1, par(1))

                dve.wait_ge(S("rows_in"), ROWS_IN)
                steps(dve, body)

            @block.tensor
            def _(pe):
                t = nc.tensor

                def up(i, u):
                    pe.wait_ge(S("h_lo"), at(B + i + 1))
                    pe.wait_ge(S("u_added"), at(B + i - 1))
                    for h in range(2):
                        last = three(t, psu[u][:, h * 512:(h + 1) * 512], hh[u], hl[u],
                                     lambda k: W["w1h"][:, k, h * 512:(h + 1) * 512],
                                     lambda k: W["w1l"][:, k, h * 512:(h + 1) * 512], KC, lambda a, k: a[:, k, :])
                    last.then_inc(S("u_psum"), 1)

                def turn_g(i, u):
                    pe.wait_ge(S("normed"), at(B + i + 1))
                    pe.wait_ge(S("g_relu"), at(B + i))
                    turn_tile(t, psg, gg[u], K2, K["ident"][:]).then_inc(S("g_turned"), 1)

                def down(i, u):
                    pe.wait_ge(S("g_lo"), at(B + i + 1))
                    pe.wait_ge(S("x_out"), at(B + i - 1))
                    three(t, psx[u][:], gh[u], gl[u], half2(W["w2h"], w2h), half2(W["w2l"], w2l), K2,
                          lambda a, k: a[:, k * P:(k + 1) * P]).then_inc(S("x_psum"), 1)

                def body(s, par, half, has):
                    if has(1):
                        up(s + 1, par(1))
                    if has(0):
                        turn_g(s, par(0))
                    if has(-1):
                        if not has(-2):
                            pe.wait_ge(S("w2_lo"), 2 * (l + 1))
                        down(s - 1, par(-1))

                steps(pe, body)


def join_layers(nc, S, K, T, A, W, EW):
    with ExitStack() as c:
        sb = lambda n, s, d=F32: c.enter_context(nc.sbuf_tensor(f"{n}_j", s, d))
        CC = 3 * KC
        cwh, cwl = sb("cwh", [P, CC, H], F32R), sb("cwl", [P, CC, H], F32R)
        abh, abl = sb("abh", [P, K2, H], F32R), sb("abl", [P, K2, H], F32R)
        cat = [sb(f"cat{u}", [P, 4, H]) for u in range(2)]
        ch, cl = ([sb(f"{n}{u}", [P, 3 * H], F32R) for u in range(2)] for n in ("ch", "cl"))
        nh, nl = sb("nh", [P, H], F32R), sb("nl", [P, H], F32R)
        yy, xt = sb("yy", [P, H]), sb("xt", [P, H])
        st, mv = sb("st", [P, 6]), sb("mv", [P, 2])
        pt, qt = sb("pt", [P, H]), sb("qt", [P, H])
        cb, b1 = sb("cb", [P, H]), sb("b1", [P, H])
        psc = c.enter_context(nc.psum_tensor("psc_j", [P, 3 * H], F32))
        psy = c.enter_context(nc.psum_tensor("psy_j", [P, H], F32))
        psn = c.enter_context(nc.psum_tensor("psn_j", [P, H], F32))
        psp = c.enter_context(nc.psum_tensor("psp_j", [P, H], F32))
        psq = c.enter_context(nc.psum_tensor("psq_j", [P, H], F32))
        cw, w1 = rows(A["L0_gnn_cw"], CC), rows(A["L1_gnn_W1"][0:H2, :], K2)
        load, high, low, _ = split_chunks(nc, S, c, "join", [
            (cw[:, 2 * k:2 * k + 2, :], cwh[:, 2 * k:2 * k + 2, :], cwl[:, 2 * k:2 * k + 2, :]) for k in range(CC // 2)] + [
            (w1[:, 2 * k:2 * k + 2, :], abh[:, 2 * k:2 * k + 2, :], abl[:, 2 * k:2 * k + 2, :]) for k in range(KC)], stages=4)
        w2 = rows(A["L1_gnn_W2"], KC)
        load_next, alone = split_alone(nc, S, c, "edge", [
            (w2[:, 2 * k:2 * k + 2, :], EW["w2h"][:, 2 * k:2 * k + 2, :], EW["w2l"][:, 2 * k:2 * k + 2, :]) for k in range(2)])
        wc = sb("wc", [P, H])
        CHUNKS = CC // 2 + KC
        tiles = lambda x: x.rearrange("(j p) d -> p j d", p=P)
        steps = lambda eng, body: pipeline(eng, 1, NT - 1, NT, body)
        with nc.Block() as block:
            @block.sync
            def _(sp):
                def bring(i, u):
                    sp.wait_ge(S("cat_turned"), at(i - 1))
                    sp.wait_ge(S("y_added"), at(i - 1))
                    for l in range(4):
                        sp.dma_start(cat[u][:, l, :], tiles(T["x"][l])[:, bass.ds(i, 1), :]).then_inc(S(f"cat_in{u}"), 16)

                S.give_credit(sp, CREDITED_2, CREDITED_DMA_2)
                bring(0, 0)
                load(sp, range(CC // 2))
                bring(1, 1)
                sp.dma_start(cb[:], A["L0_gnn_cb"].partition_broadcast(P)).then_inc(S("join_rows"), 16)
                sp.dma_start(b1[:], A["L1_gnn_b1"].partition_broadcast(P)).then_inc(S("join_rows"), 16)
                load(sp, range(CC // 2, CHUNKS))
                with sp.Fori(1, NT // 2) as it:
                    for u in range(2):
                        bring(2 * it + u, u)
                for k in range(2):
                    sp.dma_start(wc[k * ED:(k + 1) * ED, :], A["L1_gnn_W1"][H2:H2 + ED, :]).then_inc(S("wc_in"), 16)
                load_next(sp)

            @block.scalar
            def _(act):
                s = nc.scalar
                s.preload_act_table_set(EXP_AND_LOG)

                def cat_high(i, u):
                    act.wait_ge(S("cat_turned"), at(i + 1))
                    act.wait_ge(S("y_psum"), at(i - 1))
                    s.copy(ch[u][:], psc[:]).then_inc(S("cat_hi"), 1)

                def x_high(i):
                    act.wait_ge(S("n_turned"), at(i + 1))
                    act.wait_ge(S("pq_psum"), at(i))
                    s.copy(nh[:], psn[:]).then_inc(S("n_hi"), 1)

                def store(i):
                    act.wait_ge(S("pq_psum"), at(i + 1))
                    act.wait_ge(S("p_stored"), dma_at(i))
                    s.copy(pt[:], psp[:]).then_inc(S("p_out"), 1)
                    act.wait_ge(S("p_out"), at(i + 1))
                    act.dma_start(tiles(T["src_part"])[:, bass.ds(i, 1), :], pt[:]).then_inc(S("p_stored"), 16)
                    act.wait_ge(S("q_out"), at(i + 1))
                    act.dma_start(tiles(T["dst_part"])[:, bass.ds(i, 1), :], qt[:]).then_inc(S("q_stored"), 16)

                def body(s, par, half, has):
                    if has(1):
                        cat_high(s + 1, par(1))
                        if not has(0):
                            high(act, range(CC // 2))
                        elif not has(-1):
                            high(act, range(CC // 2, CHUNKS))
                    if has(-1):
                        x_high(s - 1)
                    if has(0):
                        rstd(nc, act, K, mv, S, s, "y_stat", "y_log", "y_rstd")
                    if has(-1):
                        store(s - 1)

                steps(act, body)
                act.wait_ge(S("p_stored"), dma_at(NT))
                act.wait_ge(S("q_stored"), dma_at(NT))

            @block.vector
            def _(dve):
                v = nc.vector

                def cat_low(i, u):
                    dve.wait_ge(S("cat_hi"), at(i + 1))
                    v.tensor_tensor(cl[u][:], psc[:], r32(ch[u][:]), ALU.subtract).then_inc(S("cat_lo"), 1)

                def norm(i, u, half):
                    dve.wait_ge(S(f"cat_in{u}"), dma_at(4 * half + 4))
                    dve.wait_ge(S("y_psum"), at(i + 1))
                    dve.wait_ge(S("y_norm"), at(i))
                    v.tensor_tensor(yy[:], psy[:], cb[:], ALU.add).then_inc(S("y_biased"), 1)
                    dve.wait_ge(S("y_biased"), at(i + 1))
                    v.tensor_tensor(yy[:], yy[:], cat[u][:, 0, :], ALU.add).then_inc(S("y_added"), 1)
                    dve.wait_ge(S("y_added"), at(i + 1))
                    dve.wait_ge(S("y_stat"), at(i))
                    mean_var(nc, dve, yy, 1, st, mv[:], S, i, "y_stat", "y_parts")
                    dve.wait_ge(S("y_rstd"), at(i + 1))
                    dve.wait_ge(S("n_turned"), at(i))
                    dve.wait_ge(S("x_kept"), at(i))
                    v.tensor_scalar(xt[:], yy[:], mv[:, 0:1], mv[:, 1:2], ALU.subtract, ALU.mult).then_inc(S("y_norm"), 1)

                def x_low(i):
                    dve.wait_ge(S("n_hi"), at(i + 1))
                    v.tensor_tensor(nl[:], psn[:], r32(nh[:]), ALU.subtract).then_inc(S("n_lo"), 1)

                def dst_part(i):
                    dve.wait_ge(S("pq_psum"), at(i + 1))
                    dve.wait_ge(S("q_stored"), dma_at(i))
                    v.tensor_tensor(qt[:], psq[:], b1[:], ALU.add).then_inc(S("q_out"), 1)

                def body(s, par, half, has):
                    if has(1):
                        cat_low(s + 1, par(1))
                        if not has(0):
                            low(dve, v, range(CC // 2))
                        elif not has(-1):
                            low(dve, v, range(CC // 2, CHUNKS))
                            dve.wait_ge(S("join_rows"), 32)
                    if has(-1):
                        x_low(s - 1)
                    if has(0):
                        norm(s, par(0), half(0))
                    if has(-1):
                        dst_part(s - 1)

                steps(dve, body)

            @block.gpsimd
            def _(pool):
                g = nc.gpsimd

                def keep(i):
                    pool.wait_ge(S("y_norm"), at(i + 1))
                    carry(pool, S)
                    g.tensor_copy(W["X"][:, bass.ds(i, 1), :], xt[:]).then_inc(S("x_kept"), 1)

                with pool.Fori(0, NT - 2) as i:
                    keep(i)
                pool.wait_ge(S("wc_in"), 32)
                g.tensor_copy(EW["wch2"][:], wc[:]).then_inc(S("wc_split"), 1)
                pool.wait_ge(S("wc_split"), 1)
                g.tensor_tensor(EW["wcl"][:], wc[0:ED, :], r32(EW["wch2"][0:ED, :]), ALU.subtract).then_inc(S("wc_split"), 1)
                alone(pool, range(2))
                keep(NT - 2)
                keep(NT - 1)
                pool.wait_ge(S("wc_split"), 2)
                pool.wait_ge(S("edge_lo"), 2)

            @block.tensor
            def _(pe):
                t = nc.tensor

                def turn_cat(i, u, half):
                    pe.wait_ge(S(f"cat_in{u}"), dma_at(4 * half + 4))
                    pe.wait_ge(S("cat_lo"), at(i))
                    turn_tile(t, psc, cat[u][:, 1:4, :].rearrange("p l d -> p (l d)"), CC, K["ident"][:]).then_inc(S("cat_turned"), 1)

                def product(i, u):
                    pe.wait_ge(S("cat_lo"), at(i + 1))
                    pe.wait_ge(S("y_biased"), at(i))
                    three(t, psy[:], ch[u], cl[u], lambda k: cwh[:, k, :], lambda k: cwl[:, k, :], CC,
                          lambda a, k: a[:, k * P:(k + 1) * P]).then_inc(S("y_psum"), 1)

                def turn_x(i):
                    pe.wait_ge(S("y_norm"), at(i + 1))
                    pe.wait_ge(S("n_lo"), at(i))
                    turn_tile(t, psn, xt, KC, K["ident"][:]).then_inc(S("n_turned"), 1)

                def parts(i):
                    pe.wait_ge(S("n_lo"), at(i + 1))
                    pe.wait_ge(S("p_out"), at(i))
                    pe.wait_ge(S("q_out"), at(i))
                    three(t, psp[:], nh, nl, lambda k: abh[:, k, :], lambda k: abl[:, k, :], KC,
                          lambda a, k: a[:, k * P:(k + 1) * P])
                    three(t, psq[:], nh, nl, lambda k: abh[:, KC + k, :], lambda k: abl[:, KC + k, :], KC,
                          lambda a, k: a[:, k * P:(k + 1) * P]).then_inc(S("pq_psum"), 1)

                def body(s, par, half, has):
                    if has(-1):
                        if has(1):
                            turn_cat(s + 1, par(1), half(1))
                        turn_x(s - 1)
                    if has(0):
                        if not has(-1):
                            pe.wait_ge(S("join_lo"), CC // 2)
                        product(s, par(0))
                    if has(1) and not has(-1):
                        turn_cat(s + 1, par(1), half(1))
                    if has(0) and not has(-1):
                        pe.wait_ge(S("join_lo"), CHUNKS)
                    if has(-1):
                        parts(s - 1)

                steps(pe, body)


def mish_square(v, w):
    return v.scalar_tensor_tensor(w, w, 2.0, w, ALU.add, ALU.mult)


def edge_messages(nc, S, K, T, A, W, EW, UW):
    with ExitStack() as c:
        sb = lambda n, s, d=F32: c.enter_context(nc.sbuf_tensor(f"{n}_e", s, d))
        w2h, w2l, wcl = EW["w2h"], EW["w2l"], EW["wcl"]
        wch2 = EW["wch2"]
        at_rows = [sb(f"at_rows{u}", [P, 4, P]) for u in range(2)]
        attr = sb("attr", [P, 4 * P], F32R)
        G = [sb(f"G{u}", [P, 4, H]) for u in range(2)]
        GI = [sb(f"GI{u}", [P, 4, 2], I32) for u in range(2)]
        zw = [sb(f"zw{u}", [P, H2]) for u in range(2)]
        zh = [sb(f"zh{u}", [P, H2]) for u in range(2)]
        hh, hl = ([sb(f"{n}{u}", [P, KC, 512], F32R) for u in range(2)] for n in ("hh", "hl"))
        mw = [sb(f"mw{u}", [P, H2]) for u in range(2)]
        mx = [sb(f"mx{u}", [P, H2]) for u in range(2)]
        hot = [sb(f"hot{u}", [P, 4, P]) for u in range(2)]
        b2 = sb("b2", [P, H])
        psa = c.enter_context(nc.psum_tensor("psa_e", [P, 512], F32))
        psz = [c.enter_context(nc.psum_tensor(f"psz{u}_e", [P, H2], F32)) for u in range(2)]
        psm = c.enter_context(nc.psum_tensor("psm_e", [P, H2], F32))
        pss = c.enter_context(nc.psum_tensor("pss_e", [P, H], F32))
        w3 = rows(A["L1_gnn_W3"], K2)
        load_next, alone = split_alone(nc, S, c, "w3", [
            (w3[:, 2 * k:2 * k + 2, :], UW["w3h"][:, 2 * k:2 * k + 2, :], UW["w3l"][:, 2 * k:2 * k + 2, :]) for k in range(KC)])
        table = T["table"].rearrange("(t p) f -> p t f", p=P)
        with nc.Block() as block:
            @block.sync
            def _(sp):
                sp.dma_start(b2[:], A["L1_gnn_b2"].partition_broadcast(P)).then_inc(S("edge_b2_in"), 16)
                with sp.Fori(0, QUADS // 2) as it:
                    for u in range(2):
                        q = 2 * it + u
                        sp.wait_ge(S("attr_turned"), at(q - 1))
                        sp.dma_start(at_rows[u][:, :, 0:ED], table[:, bass.ds(4 * q, 4), 0:ED]).then_inc(S(f"attr_in{u}"), 16)
                load_next(sp)

            def both(eng, body):
                body(0, 0, 0, False, True, True)
                body(1, 1, 0, True, True, True)
                with eng.Fori(1, QUADS // 2 - 1) as it:
                    for u in range(2):
                        body(2 * it + u, u, it, True, True, True)
                body(QUADS - 2, 0, QUADS // 2 - 1, True, False, True)
                body(QUADS - 1, 1, QUADS // 2 - 1, True, False, False)

            @block.gpsimd
            def _(pool):
                g = nc.gpsimd

                def index(q, u):
                    pool.wait_ge(S("z_ready"), at(2 * q - 2))
                    carry(pool, S)
                    g.tensor_copy(GI[u][:], K["src_dst"][:, bass.ds(4 * q, 4), :]).then_inc(S("index_copied"), 1)
                    pool.wait_ge(S("index_copied"), at(q + 1))
                    carry(pool, S)
                    for k in range(4):
                        g.indirect_dma_start(out=G[u][:, k, :], out_offset=None, in_=T["src_part"],
                                             in_offset=bass.IndirectOffsetOnAxis(ap=GI[u][:, k, 0:1], axis=0)).then_inc(S(f"src_rows{u}"), 16)

                def add_dst(q, u, it):
                    pool.wait_ge(S(f"src_rows{u}"), 64 * it + 64)
                    carry(pool, S)
                    for k in range(4):
                        g.indirect_dma_start(out=G[u][:, k, :], out_offset=None, in_=T["dst_part"],
                                             in_offset=bass.IndirectOffsetOnAxis(ap=GI[u][:, k, 1:2], axis=0),
                                             compute_op=ALU.add).then_inc(S(f"dst_rows{u}"), 16)

                def low_h(q, u):
                    for f in range(2):
                        n = 2 * q + f
                        pool.wait_ge(S("z_hi"), at(n + 1))
                        pool.wait_ge(S("m_ready"), at(2 * q - 2))
                        g.tensor_tensor(hl[u][:, 2 * f:2 * f + 2, :], zh[f][:].rearrange("p (a b) -> p a b", a=2),
                                        r32(hh[u][:, 2 * f:2 * f + 2, :]), ALU.subtract).then_inc(S("z_lo"), 1)

                for u in range(2):
                    g.memset(at_rows[u][:, :, ED:P], 0.0).then_inc(S("attr_zero"), 1)
                index(0, 0)
                add_dst(0, 0, 0)
                index(1, 1)
                add_dst(1, 1, 0)
                with pool.Fori(0, QUADS // 2 - 1) as it:
                    for u in range(2):
                        q = 2 * it + u
                        index(q + 2, u)
                        low_h(q, u)
                        add_dst(q + 2, u, it + 1)
                low_h(QUADS - 2, 0)
                alone(pool, range(2))
                low_h(QUADS - 1, 1)
                alone(pool, range(2, KC))
                pool.wait_ge(S("w3_lo"), KC)

            @block.tensor
            def _(pe):
                t = nc.tensor

                def turn_attr(q, u, it):
                    pe.wait_ge(S(f"attr_in{u}"), dma_at(it + 1))
                    pe.wait_ge(S("attr_lo"), at(q))
                    for k in range(4):
                        last = t.matmul(psa[:, k * P:(k + 1) * P], at_rows[u][:, k, :], K["ident"][:], is_transpose=True,
                                        start=k == 0, stop=k == 3, skip_group_check=True)
                    last.then_inc(S("attr_turned"), 1)

                def layer1(q, u, it):
                    pe.wait_ge(S(f"dst_rows{u}"), 64 * it + 64)
                    for f in range(2):
                        pe.wait_ge(S("z_h"), at(2 * q + f - 1))
                        for a in range(2):
                            j = 2 * f + a
                            for k in range(4):
                                t.matmul(psz[f][:, a * 512 + k * P:a * 512 + (k + 1) * P], G[u][:, k, j * P:(j + 1) * P], K["ident"][:],
                                         is_transpose=True, start=k == 0, stop=False, skip_group_check=True)
                        if f == 0:
                            pe.wait_ge(S("attr_lo"), at(q + 1))
                        for a in range(2):
                            j = 2 * f + a
                            out = psz[f][:, a * 512:(a + 1) * 512]
                            t.matmul(out, wch2[:, j * P:(j + 1) * P], attr[:], start=False, stop=False, skip_group_check=True)
                            last = t.matmul(out, wcl[:, j * P:(j + 1) * P], attr[0:ED, :], start=False, stop=True, skip_group_check=True)
                        last.then_inc(S("z_ready"), 1)

                def layer2(q, u, f):
                    n = 2 * q + f
                    if f == 0:
                        pe.wait_ge(S("z_lo"), at(2 * q + 2))
                    pe.wait_ge(S("m_x"), at(n))
                    for a in range(2):
                        e0 = (2 * f + a) * P
                        last = three(t, psm[:, a * 512:(a + 1) * 512], hh[u], hl[u], lambda k: w2h[:, k, :], lambda k: w2l[:, k, :],
                                     KC, lambda x, k: x[:, k, e0:e0 + P])
                    last.then_inc(S("m_ready"), 1)

                def sum_up(q, u, f):
                    n = 2 * q + f
                    pe.wait_ge(S("m_msg"), at(n + 1))
                    pe.wait_ge(S("onehot"), at(q + 1))
                    pe.wait_ge(S("seg_added"), at(n))
                    t.matmul(pss[:], hot[u][:, 2 * f, :], mw[f][:, 0:512], start=True, stop=False)
                    t.matmul(pss[:], hot[u][:, 2 * f + 1, :], mw[f][:, 512:1024], start=False, stop=True).then_inc(S("seg_ready"), 1)

                pe.wait_ge(S("attr_zero"), 2)
                turn_attr(0, 0, 0)
                layer1(0, 0, 0)
                turn_attr(1, 1, 0)

                def body(q, u, it, back, attrs, more):
                    if more:
                        layer1(q + 1, 1 - u, it + u)
                    if back:
                        sum_up(q - 1, 1 - u, 0)
                    layer2(q, u, 0)
                    if back:
                        sum_up(q - 1, 1 - u, 1)
                    if attrs:
                        turn_attr(q + 2, u, it + 1)
                    layer2(q, u, 1)

                both(pe, body)
                sum_up(QUADS - 1, 1, 0)
                sum_up(QUADS - 1, 1, 1)

            @block.scalar
            def _(act):
                s = nc.scalar
                s.preload_act_table_set(EXP_AND_LOG)

                def z_exp(q, f):
                    n = 2 * q + f
                    act.wait_ge(S("z_ready"), at(n + 1))
                    act.wait_ge(S("z_h"), at(n - 1))
                    s.activation(zw[f][:], psz[f][:], ACT.Exp).then_inc(S("z_exp"), 1)

                def z_r(q, f):
                    n = 2 * q + f
                    act.wait_ge(S("z_u"), at(n + 1))
                    s.activation(zw[f][:], zw[f][:], ACT.Ln, scale=0.5, bias=1.0).then_inc(S("z_ln"), 1)
                    act.wait_ge(S("z_ln"), at(n + 1))
                    s.activation(zw[f][:], zw[f][:], ACT.Exp, scale=-1.0).then_inc(S("z_r"), 1)

                def z_hi(q, u, f):
                    n = 2 * q + f
                    act.wait_ge(S("z_h"), at(n + 1))
                    act.wait_ge(S("m_ready"), at(2 * q - 2))
                    s.copy(hh[u][:, 2 * f:2 * f + 2, :], zh[f][:].rearrange("p (a b) -> p a b", a=2)).then_inc(S("z_hi"), 1)

                def m_exp(q, f):
                    n = 2 * q + f
                    act.wait_ge(S("m_x"), at(n + 1))
                    act.wait_ge(S("seg_ready"), at(n - 1))
                    s.activation(mw[f][:], mx[f][:], ACT.Exp).then_inc(S("m_exp"), 1)

                def m_r(q, f):
                    n = 2 * q + f
                    act.wait_ge(S("m_u"), at(n + 1))
                    s.activation(mw[f][:], mw[f][:], ACT.Ln, scale=0.5, bias=1.0).then_inc(S("m_ln"), 1)
                    act.wait_ge(S("m_ln"), at(n + 1))
                    s.activation(mw[f][:], mw[f][:], ACT.Exp, scale=-1.0).then_inc(S("m_r"), 1)

                def attr_high(q):
                    act.wait_ge(S("attr_turned"), at(q + 1))
                    act.wait_ge(S("z_ready"), at(2 * q))
                    s.copy(attr[0:ED, :], psa[0:ED, :]).then_inc(S("attr_hi"), 1)

                def hidden(q, u):
                    z_exp(q, 0)
                    z_exp(q, 1)
                    z_r(q, 0)
                    z_r(q, 1)
                    z_hi(q, u, 0)
                    z_hi(q, u, 1)

                attr_high(0)
                attr_high(1)
                hidden(0, 0)

                def body(q, u, it, back, attrs, more):
                    if back:
                        m_exp(q - 1, 1)
                    if more:
                        z_exp(q + 1, 0)
                        z_exp(q + 1, 1)
                    if back:
                        m_r(q - 1, 1)
                    if more:
                        z_r(q + 1, 0)
                        z_r(q + 1, 1)
                    m_exp(q, 0)
                    if more:
                        z_hi(q + 1, 1 - u, 0)
                        z_hi(q + 1, 1 - u, 1)
                    if attrs:
                        attr_high(q + 2)
                    m_r(q, 0)

                both(act, body)
                m_exp(QUADS - 1, 1)
                m_r(QUADS - 1, 1)

            @block.vector
            def _(dve):
                v = nc.vector

                def z_u(q, f):
                    n = 2 * q + f
                    dve.wait_ge(S("z_exp"), at(n + 1))
                    v.tensor_scalar(zw[f][:], zw[f][:], CAP, None, ALU.min).then_inc(S("z_min"), 1)
                    dve.wait_ge(S("z_min"), at(n + 1))
                    mish_square(v, zw[f][:]).then_inc(S("z_u"), 1)

                def z_h(q, f):
                    n = 2 * q + f
                    dve.wait_ge(S("z_r"), at(n + 1))
                    dve.wait_ge(S("z_lo"), at(n - 1))
                    v.scalar_tensor_tensor(zh[f][:], zw[f][:], 1.0, psz[f][:], ALU.subtract, ALU.mult).then_inc(S("z_h"), 1)

                def m_u(q, f):
                    n = 2 * q + f
                    dve.wait_ge(S("m_exp"), at(n + 1))
                    v.tensor_scalar(mw[f][:], mw[f][:], CAP, None, ALU.min).then_inc(S("m_min"), 1)
                    dve.wait_ge(S("m_min"), at(n + 1))
                    mish_square(v, mw[f][:]).then_inc(S("m_u"), 1)

                def m_x(q, f):
                    n = 2 * q + f
                    dve.wait_ge(S("m_ready"), at(n + 1))
                    dve.wait_ge(S("m_msg"), at(n - 1))
                    v.tensor_tensor(mx[f][:].rearrange("p (a b) -> p a b", a=2), b2[:].unsqueeze(1).to_broadcast([P, 2, H]),
                                    psm[:].rearrange("p (a b) -> p a b", a=2), ALU.subtract).then_inc(S("m_x"), 1)

                def m_msg(q, f):
                    n = 2 * q + f
                    dve.wait_ge(S("m_r"), at(n + 1))
                    v.scalar_tensor_tensor(mw[f][:], mw[f][:], 1.0, mx[f][:], ALU.subtract, ALU.mult).then_inc(S("m_msg"), 1)

                def attr_low(q):
                    dve.wait_ge(S("attr_hi"), at(q + 1))
                    v.tensor_tensor(attr[ED:P, :], psa[0:ED, :], r32(attr[0:ED, :]), ALU.subtract).then_inc(S("attr_lo"), 1)

                def onehots(q, u):
                    dve.wait_ge(S("seg_ready"), at(2 * q - 2))
                    for k in range(4):
                        last = v.tensor_scalar(hot[u][:, k, :], K["iota"][:], K["meta"][:, bass.ds(4 * q + k, 1), 2], None, ALU.is_equal)
                    last.then_inc(S("onehot"), 1)

                def add_sums(q, f):
                    n = 2 * q + f
                    tile = dve.value_load(K["pair_tile"][0:1, bass.ds(n, 1)], min_val=0, max_val=NT - 1)
                    dve.wait_ge(S("seg_ready"), at(n + 1))
                    agg = W["agg"][:, bass.ds(tile, 1), :]
                    dve.wait_ge(S("seg_added"), at(n))
                    v.tensor_tensor(agg, agg, pss[:], ALU.add).then_inc(S("seg_added"), 1)

                def hidden(q):
                    z_u(q, 0)
                    z_u(q, 1)
                    z_h(q, 0)
                    z_h(q, 1)

                v.memset(W["agg"][:], 0.0).then_inc(S("agg_zero"), 1)
                dve.wait_ge(S("agg_zero"), 1)
                attr_low(0)
                attr_low(1)
                hidden(0)
                onehots(0, 0)
                dve.wait_ge(S("edge_b2_in"), 16)

                def body(q, u, it, back, attrs, more):
                    if back:
                        m_u(q - 1, 1)
                    if more:
                        z_u(q + 1, 0)
                    if back:
                        m_msg(q - 1, 1)
                        add_sums(q - 1, 0)
                    if more:
                        z_u(q + 1, 1)
                    m_x(q, 0)
                    if more:
                        z_h(q + 1, 0)
                        z_h(q + 1, 1)
                    if back:
                        add_sums(q - 1, 1)
                    m_u(q, 0)
                    if attrs:
                        attr_low(q + 2)
                    m_x(q, 1)
                    m_msg(q, 0)
                    if more:
                        onehots(q + 1, 1 - u)

                both(dve, body)
                m_u(QUADS - 1, 1)
                m_msg(QUADS - 1, 1)
                add_sums(QUADS - 1, 0)
                add_sums(QUADS - 1, 1)


def update_nodes(nc, S, K, T, A, W, UW, out):
    with ExitStack() as c:
        sb = lambda n, s, d=F32: c.enter_context(nc.sbuf_tensor(f"{n}_u", s, d))
        w3h, w3l = UW["w3h"], UW["w3l"]
        w4h, w4l = sb("w4h", [P, KC, H], F32R), sb("w4l", [P, KC, H], F32R)
        xa = [sb(f"xa{u}", [P, H2]) for u in range(2)]
        xb, xe = sb("xb", [P, NT, H]), W["X"]
        oh, ol = ([sb(f"{n}{u}", [P, H2], F32R) for u in range(2)] for n in ("oh", "ol"))
        vx, vw, vo = sb("vx", [P, H]), sb("vw", [P, H]), sb("vo", [P, H])
        vh, vl = sb("vh", [P, H], F32R), sb("vl", [P, H], F32R)
        yy = sb("yy", [P, H])
        ft = [sb(f"ft{u}", [P, H]) for u in range(2)]
        st, mv = sb("st", [P, 6]), sb("mv", [P, 2])
        sf, mf = sb("sf", [P, 6]), sb("mf", [P, 2])
        b3, b4, ga, be = (sb(n, [P, H]) for n in ("b3", "b4", "ga", "be"))
        pso = c.enter_context(nc.psum_tensor("pso_u", [P, H2], F32))
        psv = [c.enter_context(nc.psum_tensor(f"psv{u}_u", [P, H], F32)) for u in range(2)]
        pst = c.enter_context(nc.psum_tensor("pst_u", [P, H], F32))
        psw = c.enter_context(nc.psum_tensor("psw_u", [P, H], F32))
        w4 = rows(A["L1_gnn_W4"], KC)
        load, high, low, _ = split_chunks(nc, S, c, "w4", [
            (w4[:, 2 * k:2 * k + 2, :], w4h[:, 2 * k:2 * k + 2, :], w4l[:, 2 * k:2 * k + 2, :]) for k in range(2)])
        steps = lambda eng, body: pipeline(eng, 3, NT - 1, NT + 2, body)

        with nc.Block() as block:
            @block.sync
            def _(sp):
                for tile, name in ((b3, "b3"), (b4, "b4"), (ga, "gamma"), (be, "beta")):
                    sp.dma_start(tile[:], A[f"L1_gnn_{name}"].partition_broadcast(P)).then_inc(S("upd_rows"), 16)
                load(sp)
                whole = out[0:(NT - 1) * P, :].rearrange("(j p) d -> p j d", p=P)

                def store(i, u):
                    sp.wait_ge(S("f_out"), at(i + 1))
                    sp.dma_start(whole[:, bass.ds(i, 1), :], ft[u][:]).then_inc(S(f"f_stored{u}"), 16)

                with sp.Fori(0, NT // 2 - 1) as it:
                    for u in range(2):
                        store(2 * it + u, u)
                store(NT - 2, 0)
                sp.wait_ge(S("f_out"), at(NT))
                sp.dma_start(out[(NT - 1) * P:N, :], ft[1][0:LAST, :]).then_inc(S("f_stored1"), 16)
                for u in range(2):
                    sp.wait_ge(S(f"f_stored{u}"), dma_at(NT // 2))

            @block.gpsimd
            def _(pool):
                g = nc.gpsimd

                def keep(i, u):
                    pool.wait_ge(S("o_turned"), at(i - 1))
                    carry(pool, S)
                    g.tensor_copy(xa[u][:, 0:H], W["X"][:, bass.ds(i, 1), :]).then_inc(S("o_kept"), 1)
                    g.tensor_copy(xa[u][:, H:H2], W["agg"][:, bass.ds(i, 1), :]).then_inc(S("o_kept"), 1)

                def bases(i):
                    one = bass.ds(i, 1)
                    g.tensor_tensor(xb[:, one, :], W["X"][:, one, :], b4[:].unsqueeze(1), ALU.add).then_inc(S("based"), 1)
                    pool.wait_ge(S("based"), at(i + 1))
                    pool.wait_ge(S("o_kept"), at(2 * i + 2))
                    carry(pool, S)
                    g.tensor_tensor(xe[:, one, :], W["X"][:, one, :], be[:].unsqueeze(1), ALU.add).then_inc(S("bases"), 1)

                pool.wait_ge(S("upd_rows"), 64)
                with pool.Fori(0, NT // 2) as it:
                    for u in range(2):
                        keep(2 * it + u, u)
                        bases(2 * it + u)

            @block.tensor
            def _(pe):
                t = nc.tensor

                def turn_xa(i, u):
                    pe.wait_ge(S("o_kept"), at(2 * i + 2))
                    pe.wait_ge(S("o_lo"), at(i))
                    turn_tile(t, pso, xa[u], K2, K["ident"][:]).then_inc(S("o_turned"), 1)

                def product3(i, u):
                    pe.wait_ge(S("o_lo"), at(i + 1))
                    pe.wait_ge(S("v_x"), at(i - 1))
                    three(t, psv[u][:], oh[u], ol[u], lambda k: w3h[:, k, :], lambda k: w3l[:, k, :], K2,
                          lambda a, k: a[:, k * P:(k + 1) * P]).then_inc(S("v_psum"), 1)

                def turn_u(i):
                    pe.wait_ge(S("v_out"), at(i + 1))
                    pe.wait_ge(S("v_lo"), at(i))
                    turn_tile(t, pst, vo, KC, K["ident"][:]).then_inc(S("v_turned"), 1)

                def product4(i):
                    pe.wait_ge(S("v_lo"), at(i + 1))
                    pe.wait_ge(S("f_y"), at(i))
                    three(t, psw[:], vh, vl, lambda k: w4h[:, k, :], lambda k: w4l[:, k, :], KC,
                          lambda a, k: a[:, k * P:(k + 1) * P]).then_inc(S("w_psum"), 1)

                def body(s, par, half, has):
                    if has(1):
                        turn_xa(s + 1, par(1))
                    if has(-2):
                        turn_u(s - 2)
                    if has(0):
                        product3(s, par(0))
                    if has(-2):
                        if not has(-3):
                            pe.wait_ge(S("w4_lo"), 2)
                        product4(s - 2)

                steps(pe, body)

            @block.scalar
            def _(act):
                s = nc.scalar
                s.preload_act_table_set(EXP_AND_LOG)

                def xa_high(i, u):
                    act.wait_ge(S("o_turned"), at(i + 1))
                    act.wait_ge(S("v_psum"), at(i - 1))
                    s.copy(oh[u][:, 0:H], pso[:, 0:H])
                    s.mul(oh[u][:, H:H2], pso[:, H:H2], -1.0).then_inc(S("o_hi"), 1)

                def mish_exp(i):
                    act.wait_ge(S("v_x"), at(i + 1))
                    act.wait_ge(S("v_out"), at(i))
                    s.activation(vw[:], vx[:], ACT.Exp).then_inc(S("v_exp"), 1)

                def mish_r(i):
                    act.wait_ge(S("v_u"), at(i + 1))
                    s.activation(vw[:], vw[:], ACT.Ln, scale=0.5, bias=1.0).then_inc(S("v_ln"), 1)
                    act.wait_ge(S("v_ln"), at(i + 1))
                    s.activation(vw[:], vw[:], ACT.Exp, scale=-1.0).then_inc(S("v_r"), 1)

                def u_high(i):
                    act.wait_ge(S("v_turned"), at(i + 1))
                    act.wait_ge(S("w_psum"), at(i))
                    s.copy(vh[:], pst[:]).then_inc(S("v_hi"), 1)

                def body(s, par, half, has):
                    if has(-1):
                        mish_exp(s - 1)
                    if has(-3):
                        rstd(nc, act, K, mv, S, s - 3, "f_stat1", "f_log1", "f_rstd1")
                    if has(1):
                        xa_high(s + 1, par(1))
                        if not has(0):
                            high(act)
                    if has(-2):
                        u_high(s - 2)
                    if has(-1):
                        mish_r(s - 1)
                    if has(-3):
                        rstd(nc, act, K, mf, S, s - 3, "f_stat2", "f_log2", "f_rstd2")

                steps(act, body)

            @block.vector
            def _(dve):
                v = nc.vector

                def xa_low(i, u):
                    dve.wait_ge(S("o_hi"), at(i + 1))
                    v.tensor_tensor(ol[u][:, 0:H], pso[:, 0:H], r32(oh[u][:, 0:H]), ALU.subtract)
                    v.scalar_tensor_tensor(ol[u][:, H:H2], pso[:, H:H2], -1.0, r32(oh[u][:, H:H2]), ALU.mult, ALU.subtract).then_inc(S("o_lo"), 1)

                def mish_x(i, u):
                    dve.wait_ge(S("v_psum"), at(i + 1))
                    dve.wait_ge(S("v_out"), at(i))
                    v.tensor_tensor(vx[:], psv[u][:], b3[:], ALU.add).then_inc(S("v_x"), 1)

                def mish_u(i):
                    dve.wait_ge(S("v_exp"), at(i + 1))
                    v.tensor_scalar(vw[:], vw[:], CAP, None, ALU.min).then_inc(S("v_min"), 1)
                    dve.wait_ge(S("v_min"), at(i + 1))
                    mish_square(v, vw[:]).then_inc(S("v_u"), 1)

                def mish_out(i):
                    dve.wait_ge(S("v_r"), at(i + 1))
                    dve.wait_ge(S("v_turned"), at(i))
                    v.scalar_tensor_tensor(vo[:], vw[:], 1.0, vx[:], ALU.subtract, ALU.mult).then_inc(S("v_out"), 1)

                def u_low(i):
                    dve.wait_ge(S("v_hi"), at(i + 1))
                    v.tensor_tensor(vl[:], pst[:], r32(vh[:]), ALU.subtract).then_inc(S("v_lo"), 1)

                def add_x(i):
                    dve.wait_ge(S("bases"), at(i + 1))
                    dve.wait_ge(S("w_psum"), at(i + 1))
                    dve.wait_ge(S("f_sum"), at(i))
                    dve.wait_ge(S("f_out"), at(i))
                    v.tensor_tensor(yy[:].unsqueeze(1), xb[:, bass.ds(i, 1), :], psw[:].unsqueeze(1), ALU.subtract).then_inc(S("f_y"), 1)
                    dve.wait_ge(S("f_y"), at(i + 1))
                    mean_var(nc, dve, yy, 1, st, mv[:], S, i, "f_stat1", "f_parts1")

                def norm1(i):
                    dve.wait_ge(S("f_rstd1"), at(i + 1))
                    v.scalar_tensor_tensor(yy[:], yy[:], mv[:, 0:1], ga[:], ALU.subtract, ALU.mult).then_inc(S("f_scaled"), 1)
                    dve.wait_ge(S("f_scaled"), at(i + 1))
                    v.scalar_tensor_tensor(yy[:].unsqueeze(1), yy[:].unsqueeze(1), mv[:, 1:2], xe[:, bass.ds(i, 1), :], ALU.mult, ALU.add).then_inc(S("f_sum"), 1)
                    dve.wait_ge(S("f_sum"), at(i + 1))
                    mean_var(nc, dve, yy, 1, sf, mf[:], S, i, "f_stat2", "f_parts2")

                def norm2(i, u, half):
                    dve.wait_ge(S("f_rstd2"), at(i + 1))
                    dve.wait_ge(S(f"f_stored{u}"), dma_at(half))
                    v.tensor_scalar(ft[u][:], yy[:], mf[:, 0:1], mf[:, 1:2], ALU.subtract, ALU.mult).then_inc(S("f_out"), 1)

                def body(s, par, half, has):
                    if has(-1):
                        mish_x(s - 1, par(-1))
                    if has(-3):
                        add_x(s - 3)
                    if has(-1):
                        mish_u(s - 1)
                    if has(1):
                        xa_low(s + 1, par(1))
                        if not has(0):
                            low(dve, v)
                    if has(-2):
                        u_low(s - 2)
                    if has(-3):
                        norm1(s - 3)
                    if has(-1):
                        mish_out(s - 1)
                    if has(-3):
                        norm2(s - 3, par(-3), half(-3))

                dve.wait_ge(S("upd_rows"), 64)
                steps(dve, body)


def program(nc, A, out):
    ctx = ExitStack()
    with ctx:
        S = Sems(nc, 1)
        sb = lambda n, s, d=F32: ctx.enter_context(nc.sbuf_tensor(n, s, d))
        dram = lambda n, s: nc.dram_tensor(n, s, F32, kind="Internal").ap()
        K = {"ident": sb("ident", [P, P]), "iota": sb("iota", [P, P]), "ln_eps": sb("ln_eps", [P, 1]),
             "pair_tile": sb("pair_tile", [P, PAIRS], I32), "meta": sb("meta", [P, TILES, 4]),
             "src_dst": sb("src_dst", [P, TILES, 2], I32)}
        T = {"table": dram("table", (ROWS, ROW)), "x": [dram(f"x{l}", (NP, H)) for l in range(4)],
             "src_part": dram("src_part", (NP, H)), "dst_part": dram("dst_part", (NP, H))}
        with ExitStack() as first:
            s0 = lambda n, s, d=F32: first.enter_context(nc.sbuf_tensor(n, s, d))
            K["ones"], K["zeros"], K["iota_n"] = s0("ones", [P, P]), s0("zeros", [P, H]), s0("iota_n", [P, NP], F16)
            K["counts"] = s0("counts", [P, NT, NP], F32R)
            with nc.sbuf_tensor("odd_counts", [P, NT, NP], F32) as odd_counts:
                K["odd_counts"] = odd_counts
                sort_edges(nc, S, K, T, A)
                count_edges(nc, S, K, T, A)
            W = {"hT": s0("hT", [P, KC, NP]), "w1h": s0("w1h", [P, KC, H2], F32R), "w1l": s0("w1l", [P, KC, H2], F32R),
                 "w2h": s0("w2h", [P, KC, H], F32R), "w2l": s0("w2l", [P, KC, H], F32R)}
            for l in range(3):
                aggregate(nc, S, K, T, A, W, l)
                feed_forward(nc, S, K, T, A, W, l)
        S.close()
        S = Sems(nc, 2)
        W = {"X": sb("X", [P, NT, H])}
        EW = {"w2h": sb("ew2h", [P, KC, H], F32R), "w2l": sb("ew2l", [P, KC, H], F32R),
              "wch2": sb("wch2", [P, H], F32R), "wcl": sb("wcl", [ED, H], F32R)}
        join_layers(nc, S, K, T, A, W, EW)
        W["agg"] = sb("agg", [P, NT, H])
        UW = {"w3h": sb("w3h", [P, K2, H], F32R), "w3l": sb("w3l", [P, K2, H], F32R)}
        edge_messages(nc, S, K, T, A, W, EW, UW)
        update_nodes(nc, S, K, T, A, W, UW, out)


_OUT = (N, H)


def kernel(**inputs):
    import numpy as np
    import concourse.bacc as bacc
    from concourse.bass_utils import run_bass_kernel_spmd as run

    nc = bacc.Bacc("TRN2", target_bir_lowering=False, num_devices=1)
    arrays, A = {}, {}
    for name, value in inputs.items():
        a = np.ascontiguousarray(value)
        arrays[f"in_{name}"] = a
        A[name] = nc.dram_tensor(f"in_{name}", a.shape, mybir.dt.from_np(a.dtype), kind="ExternalInput").ap()
    out = nc.dram_tensor("out", _OUT, F32, kind="ExternalOutput").ap()
    program(nc, A, out)
    return run(nc, [arrays], core_ids=[0]).results[0]["out"]
```
